# Optimizing a Trainium2 kernel written in Bass

```python
import numpy as np
import jax
import jax.numpy as jnp

def _softmax(x, axis=-1):
    return jax.nn.softmax(x, axis=axis)

def _gelu(x):
    return jax.nn.gelu(x, approximate=True)

def _silu(x):
    return jax.nn.silu(x)

def _sigmoid(x):
    return jax.nn.sigmoid(x)

def _layernorm(x, axis=-1, eps=1e-05):
    m = jnp.mean(x, axis=axis, keepdims=True)
    v = jnp.var(x, axis=axis, keepdims=True)
    return (x - m) / jnp.sqrt(v + eps)

def _scatter_add(tgt, idx, src, axis=0):
    return tgt.at[idx].add(src)

def _segment_sum(src, seg, n):
    return jax.ops.segment_sum(src, seg, n)
kernel_name = 'mk_cond_seq_d4_seqx_r4_46a18f'

def setup_inputs(seed: int=0):
    np.random.seed(seed)
    _w = jnp.asarray

    def _rec_inputs():
        import jax
        import jax.numpy as jnp
        _rk = jax.random.key(seed)
        x = -0.000125 + 0.9999 * jax.random.normal(jax.random.fold_in(_rk, 1), (4, 512, 256), jnp.float32)
        _lenS = 512 - jax.random.randint(jax.random.fold_in(_rk, 7), (4,), 0, max(1, 512 // 4) + 1, jnp.int32)
        _lenS2 = 512 - jax.random.randint(jax.random.fold_in(_rk, 8), (4,), 0, max(1, 512 // 4) + 1, jnp.int32)
        itok_B_0_15 = jax.random.randint(jax.random.fold_in(_rk, 11), (4,), 0, 16, jnp.int32)
        itok_B_34_63 = jax.random.randint(jax.random.fold_in(_rk, 13), (4,), 34, 64, jnp.int32)
        fside_Bx16xSxS_0 = -1.47943e-05 + 1.00017 * jax.random.normal(jax.random.fold_in(_rk, 14), (4, 16, 512, 512), jnp.float32)
        itok_B_0_7 = jax.random.randint(jax.random.fold_in(_rk, 15), (4,), 0, 8, jnp.int32)
        condB_gatescore = jax.random.uniform(jax.random.fold_in(_rk, 16), (4,), jnp.float32, 0.0, 0.581427)
        _validS = jnp.arange(512)[None, :] < _lenS[:, None]
        _validS2 = jnp.arange(512)[None, :] < _lenS2[:, None]
        _causal = jnp.tril(jnp.ones((512, 512), dtype=bool))
        mask_Bx1xSxS_bk0 = jnp.logical_not(jnp.broadcast_to(_validS[:, None, None, :], (4, 1, 512, 512)))
        return (x, itok_B_0_15, itok_B_34_63, fside_Bx16xSxS_0, itok_B_0_7, condB_gatescore, mask_Bx1xSxS_bk0)
    x, itok_B_0_15, itok_B_34_63, fside_Bx16xSxS_0, itok_B_0_7, condB_gatescore, mask_Bx1xSxS_bk0 = _rec_inputs()

    def _L0_cond_setup():
        import jax, jax.numpy as jnp
        import numpy as np
        B, S, D = (32, 256, 256)
        A = 64
        E = 16
        LN_EPS = 1e-05
        key = jax.random.key(seed)
        ks = jax.random.split(key, 10)
        s = lambda fan_in: 1.0 / np.sqrt(fan_in)
        return {'hidden_states': jax.random.normal(ks[0], (B, S, D), dtype=jnp.float32), 'domain_id': jax.random.randint(ks[1], (B,), 0, E, dtype=jnp.int64), 'down_W': jax.random.uniform(ks[2], (A, D), jnp.float32, -s(D), s(D)), 'down_b': jax.random.uniform(ks[3], (A,), jnp.float32, -s(D), s(D)), 'up_W': jax.random.uniform(ks[4], (D, A), jnp.float32, -s(A), s(A)), 'up_b': jax.random.uniform(ks[5], (D,), jnp.float32, -s(A), s(A)), 'expert_W': jax.random.uniform(ks[6], (E, A, A), jnp.float32, -s(A), s(A)), 'expert_b': jax.random.uniform(ks[7], (E, A), jnp.float32, -s(A), s(A)), 'domain_emb': jax.random.normal(ks[8], (E, A), dtype=jnp.float32), 'ln_gamma': jnp.ones((D,), jnp.float32), 'ln_beta': jnp.zeros((D,), jnp.float32)}
    _L0_cond_all = _L0_cond_setup()
    _L0_cond_in = {k: v for k, v in _L0_cond_all.items() if k in ('down_W', 'down_b', 'up_W', 'up_b', 'expert_W', 'expert_b', 'domain_emb', 'ln_gamma', 'ln_beta')}
    del _L0_cond_all

    def _L1_cond_setup():
        import jax, jax.numpy as jnp
        import numpy as np
        import math
        D_MODEL = 256
        N_HEAD = 16
        HEAD_DIM = D_MODEL // N_HEAD
        D_FF = 1024
        NUM_STEPS = 100.0
        RESCALE = 4000.0
        EPS = 1e-05

        def _sin_emb(t):
            half = D_MODEL // 2
            x = t.astype(jnp.float32) / NUM_STEPS * RESCALE
            freqs = jnp.exp(jnp.arange(half, dtype=jnp.float32) * (-math.log(10000.0) / (half - 1)))
            e = x[:, None] * freqs[None, :]
            return jnp.concatenate([jnp.sin(e), jnp.cos(e)], axis=-1)

        def _ln(x):
            m = jnp.mean(x, axis=-1, keepdims=True)
            v = jnp.var(x, axis=-1, keepdims=True)
            return (x - m) / jnp.sqrt(v + EPS)

        def _gelu2(x):
            return x * jax.nn.sigmoid(1.702 * x)
        key = jax.random.key(seed)
        ks = jax.random.split(key, 24)
        B, S, D, F = (4, 128, D_MODEL, D_FF)
        std = 0.02
        inp = {'src': jax.random.normal(ks[0], (B, S, D), dtype=jnp.float32), 'src_mask': jax.random.randint(ks[1], (B, 1, S, S), 0, 2).astype(bool), 'timestep': jax.random.randint(ks[2], (B,), 0, 100, dtype=jnp.int32), 'attention_bias': jax.random.normal(ks[3], (B, N_HEAD, S, S), dtype=jnp.float32), 'W_ada': jax.random.normal(ks[4], (D, 2 * D), dtype=jnp.float32) * std, 'b_ada': jnp.zeros((2 * D,), dtype=jnp.float32), 'Wq': jax.random.normal(ks[5], (D, D), dtype=jnp.float32) * std, 'bq': jnp.zeros((D,), dtype=jnp.float32), 'Wk': jax.random.normal(ks[6], (D, D), dtype=jnp.float32) * std, 'bk': jnp.zeros((D,), dtype=jnp.float32), 'Wv': jax.random.normal(ks[7], (D, D), dtype=jnp.float32) * std, 'bv': jnp.zeros((D,), dtype=jnp.float32), 'Wo': jax.random.normal(ks[8], (D, D), dtype=jnp.float32) * std, 'bo': jnp.zeros((D,), dtype=jnp.float32), 'W1': jax.random.normal(ks[9], (D, F), dtype=jnp.float32) * std, 'b1': jnp.zeros((F,), dtype=jnp.float32), 'W2': jax.random.normal(ks[10], (F, D), dtype=jnp.float32) * std, 'b2': jnp.zeros((D,), dtype=jnp.float32), 'g2': jnp.ones((D,), dtype=jnp.float32), 'beta2': jnp.zeros((D,), dtype=jnp.float32)}
        return inp
    _L1_cond_all = _L1_cond_setup()
    _L1_cond_in = {k: v for k, v in _L1_cond_all.items() if k in ('W_ada', 'b_ada', 'Wq', 'bq', 'Wk', 'bk', 'Wv', 'bv', 'Wo', 'bo', 'W1', 'b1', 'W2', 'b2', 'g2', 'beta2')}
    del _L1_cond_all

    def _L2_cond_setup():
        import jax, jax.numpy as jnp
        import numpy as np
        E, H, I = (8, 256, 1024)
        B, S = (4, 256)
        LN_EPS = 1e-12
        key = jax.random.key(seed)
        ks = jax.random.split(key, 8)
        x = jax.random.normal(ks[0], (B, S, H), dtype=jnp.float32)
        expert_idx = jax.random.randint(ks[1], (B,), 0, E, dtype=jnp.int64)
        Wi = jax.random.normal(ks[2], (E, H, I), dtype=jnp.float32) * 0.02
        bi = jnp.zeros((E, I), dtype=jnp.float32)
        Wo = jax.random.normal(ks[3], (E, I, H), dtype=jnp.float32) * 0.02
        bo = jnp.zeros((E, H), dtype=jnp.float32)
        gamma = jnp.ones((E, H), dtype=jnp.float32)
        beta = jnp.zeros((E, H), dtype=jnp.float32)
        return {'input_tensor': x, 'expert_idx': expert_idx, 'Wi': Wi, 'bi': bi, 'Wo': Wo, 'bo': bo, 'gamma': gamma, 'beta': beta}
    _L2_cond_all = _L2_cond_setup()
    _L2_cond_in = {k: v for k, v in _L2_cond_all.items() if k in ('Wi', 'bi', 'Wo', 'bo', 'gamma', 'beta')}
    del _L2_cond_all

    def _L3_cond_setup():
        import jax, jax.numpy as jnp
        import numpy as np
        D_MODEL = 256
        N_HEADS = 16
        D_HEAD = D_MODEL // N_HEADS
        D_FF = 1024
        EPS = 1e-05

        def layernorm(x, gamma, beta):
            mu = jnp.mean(x, axis=-1, keepdims=True)
            var = jnp.var(x, axis=-1, keepdims=True)
            return (x - mu) * jax.lax.rsqrt(var + EPS) * gamma + beta
        key = jax.random.key(seed)
        ks = jax.random.split(key, 16)
        B, T = (4, 512)
        s = 1.0 / np.sqrt(D_MODEL)
        sf = 1.0 / np.sqrt(D_FF)
        return {'x': jax.random.normal(ks[0], (B, T, D_MODEL), jnp.float32), 'gate_score': jax.random.uniform(ks[1], (B,), jnp.float32), 'Wq': jax.random.normal(ks[2], (D_MODEL, D_MODEL), jnp.float32) * s, 'bq': jnp.zeros((D_MODEL,), jnp.float32), 'Wk': jax.random.normal(ks[3], (D_MODEL, D_MODEL), jnp.float32) * s, 'bk': jnp.zeros((D_MODEL,), jnp.float32), 'Wv': jax.random.normal(ks[4], (D_MODEL, D_MODEL), jnp.float32) * s, 'bv': jnp.zeros((D_MODEL,), jnp.float32), 'Wo': jax.random.normal(ks[5], (D_MODEL, D_MODEL), jnp.float32) * s, 'bo': jnp.zeros((D_MODEL,), jnp.float32), 'W1': jax.random.normal(ks[6], (D_MODEL, D_FF), jnp.float32) * s, 'b1': jnp.zeros((D_FF,), jnp.float32), 'W2': jax.random.normal(ks[7], (D_FF, D_MODEL), jnp.float32) * sf, 'b2': jnp.zeros((D_MODEL,), jnp.float32), 'gamma1': jnp.ones((D_MODEL,), jnp.float32), 'beta1': jnp.zeros((D_MODEL,), jnp.float32), 'gamma2': jnp.ones((D_MODEL,), jnp.float32), 'beta2': jnp.zeros((D_MODEL,), jnp.float32)}
    _L3_cond_all = _L3_cond_setup()
    _L3_cond_in = {k: v for k, v in _L3_cond_all.items() if k in ('Wq', 'bq', 'Wk', 'bk', 'Wv', 'bv', 'Wo', 'bo', 'W1', 'b1', 'W2', 'b2', 'gamma1', 'beta1', 'gamma2', 'beta2')}
    del _L3_cond_all
    return {'x': x, 'itok_B_0_15': itok_B_0_15, 'itok_B_34_63': itok_B_34_63, 'fside_Bx16xSxS_0': fside_Bx16xSxS_0, 'itok_B_0_7': itok_B_0_7, 'condB_gatescore': condB_gatescore, 'mask_Bx1xSxS_bk0': mask_Bx1xSxS_bk0, 'L0_cond_down_W': _L0_cond_in['down_W'], 'L0_cond_down_b': _L0_cond_in['down_b'], 'L0_cond_up_W': _L0_cond_in['up_W'], 'L0_cond_up_b': _L0_cond_in['up_b'], 'L0_cond_expert_W': _L0_cond_in['expert_W'], 'L0_cond_expert_b': _L0_cond_in['expert_b'], 'L0_cond_domain_emb': _L0_cond_in['domain_emb'], 'L0_cond_ln_gamma': _L0_cond_in['ln_gamma'], 'L0_cond_ln_beta': _L0_cond_in['ln_beta'], 'L1_cond_W_ada': _L1_cond_in['W_ada'], 'L1_cond_b_ada': _L1_cond_in['b_ada'], 'L1_cond_Wq': _L1_cond_in['Wq'], 'L1_cond_bq': _L1_cond_in['bq'], 'L1_cond_Wk': _L1_cond_in['Wk'], 'L1_cond_bk': _L1_cond_in['bk'], 'L1_cond_Wv': _L1_cond_in['Wv'], 'L1_cond_bv': _L1_cond_in['bv'], 'L1_cond_Wo': _L1_cond_in['Wo'], 'L1_cond_bo': _L1_cond_in['bo'], 'L1_cond_W1': _L1_cond_in['W1'], 'L1_cond_b1': _L1_cond_in['b1'], 'L1_cond_W2': _L1_cond_in['W2'], 'L1_cond_b2': _L1_cond_in['b2'], 'L1_cond_g2': _L1_cond_in['g2'], 'L1_cond_beta2': _L1_cond_in['beta2'], 'L2_cond_Wi': _L2_cond_in['Wi'], 'L2_cond_bi': _L2_cond_in['bi'], 'L2_cond_Wo': _L2_cond_in['Wo'], 'L2_cond_bo': _L2_cond_in['bo'], 'L2_cond_gamma': _L2_cond_in['gamma'], 'L2_cond_beta': _L2_cond_in['beta'], 'L3_cond_Wq': _L3_cond_in['Wq'], 'L3_cond_bq': _L3_cond_in['bq'], 'L3_cond_Wk': _L3_cond_in['Wk'], 'L3_cond_bk': _L3_cond_in['bk'], 'L3_cond_Wv': _L3_cond_in['Wv'], 'L3_cond_bv': _L3_cond_in['bv'], 'L3_cond_Wo': _L3_cond_in['Wo'], 'L3_cond_bo': _L3_cond_in['bo'], 'L3_cond_W1': _L3_cond_in['W1'], 'L3_cond_b1': _L3_cond_in['b1'], 'L3_cond_W2': _L3_cond_in['W2'], 'L3_cond_b2': _L3_cond_in['b2'], 'L3_cond_gamma1': _L3_cond_in['gamma1'], 'L3_cond_beta1': _L3_cond_in['beta1'], 'L3_cond_gamma2': _L3_cond_in['gamma2'], 'L3_cond_beta2': _L3_cond_in['beta2']}

def reference(x, itok_B_0_15, itok_B_34_63, fside_Bx16xSxS_0, itok_B_0_7, condB_gatescore, mask_Bx1xSxS_bk0, L0_cond_down_W, L0_cond_down_b, L0_cond_up_W, L0_cond_up_b, L0_cond_expert_W, L0_cond_expert_b, L0_cond_domain_emb, L0_cond_ln_gamma, L0_cond_ln_beta, L1_cond_W_ada, L1_cond_b_ada, L1_cond_Wq, L1_cond_bq, L1_cond_Wk, L1_cond_bk, L1_cond_Wv, L1_cond_bv, L1_cond_Wo, L1_cond_bo, L1_cond_W1, L1_cond_b1, L1_cond_W2, L1_cond_b2, L1_cond_g2, L1_cond_beta2, L2_cond_Wi, L2_cond_bi, L2_cond_Wo, L2_cond_bo, L2_cond_gamma, L2_cond_beta, L3_cond_Wq, L3_cond_bq, L3_cond_Wk, L3_cond_bk, L3_cond_Wv, L3_cond_bv, L3_cond_Wo, L3_cond_bo, L3_cond_W1, L3_cond_b1, L3_cond_W2, L3_cond_b2, L3_cond_gamma1, L3_cond_beta1, L3_cond_gamma2, L3_cond_beta2):
    import jax
    import jax.numpy as jnp

    def _L0_cond_ref(hidden_states, domain_id, down_W, down_b, up_W, up_b, expert_W, expert_b, domain_emb, ln_gamma, ln_beta):
        import jax, jax.numpy as jnp
        import numpy as np
        B, S, D = (32, 256, 256)
        A = 64
        E = 16
        LN_EPS = 1e-05
        residual = hidden_states
        hidden = jnp.einsum('bsd,ad->bsa', hidden_states, down_W) + down_b
        hidden = jax.nn.gelu(hidden, approximate=False)
        valid = (domain_id >= 0) & (domain_id < E)
        idx = jnp.clip(domain_id, 0, E - 1)
        Wsel = expert_W[idx]
        bsel = expert_b[idx]
        expert_out = jnp.einsum('bsa,boa->bso', hidden, Wsel) + bsel[:, None, :]
        domain_output = jnp.where(valid[:, None, None], expert_out, hidden)
        hidden = domain_output + domain_emb[idx][:, None, :]
        hidden = jnp.einsum('bsa,da->bsd', hidden, up_W) + up_b
        x = hidden + residual
        mu = jnp.mean(x, axis=-1, keepdims=True)
        var = jnp.mean(jnp.square(x - mu), axis=-1, keepdims=True)
        return (x - mu) * jax.lax.rsqrt(var + LN_EPS) * ln_gamma + ln_beta

    def _L1_cond_ref(src, src_mask, timestep, attention_bias, W_ada, b_ada, Wq, bq, Wk, bk, Wv, bv, Wo, bo, W1, b1, W2, b2, g2, beta2):
        import jax, jax.numpy as jnp
        import numpy as np
        import math
        D_MODEL = 256
        N_HEAD = 16
        HEAD_DIM = D_MODEL // N_HEAD
        D_FF = 1024
        NUM_STEPS = 100.0
        RESCALE = 4000.0
        EPS = 1e-05

        def _sin_emb(t):
            half = D_MODEL // 2
            x = t.astype(jnp.float32) / NUM_STEPS * RESCALE
            freqs = jnp.exp(jnp.arange(half, dtype=jnp.float32) * (-math.log(10000.0) / (half - 1)))
            e = x[:, None] * freqs[None, :]
            return jnp.concatenate([jnp.sin(e), jnp.cos(e)], axis=-1)

        def _ln(x):
            m = jnp.mean(x, axis=-1, keepdims=True)
            v = jnp.var(x, axis=-1, keepdims=True)
            return (x - m) / jnp.sqrt(v + EPS)

        def _gelu2(x):
            return x * jax.nn.sigmoid(1.702 * x)
        B, S, D = src.shape
        emb = jax.nn.silu(_sin_emb(timestep)) @ W_ada + b_ada
        scale, shift = jnp.split(emb[:, None, :], 2, axis=-1)
        x = _ln(src) * (1.0 + scale) + shift
        q = (x @ Wq + bq).reshape(B, S, N_HEAD, HEAD_DIM).transpose(0, 2, 1, 3)
        k = (x @ Wk + bk).reshape(B, S, N_HEAD, HEAD_DIM).transpose(0, 2, 1, 3)
        v = (x @ Wv + bv).reshape(B, S, N_HEAD, HEAD_DIM).transpose(0, 2, 1, 3)
        scores = jnp.einsum('bhqd,bhkd->bhqk', q / math.sqrt(HEAD_DIM), k)
        scores = scores + attention_bias
        scores = jnp.where(src_mask, -jnp.inf, scores.astype(jnp.float32))
        probs = jax.nn.softmax(scores, axis=-1).astype(v.dtype)
        ctx = jnp.einsum('bhqk,bhkd->bhqd', probs, v)
        ctx = ctx.transpose(0, 2, 1, 3).reshape(B, S, D)
        x = x + (ctx @ Wo + bo)
        h = _ln(x) * g2 + beta2
        ff = _gelu2(h @ W1 + b1) @ W2 + b2
        return x + ff

    def _L2_cond_ref(input_tensor, expert_idx, Wi, bi, Wo, bo, gamma, beta):
        import jax, jax.numpy as jnp
        import numpy as np
        E, H, I = (8, 256, 1024)
        B, S = (4, 256)
        LN_EPS = 1e-12
        Wi_b = Wi[expert_idx]
        bi_b = bi[expert_idx]
        Wo_b = Wo[expert_idx]
        bo_b = bo[expert_idx]
        g_b = gamma[expert_idx]
        be_b = beta[expert_idx]
        h = jax.nn.gelu(jnp.einsum('bsh,bhi->bsi', input_tensor, Wi_b) + bi_b[:, None, :], approximate=False)
        o = jnp.einsum('bsi,bih->bsh', h, Wo_b) + bo_b[:, None, :]
        r = o + input_tensor
        mu = jnp.mean(r, axis=-1, keepdims=True)
        var = jnp.mean(jnp.square(r - mu), axis=-1, keepdims=True)
        y = (r - mu) * jax.lax.rsqrt(var + LN_EPS)
        return y * g_b[:, None, :] + be_b[:, None, :]

    def _L3_cond_ref(x, gate_score, Wq, bq, Wk, bk, Wv, bv, Wo, bo, W1, b1, W2, b2, gamma1, beta1, gamma2, beta2):
        import jax, jax.numpy as jnp
        import numpy as np
        D_MODEL = 256
        N_HEADS = 16
        D_HEAD = D_MODEL // N_HEADS
        D_FF = 1024
        EPS = 1e-05

        def layernorm(x, gamma, beta):
            mu = jnp.mean(x, axis=-1, keepdims=True)
            var = jnp.var(x, axis=-1, keepdims=True)
            return (x - mu) * jax.lax.rsqrt(var + EPS) * gamma + beta
        B, T, C = x.shape
        h = layernorm(x, gamma1, beta1)
        Q = (h @ Wq + bq).reshape(B, T, N_HEADS, D_HEAD).transpose(0, 2, 1, 3)
        K = (h @ Wk + bk).reshape(B, T, N_HEADS, D_HEAD).transpose(0, 2, 1, 3)
        V = (h @ Wv + bv).reshape(B, T, N_HEADS, D_HEAD).transpose(0, 2, 1, 3)
        scores = jnp.einsum('bhqd,bhkd->bhqk', Q, K) / np.sqrt(D_HEAD)
        causal = jnp.tril(jnp.ones((T, T), dtype=bool))
        scores = jnp.where(causal, scores, -jnp.inf)
        attn = jax.nn.softmax(scores, axis=-1)
        ctx = jnp.einsum('bhqk,bhkd->bhqd', attn, V)
        ctx = ctx.transpose(0, 2, 1, 3).reshape(B, T, C)
        attn_out = ctx @ Wo + bo
        x1 = x + attn_out
        h2 = layernorm(x1, gamma2, beta2)
        ff = jax.nn.gelu(h2 @ W1 + b1, approximate=False) @ W2 + b2
        x2 = x1 + ff
        g = gate_score[:, None, None]
        return x + g * (x2 - x)
    x = _L0_cond_ref(x, itok_B_0_15, L0_cond_down_W, L0_cond_down_b, L0_cond_up_W, L0_cond_up_b, L0_cond_expert_W, L0_cond_expert_b, L0_cond_domain_emb, L0_cond_ln_gamma, L0_cond_ln_beta)
    x = _L1_cond_ref(x, mask_Bx1xSxS_bk0, itok_B_34_63, fside_Bx16xSxS_0, L1_cond_W_ada, L1_cond_b_ada, L1_cond_Wq, L1_cond_bq, L1_cond_Wk, L1_cond_bk, L1_cond_Wv, L1_cond_bv, L1_cond_Wo, L1_cond_bo, L1_cond_W1, L1_cond_b1, L1_cond_W2, L1_cond_b2, L1_cond_g2, L1_cond_beta2)
    x = _L2_cond_ref(x, itok_B_0_7, L2_cond_Wi, L2_cond_bi, L2_cond_Wo, L2_cond_bo, L2_cond_gamma, L2_cond_beta)
    x = _L3_cond_ref(x, condB_gatescore, L3_cond_Wq, L3_cond_bq, L3_cond_Wk, L3_cond_bk, L3_cond_Wv, L3_cond_bv, L3_cond_Wo, L3_cond_bo, L3_cond_W1, L3_cond_b1, L3_cond_W2, L3_cond_b2, L3_cond_gamma1, L3_cond_beta1, L3_cond_gamma2, L3_cond_beta2)
    return x

_drawn_inputs = setup_inputs


def setup_inputs(seed=0):
    import zlib

    import numpy as np

    out = dict(_drawn_inputs(seed))
    spreads = {'L0_cond_ln_gamma': (1.0, 0.2),
     'L0_cond_ln_beta': (0.0, 0.1),
     'L1_cond_b_ada': (0.0, 0.1),
     'L1_cond_bq': (0.0, 0.8),
     'L1_cond_bk': (0.0, 0.8),
     'L1_cond_bv': (0.0, 0.276),
     'L1_cond_bo': (0.0, 0.1),
     'L1_cond_b1': (0.0, 0.1),
     'L1_cond_b2': (0.0, 0.1),
     'L1_cond_g2': (1.0, 0.6),
     'L1_cond_beta2': (0.0, 0.693),
     'L2_cond_bi': (0.0, 0.1),
     'L2_cond_bo': (0.0, 0.1),
     'L2_cond_gamma': (1.0, 0.2),
     'L2_cond_beta': (0.0, 0.1),
     'L3_cond_bq': (0.0, 0.8),
     'L3_cond_bk': (0.0, 0.8),
     'L3_cond_bv': (0.0, 0.724),
     'L3_cond_bo': (0.0, 0.703),
     'L3_cond_b1': (0.0, 0.8),
     'L3_cond_b2': (0.0, 0.8),
     'L3_cond_gamma1': (1.0, 0.6),
     'L3_cond_beta1': (0.0, 0.704),
     'L3_cond_gamma2': (1.0, 0.6),
     'L3_cond_beta2': (0.0, 0.8)}
    factors = {'fside_Bx16xSxS_0': 8.0,
     'L0_cond_down_b': 8.0,
     'L1_cond_Wq': 8.0,
     'L1_cond_Wk': 8.0,
     'L3_cond_Wq': 4.609,
     'L3_cond_Wk': 4.527}
    for name, (base, spread) in spreads.items():
        noise = np.random.default_rng([zlib.crc32(name.encode()), seed]).standard_normal(out[name].shape)
        drawn = base * np.exp(spread * noise) if base else spread * noise
        out[name] = jnp.asarray(drawn.astype(out[name].dtype))
    for name, factor in factors.items():
        out[name] = (out[name] * factor).astype(out[name].dtype)
    return out
```

```python
import math
from contextlib import ExitStack

import numpy as np

import concourse.bass as bass
from concourse import mybir

F32 = mybir.dt.float32
F32R = mybir.dt.float32r
BF16 = mybir.dt.bfloat16
I32 = mybir.dt.int32
U8 = mybir.dt.uint8
ALU = mybir.AluOpType
ACT = mybir.ActivationFunctionType
AX = mybir.AxisListType

P = 128
B, S, D = 4, 512, 256
T = S // P
DK = D // P
H = 16
DH = D // H
F = 1024
FK = F // P
A = 64
SC = 1.0 / math.sqrt(DH)
MASKED = -1.0e30
ROUND = 1.5 * 2.0 ** 23
TURN = (6.28125, 0.0019354820251464844, 2 * math.pi - 6.28125 - 0.0019354820251464844)
PI_BELOW = 3.1415925
SIN_READY = 16
SET = 7
NORM_STEPS = 24


def settle(eng, passed):
    eng.sem_inc(passed, 1)


def layer_norm(dve, passed, src, dst, stats, mv, tmp, eps, norm_step, base):
    for t in range(T):
        dve.bn_stats(stats[:, t, :], src[:, t, :]).then_inc(norm_step, 1)
    dve.wait_ge(norm_step, base + 4)
    settle(dve, passed)
    for t in range(T):
        dve.bn_aggr(mv[:, t, :], stats[:, t, :]).then_inc(norm_step, 1)
    var, bits, y, q = tmp[:, 0, :], tmp[:, 1, :], tmp[:, 2, :], tmp[:, 3, :]
    dve.wait_ge(norm_step, base + 8)
    dve.tensor_scalar(var, mv[:, :, 1], eps, None, ALU.add).then_inc(norm_step, 1)
    dve.wait_ge(norm_step, base + 9)
    dve.tensor_scalar(bits.bitcast(I32), var.bitcast(I32), 1, None,
                      ALU.logical_shift_right).then_inc(norm_step, 1)
    dve.wait_ge(norm_step, base + 10)
    dve.tensor_scalar(y.bitcast(I32), bits.bitcast(I32), -1.0, float(0x5F3759DF), ALU.mult,
                      ALU.add).then_inc(norm_step, 1)
    for n in range(3):
        dve.wait_ge(norm_step, base + 11 + 3 * n)
        dve.tensor_tensor(q, y, y, ALU.mult).then_inc(norm_step, 1)
        dve.wait_ge(norm_step, base + 12 + 3 * n)
        dve.scalar_tensor_tensor(out=q, in0=q, scalar=-0.5, in1=var, op0=ALU.mult,
                                 op1=ALU.mult).then_inc(norm_step, 1)
        dve.wait_ge(norm_step, base + 13 + 3 * n)
        dve.scalar_tensor_tensor(out=y, in0=q, scalar=1.5, in1=y, op0=ALU.add,
                                 op1=ALU.mult).then_inc(norm_step, 1)
    dve.wait_ge(norm_step, base + 20)
    for t in range(T):
        dve.tensor_scalar(dst[:, t, :], src[:, t, :], mv[:, t, 0:1], y[:, t:t + 1], ALU.subtract,
                          ALU.mult).then_inc(norm_step, 1)


def product(pe, out, a, b, first, last):
    pe.matmul(out, a[0], b[0], start=first, stop=False)
    pe.matmul(out, a[0], b[1], start=False, stop=False)
    return pe.matmul(out, a[1], b[0], start=False, stop=last)


def flip(pe, banks, src, ident, flipped):
    for dk in range(DK):
        for t in range(T):
            last = pe.transpose(banks[dk][:, t * P:(t + 1) * P], src[:, t, dk * P:(dk + 1) * P], ident)
        last.then_inc(flipped, 1)


def over_rows(ap, n=T):
    return ap.unsqueeze(1).to_broadcast([P, n, D])


def adapter_layer(nc, x_in, x_out, w, c):
    with ExitStack() as ctx:
        def sb(name, shape, dt=F32):
            return ctx.enter_context(nc.sbuf_tensor("a_" + name, shape, dt))

        def sem(name):
            return nc.alloc_semaphore("a_" + name)

        bank = [ctx.enter_context(nc.psum_tensor(f"a_bank{i}", [P, 512], F32)) for i in range(4)]
        flips = ctx.enter_context(nc.psum_tensor("a_flips", [P, DK, 512], F32))
        ident = sb("ident", [P, P])
        down_raw, up_raw = sb("down_raw", [A, D]), sb("up_raw", [P, DK, A])
        down_t, up_t = sb("down_t", [P, DK, A]), sb("up_t", [A, D])
        down_b, up_b = sb("down_b", [A, 1]), sb("up_b", [P, D])
        gamma, beta = sb("gamma", [P, D]), sb("beta", [P, D])
        ids, id_row = sb("ids", [A, B], I32), sb("id_row", [1, B], I32)
        idf, valid, invalid, past = sb("idf", [A, B]), sb("valid", [A, B]), sb("invalid", [A, B]), sb("past", [A, B])
        x, xb, y = sb("x", [P, 2, T, D]), sb("xb", [P, T, D]), sb("y", [P, T, D])
        xt = sb("xt", [P, DK, S])
        e_raw, e_b, e_emb = sb("e_raw", [A, 2, A]), sb("e_b", [A, 2, 1]), sb("e_emb", [A, 2, 1])
        keep, e_t, add = sb("keep", [A, 2, A]), sb("e_t", [A, 2, A]), sb("add", [A, 2, 1])
        hid, hid2 = sb("hid", [A, S]), sb("hid2", [A, S])
        stats, mv, nt = sb("stats", [P, T, 6]), sb("mv", [P, T, 2]), sb("nt", [P, 4, T])

        dve_passed, pe_passed = sem("dve_passed"), sem("pe_passed")
        ids_loaded, small_loaded, set_flipped, set_step = sem("ids_loaded"), sem("small_loaded"), sem("set_flipped"), sem("set_step")
        x_loaded, expert_loaded = [sem("x_loaded0"), sem("x_loaded1")], [sem("expert_loaded0"), sem("expert_loaded1")]
        flipped, turned, expert_turned, kept, expert_made = (
            sem(n) for n in ("flipped", "turned", "expert_turned", "kept", "expert_made"))
        down_done, hid_made, expert_done, hid2_made, up_done = (
            sem(n) for n in ("down_done", "hid_made", "expert_done", "hid2_made", "up_done"))
        xb_made, summed, norm_step, scaled, y_made, y_stored = (
            sem(n) for n in ("xb_made", "summed", "norm_step", "scaled", "y_made", "y_stored"))
        block = ctx.enter_context(nc.Block())

        @block.sync
        def _(sp):
            spread = lambda a, n: a.rearrange("(o n) -> o n", o=1).to_broadcast([n, a.shape[0]])
            col = lambda a: a.rearrange("(p o) -> p o", o=1)
            sp.dma_start(id_row[:, :], spread(c["expert"], 1)).then_inc(ids_loaded, 16)
            for dst, src in ((ident[:, :], c["ident"]), (down_raw[:, :], w["down_W"]),
                             (up_raw[:, :, :], w["up_W"].rearrange("(k p) a -> p k a", p=P)),
                             (down_b[:, :], col(w["down_b"])), (up_b[:, :], spread(w["up_b"], P)),
                             (gamma[:, :], spread(w["ln_gamma"], P)), (beta[:, :], spread(w["ln_beta"], P)),
                             (ids[:, :], spread(c["expert"], A))):
                sp.dma_start(dst, src).then_inc(small_loaded, 16)
            sp.wait_ge(ids_loaded, 16)
            row = sp.alloc_register("a_expert")
            with sp.Fori(0, B // 2) as pair:
                for s in range(2):
                    b = pair * 2 + s
                    sp.wait_ge(y_stored, pair * 32)
                    sp.dma_start(x[:, s, :, :], x_in[bass.ds(b, 1)].rearrange("b (t p) d -> p (b t) d", p=P)).then_inc(x_loaded[s], 16)
                    sp.reg_alu(row, sp.value_load(id_row[0:1, bass.ds(b, 1)]), 0, ALU.max)
                    sp.reg_alu(row, row, w["expert_W"].shape[0] - 1, ALU.min)
                    e = sp.snap(row, min_val=0, max_val=w["expert_W"].shape[0] - 1)
                    sp.dma_start(e_raw[:, s, :], w["expert_W"][bass.ds(e, 1)].rearrange("e o a -> o (e a)")).then_inc(expert_loaded[s], 16)
                    sp.dma_start(e_b[:, s, :], w["expert_b"][bass.ds(e, 1)].rearrange("e a -> a e"),
                                 allow_slow_non_contiguous=True).then_inc(expert_loaded[s], 16)
                    sp.dma_start(e_emb[:, s, :], w["domain_emb"][bass.ds(e, 1)].rearrange("e a -> a e"),
                                 allow_slow_non_contiguous=True).then_inc(expert_loaded[s], 16)
                for s in range(2):
                    sp.wait_ge(y_made, pair * 2 + s + 1)
                    sp.dma_start(x_out[bass.ds(pair * 2 + s, 1)].rearrange("b (t p) d -> p (b t) d", p=P), y[:, :, :]).then_inc(y_stored, 16)
            sp.wait_ge(y_stored, 16 * B)

        @block.tensor
        def _(pe):
            pe.wait_ge(small_loaded, 128)
            for k in range(DK):
                pe.transpose(bank[0][:, k * A:(k + 1) * A], down_raw[:, k * P:(k + 1) * P], ident[0:A, 0:A])
            for k in range(DK):
                last = pe.transpose(bank[1][0:A, k * P:(k + 1) * P], up_raw[:, k, :], ident[:, :])
            last.then_inc(set_flipped, 1)
            pe.wait_ge(set_step, 2)
            with pe.Fori(0, B // 2) as pair:
                for s in range(2):
                    b = pair * 2 + s
                    pe.wait_ge(x_loaded[s], pair * 16 + 16)
                    flip(pe, (flips[:, 0, :], flips[:, 1, :]), x[:, s, :, :], ident[:, :], flipped)
                    pe.wait_ge(expert_loaded[s], pair * 48 + 48)
                    pe.wait_ge(hid2_made, b)
                    settle(pe, pe_passed)
                    pe.transpose(bank[1][0:A, 0:A], e_raw[:, s, :], ident[0:A, 0:A]).then_inc(expert_turned, 1)
                    pe.wait_ge(turned, b + 1)
                    for k in range(DK):
                        last = pe.matmul(bank[0][0:A, :], down_t[:, k, :], xt[:, k, :], start=k == 0, stop=k == DK - 1)
                    last.then_inc(down_done, 1)
                    pe.wait_ge(hid_made, b + 1)
                    pe.wait_ge(expert_made, b + 1)
                    settle(pe, pe_passed)
                    pe.matmul(bank[1][0:A, :], e_t[:, s, :], hid[:, :], start=True, stop=True).then_inc(expert_done, 1)
                    pe.wait_ge(hid2_made, b + 1)
                    pe.wait_ge(summed, b * 2)
                    for t in range(T):
                        last = pe.matmul(bank[2 + t // 2][:, (t % 2) * D:(t % 2 + 1) * D], hid2[:, t * P:(t + 1) * P], up_t[:, :],
                                         start=True, stop=True)
                        if t % 2:
                            last.then_inc(up_done, 1)

        @block.scalar
        def _(act):
            act.wait_ge(set_step, 2)
            with act.Fori(0, B // 2) as pair:
                for s in range(2):
                    b = pair * 2 + s
                    act.wait_ge(flipped, b * 2 + 2)
                    act.wait_ge(down_done, b)
                    act.activation(xt[:, :, :], flips[:, :, :], ACT.Copy).then_inc(turned, 1)
                    act.wait_ge(down_done, b + 1)
                    act.activation(hid[:, :], bank[0][0:A, :], ACT.Gelu, bias=down_b[:, :]).then_inc(hid_made, 1)
                    act.wait_ge(expert_done, b + 1)
                    act.wait_ge(up_done, b * 2)
                    act.activation(hid2[:, :], bank[1][0:A, :], ACT.Identity, bias=add[:, s, :]).then_inc(hid2_made, 1)

        @block.vector
        def _(dve):
            dve.wait_ge(small_loaded, 128)
            dve.wait_ge(set_flipped, 1)
            dve.tensor_copy(down_t[:, :, :], bank[0][:, 0:DK * A].rearrange("p (k a) -> p k a", k=DK)).then_inc(set_step, 1)
            dve.tensor_copy(up_t[:, :], bank[1][0:A, 0:D]).then_inc(set_step, 1)
            n_experts = float(w["expert_W"].shape[0])
            dve.tensor_copy(idf[:, :], ids[:, :]).then_inc(set_step, 1)
            dve.wait_ge(set_step, 3)
            dve.tensor_scalar(past[:, :], idf[:, :], n_experts, None, ALU.is_lt).then_inc(set_step, 1)
            dve.wait_ge(set_step, 4)
            dve.scalar_tensor_tensor(out=valid[:, :], in0=idf[:, :], scalar=0.0, in1=past[:, :], op0=ALU.is_ge,
                                     op1=ALU.mult).then_inc(set_step, 1)
            dve.wait_ge(set_step, 5)
            dve.tensor_scalar(invalid[:, :], valid[:, :], -1.0, 1.0, ALU.mult, ALU.add).then_inc(set_step, 1)
            dve.wait_ge(set_step, 6)
            with dve.Fori(0, B // 2) as pair:
                for s in range(2):
                    b = pair * 2 + s
                    base = b * NORM_STEPS
                    dve.wait_ge(expert_loaded[s], pair * 48 + 48)
                    dve.tensor_scalar(keep[:, s, :], ident[0:A, 0:A], invalid[:, bass.ds(b, 1)], None, ALU.mult).then_inc(kept, 1)
                    dve.wait_ge(kept, b + 1)
                    dve.wait_ge(expert_turned, b + 1)
                    dve.scalar_tensor_tensor(out=add[:, s, :], in0=e_b[:, s, :], scalar=valid[:, bass.ds(b, 1)],
                                             in1=e_emb[:, s, :], op0=ALU.mult, op1=ALU.add)
                    dve.scalar_tensor_tensor(out=e_t[:, s, :], in0=bank[1][0:A, 0:A], scalar=valid[:, bass.ds(b, 1)],
                                             in1=keep[:, s, :], op0=ALU.mult, op1=ALU.add).then_inc(expert_made, 1)
                    dve.wait_ge(x_loaded[s], pair * 16 + 16)
                    dve.tensor_tensor(xb[:, :, :], x[:, s, :, :], over_rows(up_b[:, :]), ALU.add).then_inc(xb_made, 1)
                    dve.wait_ge(xb_made, b + 1)
                    for i in range(2):
                        dve.wait_ge(up_done, b * 2 + i + 1)
                        dve.tensor_tensor(xb[:, 2 * i:2 * i + 2, :], bank[2 + i][:, :].rearrange("p (t d) -> p t d", d=D),
                                          xb[:, 2 * i:2 * i + 2, :], ALU.add).then_inc(summed, 1)
                    dve.wait_ge(summed, b * 2 + 2)
                    dve.wait_ge(y_stored, b * 16)
                    layer_norm(dve, dve_passed, xb, y, stats, mv, nt, 1e-5, norm_step, base)
                    dve.wait_ge(norm_step, base + NORM_STEPS)
                    dve.tensor_tensor(y[:, :, :], y[:, :, :], over_rows(gamma[:, :]), ALU.mult).then_inc(scaled, 1)
                    dve.wait_ge(scaled, b + 1)
                    dve.tensor_tensor(y[:, :, :], y[:, :, :], over_rows(beta[:, :]), ALU.add).then_inc(y_made, 1)


def biased_attention_layer(nc, x_in, x_out, w, c, scratch):
    qk_dram, ada_dram = scratch["halves"], scratch["ada"]
    with ExitStack() as ctx:
        def sb(name, shape, dt=F32):
            return ctx.enter_context(nc.sbuf_tensor("b_" + name, shape, dt))

        def sem(name):
            return nc.alloc_semaphore("b_" + name)

        bank = [ctx.enter_context(nc.psum_tensor(f"b_bank{i}", [P, 512], F32)) for i in range(2)]
        flips = ctx.enter_context(nc.psum_tensor("b_flips", [P, 4, 512], F32))
        o_bank = ctx.enter_context(nc.psum_tensor("b_obank", [P, 512], F32))
        n_bank = ctx.enter_context(nc.psum_tensor("b_nbank", [P, 512], F32))
        F0, F1, F2, F3 = (flips[:, i, :] for i in range(4))

        w_hi, w_lo = sb("w_hi", [P, 12 * 512], F32R), sb("w_lo", [P, 12 * 512], F32R)

        def weight(at, n, k):
            return tuple(x[:, at:at + n * k].rearrange("p (k n) -> p k n", k=k) for x in (w_hi, w_lo))

        wq, wk, wv, wo = (weight(512 * i, D, DK) for i in range(4))
        w1, w2 = weight(2048, F, DK), weight(4096, D, FK)
        ident, ident_bf = sb("ident", [P, P]), sb("ident_bf", [P, P], BF16)
        bq, bk = sb("bq", [P, DK]), sb("bk", [P, DK])
        b1, g2, be2 = sb("b1", [P, FK]), sb("g2", [P, DK]), sb("be2", [P, DK])
        bv, bo, b2 = sb("bv", [P, D]), sb("bo", [P, D]), sb("b2", [P, D])
        x = sb("x", [P, T, D])
        res = sb("res", [P, T, D])
        ctxt = sb("ctxt", [P, T, D])
        xt_hi, xt_lo = sb("xt_hi", [P, DK, S], F32R), sb("xt_lo", [P, DK, S], F32R)
        y = sb("y", [P, 2, S])
        ring_hi, ring_lo = sb("ring_hi", [P, 4, S], F32R), sb("ring_lo", [P, 4, S], F32R)
        v = sb("v", [P, T, D])
        v_one = sb("v_one", [P, 2, T, 4, 32])
        q_stack, k_stack = sb("q_stack", [P, 4, S], F32R), sb("k_stack", [P, 4, S], F32R)
        mask_u8, mask_add = sb("mask_u8", [P, T, S], U8), sb("mask_add", [P, T, S], BF16)
        bias = sb("bias", [P, 4, T, S])
        scores = sb("scores", [P, 2, T, S])
        row_max = sb("row_max", [P, 2, T])
        probs = sb("probs", [P, 4, T, S])
        o_sb = sb("o_sb", [P, S])
        one_over = sb("one_over", [P, T, 4])
        ada = sb("ada", [P, 2, D])
        stats, mv, nt = sb("stats", [P, T, 6]), sb("mv", [P, T, 2]), sb("nt", [P, 4, T])
        emb = sb("emb", [P, 8, B])
        tstep = sb("tstep", [P, B], I32)
        freq = sb("freq", [P, 1])
        adarow = v[0:B, :, :].rearrange("p t d -> p (t d)")[:, 0:2 * D]
        adab = v[0:B, :, :].rearrange("p t d -> p (t d)")[:, 2 * D:4 * D]

        pool_passed, dve_passed = sem("pool_passed"), sem("dve_passed")
        small_loaded, weights_loaded = sem("small_loaded"), sem("weights_loaded")
        halves_made, set_step, res_step = sem("halves_made"), sem("set_step"), sem("res_step")
        sin_done, ada_done, ada_stored = sem("sin_done"), sem("ada_done"), sem("ada_stored")
        x_loaded, mask_loaded, ada_loaded = sem("x_loaded"), sem("mask_loaded"), sem("ada_loaded")
        bias_loaded = [sem(f"bias_loaded{i}") for i in range(4)]
        norm_step, res_ready, mask_made = sem("norm_step"), sem("res_ready"), sem("mask_made")
        flipped, hi_made, lo_made, affine_made = (sem(n) for n in ("flipped", "hi_made", "lo_made", "affine_made"))
        projected, part_hi, part_lo, v_projected, v_ready = (
            sem(n) for n in ("projected", "part_hi", "part_lo", "v_projected", "v_ready"))
        halves_stored, stack_loaded, v_packed = sem("halves_stored"), [sem("stack_loaded0"), sem("stack_loaded1")], sem("v_packed")
        scores_ready, scored, shifted = sem("scores_ready"), sem("scored"), sem("shifted")
        turned, exped, weighed, o_copied, o_turned, inverted, ctx_made = (
            sem(n) for n in ("turned", "exped", "weighed", "o_copied", "o_turned", "inverted", "ctx_made"))
        attn_out, first_res, up_done, gelu_done, ff_hi, ff_lo, down_done, out_ready, out_stored = (
            sem(n) for n in ("attn_out", "first_res", "up_done", "gelu_done", "ff_hi", "ff_lo", "down_done", "out_ready", "out_stored"))

        block = ctx.enter_context(nc.Block())

        @block.sync
        def _(sp):
            raw = bias
            for i, name in enumerate(("Wq", "Wk", "Wv", "Wo")):
                sp.dma_start(raw[:, 0, i, :].rearrange("p (k n) -> p k n", k=DK),
                             w[name].rearrange("(k p) n -> p k n", p=P)).then_inc(weights_loaded, 16)
            sp.dma_start(raw[:, 1, :, :].rearrange("p t s -> p (t s)").rearrange("p (k n) -> p k n", k=DK),
                         w["W1"].rearrange("(k p) n -> p k n", p=P)).then_inc(weights_loaded, 16)
            sp.dma_start(raw[:, 2, :, :].rearrange("p t s -> p (t s)").rearrange("p (k n) -> p k n", k=FK),
                         w["W2"].rearrange("(k p) n -> p k n", p=P)).then_inc(weights_loaded, 16)
            sp.dma_start(raw[:, 3, 0:2, :], w["W_ada"].rearrange("(k p) n -> p k n", p=P)).then_inc(weights_loaded, 16)
            sp.wait_ge(ada_done, 2)
            sp.dma_start(ada_dram, adarow).then_inc(ada_stored, 16)
            sp.wait_ge(ada_stored, 16)
            with sp.Fori(0, B) as b:
                sp.dma_start(x[:, :, :], x_in[bass.ds(b, 1)].rearrange("b (t p) d -> p (b t) d", p=P)).then_inc(x_loaded, 16)
                sp.dma_start(ada[:, :, :].rearrange("p a d -> p (a d)"),
                             ada_dram[bass.ds(b, 1), :].to_broadcast([P, 2 * D])).then_inc(ada_loaded, 16)
                sp.dma_start(mask_u8[:, :, :], c["mask"][bass.ds(b, 1)].rearrange("b (t p) k -> p (b t) k", p=P)).then_inc(mask_loaded, 16)
                with sp.Fori(0, 2) as g:
                    it = b * 2 + g
                    for n in range(8):
                        sp.wait_ge(scored, it * 32 + 4 * n + 4)
                        sp.dma_start(bias[:, n % 4, :, :],
                                     c["bias"][bass.ds(it * 8 + n, 1)].rearrange("h (t p) k -> p (h t) k", p=P)
                                     ).then_inc(bias_loaded[n % 4], 16)
                sp.wait_ge(out_ready, b * T + T)
                sp.dma_start(x_out[bass.ds(b, 1)].rearrange("b (t p) d -> p (b t) d", p=P), res[:, :, :]).then_inc(out_stored, 16)
            sp.wait_ge(out_stored, 16 * B)

        @block.gpsimd
        def _(pool):
            bc = lambda a, n: a.rearrange("(o n) -> o n", o=1).to_broadcast([n, a.shape[0]])
            cols = lambda a: a.rearrange("(k p) -> p k", p=P)
            for dst, src in ((ident[:, :], c["ident"]), (freq[:, :], c["freq"]),
                             (tstep[:, :], bc(c["timestep"], P)), (adab, bc(w["b_ada"], B)),
                             (bq[:, :], cols(w["bq"])), (bk[:, :], cols(w["bk"])), (b1[:, :], cols(w["b1"])),
                             (g2[:, :], cols(w["g2"])), (be2[:, :], cols(w["beta2"])),
                             (bv[:, :], bc(w["bv"], P)), (bo[:, :], bc(w["bo"], P)), (b2[:, :], bc(w["b2"], P))):
                pool.dma_start(dst, src, allow_slow_non_contiguous=True).then_inc(small_loaded, 16)
            pool.memset(v_one[:, :, :, :, :], 0.0).then_inc(set_step, 1)
            pool.wait_ge(set_step, 1)
            pool.memset(v_one[:, :, :, :, DH:DH + 1], 1.0).then_inc(set_step, 1)
            with pool.Fori(0, B) as b:
                pool.wait_ge(mask_loaded, b * 16 + 16)
                pool.wait_ge(res_ready, b + 1)
                settle(pool, pool_passed)
                pool.tensor_scalar(mask_add[:, :, :], mask_u8[:, :, :], MASKED, None, ALU.mult).then_inc(mask_made, 1)
                for n in range(4):
                    pool.wait_ge(part_lo, b * 4 + n + 1)
                    settle(pool, pool_passed)
                    for half, ring in enumerate((ring_hi, ring_lo)):
                        pool.dma_start(qk_dram[2 * (n // 2) + half, (n % 2) * P:(n % 2 + 1) * P, :],
                                       ring[:, n, :].bitcast(F32)).then_inc(halves_stored, 16)
                pool.wait_ge(halves_stored, b * 128 + 128)
                settle(pool, pool_passed)
                with pool.Fori(0, 2) as g:
                    it = b * 2 + g
                    for par in range(2):
                        pool.wait_ge(scored, it * 32 + par * 16)
                        settle(pool, pool_passed)
                        rows = (g * 2 + par) * 64
                        heads = qk_dram[:, bass.ds(rows, 64), :].rearrange("c (h r) n -> c r h n", r=DH)
                        for i in range(4):
                            at = 64 * par + DH * i
                            pool.dma_start(q_stack[at:at + DH, :, :].bitcast(F32), heads[i % 2]).then_inc(stack_loaded[par], 16)
                            pool.dma_start(k_stack[at:at + DH, :, :].bitcast(F32), heads[2 + i // 2]).then_inc(stack_loaded[par], 16)
                        pool.wait_ge(v_ready, b * 2 + 2)
                        pool.wait_ge(weighed, it * 2 + par)
                        settle(pool, pool_passed)
                        pool.tensor_copy(v_one[:, par, :, :, 0:DH],
                                         v[:, :, bass.ds(rows, 64)].rearrange("p t (h d) -> p t h d", d=DH)
                                         ).then_inc(v_packed, 1)

        @block.tensor
        def _(pe):
            pe.sem_inc(turned, 8)
            pe.sem_inc(weighed, 1)
            pe.wait_ge(sin_done, 2)
            pe.wait_ge(weights_loaded, 112)
            for k in range(2):
                last = pe.matmul(bank[0][0:B, :], emb[:, 6 + k, :], bias[:, 3, k, :], start=k == 0, stop=k == 1)
            last.then_inc(ada_done, 1)

            def halves(m, k, lo, n):
                return tuple(x[:, k, lo:lo + n] for x in m)

            xt = (xt_hi, xt_lo)
            with pe.Fori(0, B) as b:
                pe.wait_ge(res_ready, b + 1)
                flip(pe, (F0, F1), res, ident[:, :], flipped)
                pe.wait_ge(lo_made, b * 6 + 2)
                for n, (m, out) in enumerate(((wq, bank[0][:, :]), (wq, bank[1][:, :]), (wk, F2), (wk, F3))):
                    for k in range(DK):
                        last = product(pe, out, halves(m, k, (n % 2) * P, P), halves(xt, k, 0, S), k == 0, k == DK - 1)
                    last.then_inc(projected, 1)
                for t in range(T):
                    out = (F0, F1)[t // 2][:, (t % 2) * D:(t % 2 + 1) * D]
                    for k in range(DK):
                        last = product(pe, out, halves(xt, k, t * P, P), halves(wv, k, 0, D), k == 0, k == DK - 1)
                    if t % 2:
                        last.then_inc(v_projected, 1)

                with pe.Fori(0, 2) as g:
                    it = b * 2 + g

                    def score(n, t):
                        par = n // 4
                        rows = slice(64 * par, 64 * par + 64)
                        if n == 0 and t == 0:
                            pe.wait_ge(mask_made, b + 1)
                        if n % 4 == 0 and t == 0:
                            pe.wait_ge(stack_loaded[par], it * 128 + 128)
                        pe.wait_ge(scored, it * 32 + 4 * n + t + 15)
                        pe.matmul(bank[t % 2][:, :], q_stack[rows, n % 4, t * P:(t + 1) * P], k_stack[rows, n % 4, :],
                                  start=True, stop=False)
                        pe.matmul(bank[t % 2][:, :], ident_bf[:, :], mask_add[:, t, :], start=False,
                                  stop=True).then_inc(scores_ready, 1)

                    def turn(n, kt):
                        if kt == 0:
                            pe.wait_ge(shifted, it * 32 + 4 * n + 4)
                        if kt % 2 == 0:
                            pe.wait_ge(exped, it * 16 + 2 * n + 1 + kt // 2)
                        for t in range(T):
                            last = pe.transpose(flips[:, kt, t * P:(t + 1) * P],
                                                scores[:, n % 2, t, kt * P:(kt + 1) * P], ident[:, :])
                        last.then_inc(turned, 1)

                    def weigh(par):
                        pe.wait_ge(exped, it * 16 + 8 * par + 10)
                        pe.wait_ge(v_packed, it * 2 + par + 1)
                        pe.wait_ge(o_copied, it * 2 + par)
                        for kt in range(T):
                            for j in range(4):
                                last = pe.matmul(o_bank[32 * j:32 * j + 32, :], v_one[:, par, kt, j, :],
                                                 probs[:, j, kt, :], start=kt == 0, stop=kt == T - 1,
                                                 skip_group_check=True)
                        last.then_inc(weighed, 1)

                    def turn_back(par):
                        pe.wait_ge(o_copied, it * 2 + par + 1)
                        pe.wait_ge(ctx_made, it * 2 + par)
                        for t in range(T):
                            last = pe.transpose(n_bank[:, t * P:(t + 1) * P], o_sb[:, t * P:(t + 1) * P], ident[:, :])
                        last.then_inc(o_turned, 1)

                    for n in range(9):
                        for t in range(T):
                            if n < 8:
                                score(n, t)
                            if n:
                                turn(n - 1, t)
                            if n == 5 and t == 1:
                                weigh(0)
                        if n == 5:
                            turn_back(0)
                    weigh(1)
                    turn_back(1)

                pe.wait_ge(ctx_made, b * 4 + 4)
                flip(pe, (F0, F1), ctxt, ident[:, :], flipped)
                pe.wait_ge(lo_made, b * 6 + 4)
                for t in range(T):
                    out = (F2, F3)[t // 2][:, (t % 2) * D:(t % 2 + 1) * D]
                    for k in range(DK):
                        last = product(pe, out, halves(xt, k, t * P, P), halves(wo, k, 0, D), k == 0, k == DK - 1)
                    if t % 2:
                        last.then_inc(attn_out, 1)
                pe.wait_ge(norm_step, b * 2 * NORM_STEPS + 2 * NORM_STEPS)
                flip(pe, (F0, F1), ctxt, ident[:, :], flipped)
                pe.wait_ge(lo_made, b * 6 + 6)
                outs = (F2, F3, o_bank[:, :], n_bank[:, :])

                def down(m):
                    pe.wait_ge(ff_lo, b * FK + m + 1)
                    for t in range(T):
                        last = product(pe, outs[t][:, 0:D], halves((ring_hi, ring_lo), m % 4, t * P, P),
                                       halves(w2, m, 0, D), m == 0, m == FK - 1)
                    last.then_inc(down_done, 1)

                for m in range(FK):
                    if m >= 2:
                        pe.wait_ge(gelu_done, b * FK + m - 1)
                    for k in range(DK):
                        last = product(pe, bank[m % 2][:, :], halves(w1, k, m * P, P), halves(xt, k, 0, S), k == 0, k == DK - 1)
                    last.then_inc(up_done, 1)
                    if m >= 2:
                        down(m - 2)
                down(FK - 2)
                down(FK - 1)

        @block.scalar
        def _(act):
            act.sem_inc(exped, 2)
            act.wait_ge(small_loaded, 16 * 12)
            act.wait_ge(set_step, 2)
            act.wait_ge(set_step, SIN_READY)
            act.activation(emb[:, 4:6, :], emb[:, 2:4, :], ACT.Sin).then_inc(sin_done, 1)
            act.wait_ge(sin_done, 1)
            act.activation(emb[:, 6:8, :], emb[:, 4:6, :], ACT.Silu).then_inc(sin_done, 1)
            act.wait_ge(weights_loaded, 112)
            act.wait_ge(halves_made, 1)
            for n in range(3):
                act.activation(w_hi[:, n * 2048:(n + 1) * 2048], bias[:, n, :, :].rearrange("p t s -> p (t s)"),
                               ACT.Copy).then_inc(halves_made, 1)
            with act.Fori(0, B) as b:
                def hi(at, at2):
                    for k in range(DK):
                        act.wait_ge(flipped, b * 6 + at + k + 1)
                        act.activation(xt_hi[:, k, :], flips[:, k, :], ACT.Copy).then_inc(hi_made, 1)

                hi(0, 0)
                for n, (src, add) in enumerate(((bank[0][:, :], bq[:, 0:1]), (bank[1][:, :], bq[:, 1:2]),
                                                (F2, bk[:, 0:1]), (F3, bk[:, 1:2]))):
                    act.wait_ge(projected, b * 4 + n + 1)
                    act.activation(ring_hi[:, n, :], src, ACT.Identity, bias=add).then_inc(part_hi, 1)
                with act.Fori(0, 2) as g:
                    it = b * 2 + g
                    for n in range(8):
                        if n == 4:
                            act.wait_ge(weighed, it * 2 + 2)
                            act.wait_ge(o_turned, it * 2)
                            act.activation(o_sb[:, :], o_bank[:, :], ACT.Copy).then_inc(o_copied, 1)
                        for half in range(2):
                            if n % 4 == 0 and half == 0:
                                act.wait_ge(weighed, it * 2 + n // 4 + 1)
                            act.wait_ge(turned, it * 32 + 4 * n + 2 * half + 10)
                            act.activation(probs[:, n % 4, 2 * half:2 * half + 2, :], flips[:, 2 * half:2 * half + 2, :],
                                           ACT.Exp).then_inc(exped, 1)
                    act.wait_ge(weighed, it * 2 + 3)
                    act.wait_ge(o_turned, it * 2 + 1)
                    act.activation(o_sb[:, :], o_bank[:, :], ACT.Copy).then_inc(o_copied, 1)
                hi(2, 2)
                for k in range(DK):
                    act.wait_ge(flipped, b * 6 + 5 + k)
                    act.activation(y[:, k, :], flips[:, k, :], ACT.Identity, bias=be2[:, k:k + 1],
                                   scale=g2[:, k:k + 1]).then_inc(affine_made, 1)
                for m in range(FK):
                    act.wait_ge(up_done, b * FK + m + 1)
                    if m < 2:
                        act.wait_ge(lo_made, b * 6 + 5 + m)
                    else:
                        act.wait_ge(ff_lo, b * FK + m - 1)
                    act.activation(y[:, m % 2, :], bank[m % 2][:, :], ACT.Gelu_apprx_sigmoid,
                                   bias=b1[:, m:m + 1]).then_inc(gelu_done, 1)

        @block.vector
        def _(dve):
            dve.wait_ge(small_loaded, 16 * 12)
            dve.wait_ge(set_step, 2)
            step = [2]

            def link(ins):
                step[0] += 1
                ins.then_inc(set_step, 1)
                dve.wait_ge(set_step, step[0])

            link(dve.tensor_copy(ident_bf[:, :], ident[:, :]))
            link(dve.tensor_scalar(bq[:, :], bq[:, :], SC, None, ALU.mult))
            angle, turns, r, cosr = emb[:, 0, :], emb[:, 1, :], emb[:, 2, :], emb[:, 3, :]
            link(dve.tensor_copy(r, tstep[:, :]))
            link(dve.tensor_scalar(angle, r, 40.0, freq[:, 0:1], ALU.mult, ALU.mult))
            link(dve.tensor_scalar(turns, angle, 1.0 / (2 * math.pi), ROUND, ALU.mult, ALU.add))
            link(dve.tensor_scalar(turns, turns, -ROUND, None, ALU.add))
            link(dve.tensor_copy(r, angle))
            for part in TURN:
                link(dve.scalar_tensor_tensor(out=r, in0=turns, scalar=-part, in1=r, op0=ALU.mult, op1=ALU.add))
            link(dve.tensor_scalar(cosr, r, math.pi / 2, None, ALU.add))
            link(dve.tensor_scalar(angle, cosr, math.pi, -2 * math.pi, ALU.is_gt, ALU.mult))
            link(dve.tensor_tensor(cosr, cosr, angle, ALU.add))
            link(dve.tensor_scalar(emb[:, 2:4, :], emb[:, 2:4, :], PI_BELOW, -PI_BELOW, ALU.min, ALU.max))
            assert step[0] == SIN_READY
            dve.wait_ge(weights_loaded, 112)
            dve.tensor_scalar(bias[:, 0, 0, :], bias[:, 0, 0, :], SC, None, ALU.mult).then_inc(halves_made, 1)
            for n in range(3):
                dve.wait_ge(halves_made, 2 + n)
                dve.tensor_tensor(w_lo[:, n * 2048:(n + 1) * 2048], bias[:, n, :, :].rearrange("p t s -> p (t s)"),
                                  w_hi[:, n * 2048:(n + 1) * 2048].bitcast(F32), ALU.subtract).then_inc(set_step, 1)
            dve.wait_ge(set_step, SIN_READY + 3)
            dve.wait_ge(ada_done, 1)
            dve.tensor_tensor(adarow, bank[0][0:B, :], adab, ALU.add).then_inc(set_step, 1)
            dve.wait_ge(set_step, SIN_READY + 4)
            dve.tensor_scalar(adarow[:, 0:D], adarow[:, 0:D], 1.0, None, ALU.add).then_inc(ada_done, 1)
            dve.sem_inc(scored, 16)
            with dve.Fori(0, B) as b:
                base = b * 2 * NORM_STEPS
                dve.wait_ge(x_loaded, b * 16 + 16)
                dve.wait_ge(out_stored, b * 16)
                layer_norm(dve, dve_passed, x, res, stats, mv, nt, 1e-5, norm_step, base)
                dve.wait_ge(ada_loaded, b * 16 + 16)
                dve.wait_ge(norm_step, base + NORM_STEPS)
                dve.tensor_tensor(res[:, :, :], res[:, :, :], over_rows(ada[:, 0, :]), ALU.mult).then_inc(res_step, 1)
                dve.wait_ge(res_step, b * 3 + 1)
                dve.tensor_tensor(res[:, :, :], res[:, :, :], over_rows(ada[:, 1, :]), ALU.add).then_inc(res_ready, 1)

                def lo(at):
                    for k in range(DK):
                        dve.wait_ge(hi_made, b * 4 + at + k + 1)
                        dve.tensor_tensor(xt_lo[:, k, :], flips[:, k, :], xt_hi[:, k, :].bitcast(F32),
                                          ALU.subtract).then_inc(lo_made, 1)

                lo(0)
                for n, (src, add) in enumerate(((bank[0][:, :], bq[:, 0:1]), (bank[1][:, :], bq[:, 1:2]),
                                                (F2, bk[:, 0:1]), (F3, bk[:, 1:2]))):
                    dve.wait_ge(part_hi, b * 4 + n + 1)
                    dve.scalar_tensor_tensor(out=ring_lo[:, n, :], in0=src, scalar=add, in1=ring_hi[:, n, :].bitcast(F32),
                                             op0=ALU.add, op1=ALU.subtract).then_inc(part_lo, 1)
                for i in range(2):
                    dve.wait_ge(v_projected, b * 2 + i + 1)
                    dve.tensor_tensor(v[:, 2 * i:2 * i + 2, :], flips[:, i, :].rearrange("p (t d) -> p t d", d=D),
                                      over_rows(bv[:, :], 2), ALU.add).then_inc(v_ready, 1)
                dve.tensor_tensor(res[:, :, :], res[:, :, :], over_rows(bo[:, :]), ALU.add).then_inc(res_step, 1)

                with dve.Fori(0, 2) as g:
                    it = b * 2 + g

                    def normalise(par):
                        dve.wait_ge(o_turned, it * 2 + par + 1)
                        o = n_bank[:, :].rearrange("p (t h c) -> p t h c", t=T, h=4)
                        dve.reciprocal(one_over[:, :, :], o[:, :, :, DH]).then_inc(inverted, 1)
                        dve.wait_ge(inverted, it * 2 + par + 1)
                        dve.tensor_tensor(ctxt[:, :, bass.ds((g * 2 + par) * 64, 64)].rearrange("p t (h d) -> p t h d", d=DH),
                                          o[:, :, :, 0:DH], one_over[:, :, :].unsqueeze(3).to_broadcast([P, T, 4, DH]),
                                          ALU.mult).then_inc(ctx_made, 1)

                    for n in range(8):
                        for t in range(T):
                            if t == 0:
                                dve.wait_ge(bias_loaded[n % 4], it * 32 + 16 * (n // 4 + 1))
                                dve.wait_ge(turned, it * 32 + 4 * n + 4)
                            dve.wait_ge(scores_ready, it * 32 + 4 * n + t + 1)
                            settle(dve, dve_passed)
                            dve.tensor_tensor_reduce(out=scores[:, n % 2, t, :], in0=bank[t % 2][:, :], in1=bias[:, n % 4, t, :],
                                                     scale=1.0, scalar=-3.0e38, op0=ALU.add, op1=ALU.max,
                                                     accum_out=row_max[:, n % 2, t:t + 1]).then_inc(scored, 1)
                            dve.wait_ge(scored, it * 32 + 4 * n + t + 17)
                            dve.tensor_scalar(scores[:, n % 2, t, :], scores[:, n % 2, t, :], row_max[:, n % 2, t:t + 1],
                                              None, ALU.subtract).then_inc(shifted, 1)
                            if n == 6 and t == 1:
                                normalise(0)
                    normalise(1)

                lo(2)
                for i in range(2):
                    dve.wait_ge(attn_out, b * 2 + i + 1)
                    dve.wait_ge(res_step, b * 3 + 2)
                    dve.tensor_tensor(res[:, 2 * i:2 * i + 2, :], flips[:, 2 + i, :].rearrange("p (t d) -> p t d", d=D),
                                      res[:, 2 * i:2 * i + 2, :], ALU.add).then_inc(first_res, 1)
                dve.wait_ge(first_res, b * 2 + 2)
                layer_norm(dve, dve_passed, res, ctxt, stats, mv, nt, 1e-5, norm_step, base + NORM_STEPS)
                dve.wait_ge(norm_step, base + 2 * NORM_STEPS)
                dve.tensor_tensor(res[:, :, :], res[:, :, :], over_rows(b2[:, :]), ALU.add).then_inc(res_step, 1)
                for k in range(DK):
                    dve.wait_ge(affine_made, b * 2 + k + 1)
                    dve.tensor_copy(xt_hi[:, k, :], y[:, k, :]).then_inc(ff_hi, 1)
                    dve.wait_ge(ff_hi, b * (DK + FK) + k + 1)
                    dve.tensor_tensor(xt_lo[:, k, :], y[:, k, :], xt_hi[:, k, :].bitcast(F32), ALU.subtract).then_inc(lo_made, 1)
                for m in range(FK):
                    dve.wait_ge(gelu_done, b * FK + m + 1)
                    if m >= 4:
                        dve.wait_ge(down_done, b * FK + m - 3)
                    dve.tensor_copy(ring_hi[:, m % 4, :], y[:, m % 2, :]).then_inc(ff_hi, 1)
                    dve.wait_ge(ff_hi, b * (DK + FK) + DK + m + 1)
                    dve.tensor_tensor(ring_lo[:, m % 4, :], y[:, m % 2, :], ring_hi[:, m % 4, :].bitcast(F32),
                                      ALU.subtract).then_inc(ff_lo, 1)
                dve.wait_ge(down_done, b * FK + FK)
                dve.wait_ge(res_step, b * 3 + 3)
                for t, src in enumerate((F2, F3, o_bank[:, :], n_bank[:, :])):
                    dve.tensor_tensor(res[:, t, :], src[:, 0:D], res[:, t, :], ALU.add).then_inc(out_ready, 1)


def expert_mlp_layer(nc, x_in, x_out, w, c):
    n_experts = w["Wi"].shape[0]
    with ExitStack() as ctx:
        def sb(name, shape, dt=F32):
            return ctx.enter_context(nc.sbuf_tensor("c_" + name, shape, dt))

        def sem(name):
            return nc.alloc_semaphore("c_" + name)

        bank = [ctx.enter_context(nc.psum_tensor(f"c_bank{i}", [P, 512], F32)) for i in range(2)]
        flips = ctx.enter_context(nc.psum_tensor("c_flips", [P, DK, 512], F32))
        outs = [ctx.enter_context(nc.psum_tensor(f"c_out{i}", [P, 512], F32)) for i in range(4)]
        ident, id_row = sb("ident", [P, P]), sb("id_row", [1, B], I32)
        x, y = sb("x", [P, 2, T, D]), sb("y", [P, T, D])
        raw = sb("raw", [P, 2, 2048])
        w_hi, w_lo = sb("w_hi", [P, 2, 2, 2048], F32R), sb("w_lo", [P, 2, 2, 2048], F32R)
        bi = sb("bi", [P, 2, FK])
        bo, gamma, beta = sb("bo", [P, 2, D]), sb("gamma", [P, 2, D]), sb("beta", [P, 2, D])
        xt_hi, xt_lo = sb("xt_hi", [P, DK, S], F32R), sb("xt_lo", [P, DK, S], F32R)
        g = sb("g", [P, 2, S])
        ring_hi, ring_lo = sb("ring_hi", [P, 4, S], F32R), sb("ring_lo", [P, 4, S], F32R)
        stats, mv, nt = sb("stats", [P, T, 6]), sb("mv", [P, T, 2]), sb("nt", [P, 4, T])

        dve_passed, pool_passed = sem("dve_passed"), sem("pool_passed")
        ids_loaded, ident_loaded = sem("ids_loaded"), sem("ident_loaded")
        x_loaded, raw_loaded, small_loaded = ([sem(f"{n}{s}") for s in range(2)] for n in ("x_loaded", "raw_loaded", "small_loaded"))
        w_hi_made, w_lo_made, flipped, hi_made, lo_made = (
            sem(n) for n in ("w_hi_made", "w_lo_made", "flipped", "hi_made", "lo_made"))
        up_done, gelu_done, ff_hi, ff_lo, down_done = (sem(n) for n in ("up_done", "gelu_done", "ff_hi", "ff_lo", "down_done"))
        biased, summed, norm_step, scaled, y_made, y_stored = (
            sem(n) for n in ("biased", "summed", "norm_step", "scaled", "y_made", "y_stored"))
        block = ctx.enter_context(nc.Block())

        @block.sync
        def _(sp):
            sp.dma_start(id_row[:, :], c["mlp_expert"].rearrange("(o n) -> o n", o=1)).then_inc(ids_loaded, 16)
            sp.dma_start(ident[:, :], c["ident"]).then_inc(ident_loaded, 16)
            sp.wait_ge(ids_loaded, 16)
            row = sp.alloc_register("c_expert")
            with sp.Fori(0, B // 2) as pair:
                for s in range(2):
                    b = pair * 2 + s
                    sp.reg_alu(row, sp.value_load(id_row[0:1, bass.ds(b, 1)]), 0, ALU.max)
                    sp.reg_alu(row, row, n_experts - 1, ALU.min)
                    e = sp.snap(row, min_val=0, max_val=n_experts - 1)
                    sp.wait_ge(y_made, pair * 2)
                    sp.dma_start(x[:, s, :, :], x_in[bass.ds(b, 1)].rearrange("b (t p) d -> p (b t) d", p=P)).then_inc(x_loaded[s], 16)
                    for dst, name in ((bo, "bo"), (gamma, "gamma"), (beta, "beta")):
                        sp.dma_start(dst[:, s, :], w[name][bass.ds(e, 1), :].to_broadcast([P, D])).then_inc(small_loaded[s], 16)
                    sp.dma_start(bi[:, s, :], w["bi"][bass.ds(e, 1)].rearrange("e (k p) -> p (e k)", p=P),
                                 allow_slow_non_contiguous=True).then_inc(small_loaded[s], 16)
                    for i, (name, k) in enumerate((("Wi", DK), ("Wo", FK))):
                        sp.wait_ge(w_lo_made, b * 2 + i)
                        if i == 0:
                            sp.wait_ge(w_lo_made, b * 2)
                        sp.dma_start(raw[:, i, :].rearrange("p (k n) -> p k n", k=k),
                                     w[name][bass.ds(e, 1)].rearrange("e (k p) n -> p (e k) n", p=P)).then_inc(raw_loaded[i], 16)
                for s in range(2):
                    sp.wait_ge(y_made, pair * 2 + s + 1)
                    sp.dma_start(x_out[bass.ds(pair * 2 + s, 1)].rearrange("b (t p) d -> p (b t) d", p=P), y[:, :, :]).then_inc(y_stored, 16)
            sp.wait_ge(y_stored, 16 * B)

        @block.gpsimd
        def _(pool):
            with pool.Fori(0, B // 2) as pair:
                for s in range(2):
                    b = pair * 2 + s
                    for i in range(2):
                        pool.wait_ge(raw_loaded[i], b * 16 + 16)
                        pool.wait_ge(y_made, pair * 2)
                        settle(pool, pool_passed)
                        pool.tensor_copy(w_hi[:, s, i, :], raw[:, i, :]).then_inc(w_hi_made, 1)
                        pool.wait_ge(w_hi_made, b * 2 + i + 1)
                        settle(pool, pool_passed)
                        pool.tensor_tensor(w_lo[:, s, i, :], raw[:, i, :], w_hi[:, s, i, :].bitcast(F32),
                                           ALU.subtract).then_inc(w_lo_made, 1)

        @block.tensor
        def _(pe):
            pe.wait_ge(ident_loaded, 16)
            xt = (xt_hi, xt_lo)
            with pe.Fori(0, B // 2) as pair:
                for s in range(2):
                    b = pair * 2 + s
                    w1 = tuple(m[:, s, 0, :].rearrange("p (k n) -> p k n", k=DK) for m in (w_hi, w_lo))
                    w2 = tuple(m[:, s, 1, :].rearrange("p (k n) -> p k n", k=FK) for m in (w_hi, w_lo))
                    pe.wait_ge(x_loaded[s], pair * 16 + 16)
                    flip(pe, (flips[:, 0, :], flips[:, 1, :]), x[:, s, :, :], ident[:, :], flipped)
                    pe.wait_ge(lo_made, b * 2 + 2)
                    pe.wait_ge(w_lo_made, b * 2 + 1)

                    def down(m):
                        if m == 0:
                            pe.wait_ge(w_lo_made, b * 2 + 2)
                            pe.wait_ge(summed, b * T)
                        pe.wait_ge(ff_lo, b * FK + m + 1)
                        for t in range(T):
                            a = tuple(r[:, m % 4, t * P:(t + 1) * P] for r in (ring_hi, ring_lo))
                            last = product(pe, outs[t][:, 0:D], a, tuple(x[:, m, :] for x in w2), m == 0, m == FK - 1)
                        last.then_inc(down_done, 1)

                    for m in range(FK):
                        if m >= 2:
                            pe.wait_ge(gelu_done, b * FK + m - 1)
                        for k in range(DK):
                            last = product(pe, bank[m % 2][:, :], tuple(x[:, k, m * P:(m + 1) * P] for x in w1),
                                           tuple(x[:, k, :] for x in xt), k == 0, k == DK - 1)
                        last.then_inc(up_done, 1)
                        if m >= 2:
                            down(m - 2)
                    down(FK - 2)
                    down(FK - 1)

        @block.scalar
        def _(act):
            with act.Fori(0, B // 2) as pair:
                for s in range(2):
                    b = pair * 2 + s
                    for k in range(DK):
                        act.wait_ge(flipped, b * 2 + k + 1)
                        act.wait_ge(up_done, b * FK)
                        act.activation(xt_hi[:, k, :], flips[:, k, :], ACT.Copy).then_inc(hi_made, 1)
                    act.wait_ge(small_loaded[s], pair * 64 + 64)
                    for m in range(FK):
                        act.wait_ge(up_done, b * FK + m + 1)
                        if m >= 2:
                            act.wait_ge(ff_lo, b * FK + m - 1)
                        act.activation(g[:, m % 2, :], bank[m % 2][:, :], ACT.Gelu, bias=bi[:, s, m:m + 1]).then_inc(gelu_done, 1)

        @block.vector
        def _(dve):
            with dve.Fori(0, B // 2) as pair:
                for s in range(2):
                    b = pair * 2 + s
                    base = b * NORM_STEPS
                    for k in range(DK):
                        dve.wait_ge(hi_made, b * 2 + k + 1)
                        dve.tensor_tensor(xt_lo[:, k, :], flips[:, k, :], xt_hi[:, k, :].bitcast(F32), ALU.subtract).then_inc(lo_made, 1)
                    dve.wait_ge(small_loaded[s], pair * 64 + 64)
                    dve.tensor_tensor(x[:, s, :, :], x[:, s, :, :], over_rows(bo[:, s, :]), ALU.add).then_inc(biased, 1)
                    for m in range(FK):
                        dve.wait_ge(gelu_done, b * FK + m + 1)
                        if m >= 4:
                            dve.wait_ge(down_done, b * FK + m - 3)
                        dve.tensor_copy(ring_hi[:, m % 4, :], g[:, m % 2, :]).then_inc(ff_hi, 1)
                        dve.wait_ge(ff_hi, b * FK + m + 1)
                        dve.tensor_tensor(ring_lo[:, m % 4, :], g[:, m % 2, :], ring_hi[:, m % 4, :].bitcast(F32),
                                          ALU.subtract).then_inc(ff_lo, 1)
                    dve.wait_ge(down_done, b * FK + FK)
                    dve.wait_ge(biased, b + 1)
                    for t in range(T):
                        dve.tensor_tensor(x[:, s, t, :], outs[t][:, 0:D], x[:, s, t, :], ALU.add).then_inc(summed, 1)
                    dve.wait_ge(summed, b * T + T)
                    dve.wait_ge(y_stored, b * 16)
                    layer_norm(dve, dve_passed, x[:, s, :, :], y, stats, mv, nt, 1e-12, norm_step, base)
                    dve.wait_ge(norm_step, base + NORM_STEPS)
                    dve.tensor_tensor(y[:, :, :], y[:, :, :], over_rows(gamma[:, s, :]), ALU.mult).then_inc(scaled, 1)
                    dve.wait_ge(scaled, b + 1)
                    dve.tensor_tensor(y[:, :, :], y[:, :, :], over_rows(beta[:, s, :]), ALU.add).then_inc(y_made, 1)


def causal_attention_layer(nc, x_in, x_out, w, c, scratch):
    qk_dram = scratch["halves"]
    with ExitStack() as ctx:
        def sb(name, shape, dt=F32):
            return ctx.enter_context(nc.sbuf_tensor("d_" + name, shape, dt))

        def sem(name):
            return nc.alloc_semaphore("d_" + name)

        bank = [ctx.enter_context(nc.psum_tensor(f"d_bank{i}", [P, 512], F32)) for i in range(2)]
        flips = ctx.enter_context(nc.psum_tensor("d_flips", [P, 4, 512], F32))
        o_bank = ctx.enter_context(nc.psum_tensor("d_obank", [P, 512], F32))
        n_bank = ctx.enter_context(nc.psum_tensor("d_nbank", [P, 512], F32))
        F0, F1, F2, F3 = (flips[:, i, :] for i in range(4))

        w_hi, w_lo = sb("w_hi", [P, 12 * 512], F32R), sb("w_lo", [P, 12 * 512], F32R)

        def weight(at, n, k):
            return tuple(x[:, at:at + n * k].rearrange("p (k n) -> p k n", k=k) for x in (w_hi, w_lo))

        wq, wk, wv, wo = (weight(512 * i, D, DK) for i in range(4))
        w1, w2 = weight(2048, F, DK), weight(4096, D, FK)
        ident, ident_bf, causal = sb("ident", [P, P]), sb("ident_bf", [P, P], BF16), sb("causal", [P, P])
        causal_qk, causal_kq = sb("causal_qk", [P, P], BF16), sb("causal_kq", [P, P], BF16)
        bq, bk, b1 = sb("bq", [P, DK]), sb("bk", [P, DK]), sb("b1", [P, FK])
        g1, be1, g2, be2 = (sb(n, [P, DK]) for n in ("g1", "be1", "g2", "be2"))
        bv, bo, b2 = sb("bv", [P, D]), sb("bo", [P, D]), sb("b2", [P, D])
        gates, gate = sb("gates", [P, B]), sb("gate", [P, 1])
        x, res, ctxt = sb("x", [P, T, D]), sb("res", [P, T, D]), sb("ctxt", [P, T, D])
        xt_hi, xt_lo = sb("xt_hi", [P, DK, S], F32R), sb("xt_lo", [P, DK, S], F32R)
        y = sb("y", [P, 2, S])
        ring_hi, ring_lo = sb("ring_hi", [P, 4, S], F32R), sb("ring_lo", [P, 4, S], F32R)
        v_one = sb("v_one", [P, T, H, 32])
        q_stack, k_stack = sb("q_stack", [DH * 4 + 1, H, S], F32R), sb("k_stack", [DH * 4 + 1, H, S], F32R)
        less_max, max_row = sb("less_max", [P, 2, 4 * T]), sb("max_row", [4 * T, 2, P], F32R)
        probs = sb("probs", [P, 4, T, S])
        o_sb, one_over = sb("o_sb", [P, S]), sb("one_over", [P, T, 4])
        stats, mv, nt = sb("stats", [P, T, 6]), sb("mv", [P, T, 2]), sb("nt", [P, 4, T])

        dve_passed, pool_set = sem("dve_passed"), sem("pool_set")
        small_loaded, weights_loaded, halves_made, set_step = (
            sem(n) for n in ("small_loaded", "weights_loaded", "halves_made", "set_step"))
        x_loaded, norm_step, flipped, affine_made, hi_made, lo_made = (
            sem(n) for n in ("x_loaded", "norm_step", "flipped", "affine_made", "hi_made", "lo_made"))
        ctx_hi, projected, part_hi, part_lo, v_projected, v_ready, res_step = (
            sem(n) for n in ("ctx_hi", "projected", "part_hi", "part_lo", "v_projected", "v_ready", "res_step"))
        halves_stored, first_stack, rest_stack = sem("halves_stored"), sem("first_stack"), sem("rest_stack")
        scores_ready, maxed, max_turned, row_made = (sem(n) for n in ("scores_ready", "maxed", "max_turned", "row_made"))
        row_loaded = [sem("row_loaded0"), sem("row_loaded1")]
        shifted, exped, weighed, o_copied, o_turned, inverted, ctx_made = (
            sem(n) for n in ("shifted", "exped", "weighed", "o_copied", "o_turned", "inverted", "ctx_made"))
        attn_out, first_res, up_done, gelu_done, ff_hi, ff_lo, down_done, mixed, out_ready, out_stored = (
            sem(n) for n in ("attn_out", "first_res", "up_done", "gelu_done", "ff_hi", "ff_lo", "down_done", "mixed",
                             "out_ready", "out_stored"))
        block = ctx.enter_context(nc.Block())
        raw = probs

        @block.sync
        def _(sp):
            for i, name in enumerate(("Wq", "Wk", "Wv", "Wo")):
                sp.dma_start(raw[:, 0, i, :].rearrange("p (k n) -> p k n", k=DK),
                             w[name].rearrange("(k p) n -> p k n", p=P)).then_inc(weights_loaded, 16)
            for i, (name, k) in enumerate((("W1", DK), ("W2", FK))):
                sp.dma_start(raw[:, 1 + i, :, :].rearrange("p t s -> p (t s)").rearrange("p (k n) -> p k n", k=k),
                             w[name].rearrange("(k p) n -> p k n", p=P)).then_inc(weights_loaded, 16)
            with sp.Fori(0, B) as b:
                sp.dma_start(x[:, :, :], x_in[bass.ds(b, 1)].rearrange("b (t p) d -> p (b t) d", p=P)).then_inc(x_loaded, 16)
                for n in range(4):
                    sp.wait_ge(part_lo, b * 4 + n + 1)
                    for half, ring in enumerate((ring_hi, ring_lo)):
                        sp.dma_start(qk_dram[2 * (n // 2) + half, (n % 2) * P:(n % 2 + 1) * P, :],
                                     ring[:, n, :].bitcast(F32)).then_inc(halves_stored, 16)
                sp.wait_ge(halves_stored, b * 128 + 128)
                for first, last, loaded in ((0, 4, first_stack), (4, H, rest_stack)):
                    heads = qk_dram[:, first * DH:last * DH, :].rearrange("c (h r) n -> c r h n", r=DH)
                    for i in range(4):
                        rows = slice(DH * i, DH * i + DH)
                        sp.dma_start(q_stack[rows, first:last, :].bitcast(F32), heads[i % 2]).then_inc(loaded, 16)
                        sp.dma_start(k_stack[rows, first:last, :].bitcast(F32), heads[2 + i // 2]).then_inc(loaded, 16)
                for g in range(4):
                    sp.wait_ge(row_made, b * 4 + g + 1)
                    sp.dma_start(q_stack[4 * DH:4 * DH + 1, 4 * g:4 * g + 4, :].rearrange("o h (t n) -> o (h t) n", n=P).bitcast(F32),
                                 max_row[:, g % 2, :].bitcast(F32)).then_inc(row_loaded[g % 2], 16)
                sp.wait_ge(out_ready, b * T + T)
                sp.dma_start(x_out[bass.ds(b, 1)].rearrange("b (t p) d -> p (b t) d", p=P), res[:, :, :]).then_inc(out_stored, 16)
            sp.wait_ge(out_stored, 16 * B)

        @block.gpsimd
        def _(pool):
            spread = lambda a: a.rearrange("(o n) -> o n", o=1).to_broadcast([P, a.shape[0]])
            cols = lambda a: a.rearrange("(k p) -> p k", p=P)
            for dst, src in ((ident, c["ident"]), (causal, c["causal"]), (gates, spread(c["gate"])),
                             (bq, cols(w["bq"])), (bk, cols(w["bk"])), (b1, cols(w["b1"])),
                             (g1, cols(w["gamma1"])), (be1, cols(w["beta1"])), (g2, cols(w["gamma2"])), (be2, cols(w["beta2"])),
                             (bv, spread(w["bv"])), (bo, spread(w["bo"])), (b2, spread(w["b2"]))):
                pool.dma_start(dst[:, :], src, allow_slow_non_contiguous=True).then_inc(small_loaded, 16)
            pool.memset(k_stack[4 * DH:4 * DH + 1, :, :].bitcast(F32), 1.0).then_inc(pool_set, 1)
            pool.wait_ge(pool_set, 1)
            pool.memset(v_one[:, :, :, :], 0.0).then_inc(pool_set, 1)
            pool.wait_ge(pool_set, 2)
            pool.memset(v_one[:, :, :, DH:DH + 1], 1.0).then_inc(pool_set, 1)

        @block.tensor
        def _(pe):
            pe.wait_ge(small_loaded, 16 * 13)
            pe.wait_ge(pool_set, 3)
            pe.transpose(bank[0][:, 0:P], causal[:, :], ident[:, :]).then_inc(max_turned, 1)
            pe.wait_ge(set_step, SET)

            def halves(m, k, lo, n):
                return tuple(x[:, k, lo:lo + n] for x in m)

            xt = (xt_hi, xt_lo)
            with pe.Fori(0, B) as b:
                pe.wait_ge(norm_step, b * 2 * NORM_STEPS + NORM_STEPS)
                flip(pe, (F0, F1), ctxt, ident[:, :], flipped)
                pe.wait_ge(lo_made, b * 6 + 2)
                for n, (m, out) in enumerate(((wq, bank[0][:, :]), (wq, bank[1][:, :]), (wk, F2), (wk, F3))):
                    for k in range(DK):
                        last = product(pe, out, halves(m, k, (n % 2) * P, P), halves(xt, k, 0, S), k == 0, k == DK - 1)
                    last.then_inc(projected, 1)
                for t in range(T):
                    out = (F0, F1)[t // 2][:, (t % 2) * D:(t % 2 + 1) * D]
                    for k in range(DK):
                        last = product(pe, out, halves(xt, k, t * P, P), halves(wv, k, 0, D), k == 0, k == DK - 1)
                    if t % 2:
                        last.then_inc(v_projected, 1)

                def score(g, j, t):
                    n = 16 * g + 4 * j + t
                    if n == 0:
                        pe.wait_ge(first_stack, b * 128 + 128)
                    if n == 16:
                        pe.wait_ge(rest_stack, b * 128 + 128)
                    if n >= 2:
                        pe.wait_ge(maxed, b * 64 + n - 1)
                    h = 4 * g + j
                    pe.matmul(bank[n % 2][:, 0:(t + 1) * P], q_stack[0:4 * DH, h, t * P:(t + 1) * P],
                              k_stack[0:4 * DH, h, 0:(t + 1) * P], start=True, stop=False)
                    pe.matmul(bank[n % 2][:, t * P:(t + 1) * P], ident_bf[:, :], causal_qk[:, :], start=False,
                              stop=True).then_inc(scores_ready, 1)

                def turn_max(g):
                    pe.wait_ge(maxed, b * 64 + 16 * g + 16)
                    pe.wait_ge(ctx_made, b * 4 + max(g - 1, 0))
                    pe.transpose(n_bank[0:4 * T, 0:P], less_max[:, g % 2, :], ident[:, :]).then_inc(max_turned, 1)

                def score_keys(g, j, kt):
                    n = 16 * g + 4 * j + kt
                    if j == 0 and kt == 0:
                        pe.wait_ge(row_loaded[g % 2], b * 32 + 16 * (g // 2 + 1))
                    if n < 2:
                        pe.wait_ge(v_ready, b * 2 + n + 1)
                    if n >= 4:
                        pe.wait_ge(exped, b * 64 + n - 3)
                    h = 4 * g + j
                    pe.matmul(flips[:, kt, kt * P:S], k_stack[:, h, kt * P:(kt + 1) * P], q_stack[:, h, kt * P:S],
                              start=True, stop=False)
                    pe.matmul(flips[:, kt, kt * P:(kt + 1) * P], ident_bf[:, :], causal_kq[:, :], start=False,
                              stop=True).then_inc(shifted, 1)

                def weigh(g):
                    pe.wait_ge(exped, b * 64 + 16 * g + 16)
                    pe.wait_ge(o_copied, b * 4 + g)
                    for kt in range(T):
                        for j in range(4):
                            last = pe.matmul(o_bank[32 * j:32 * j + 32, kt * P:S], v_one[:, kt, 4 * g + j, :],
                                             probs[:, j, kt, kt * P:S], start=kt == 0, stop=kt == T - 1,
                                             skip_group_check=True)
                    last.then_inc(weighed, 1)

                def turn_back(g):
                    pe.wait_ge(o_copied, b * 4 + g + 1)
                    pe.wait_ge(row_made, b * 4 + min(g + 2, 4))
                    pe.wait_ge(ctx_made, b * 4 + g)
                    for t in range(T):
                        last = pe.transpose(n_bank[:, t * P:(t + 1) * P], o_sb[:, t * P:(t + 1) * P], ident[:, :])
                    last.then_inc(o_turned, 1)

                for j in range(4):
                    for t in range(T):
                        score(0, j, t)
                turn_max(0)
                for g in range(4):
                    for j in range(4):
                        for t in range(T):
                            score_keys(g, j, t)
                            if g < 3:
                                score(g + 1, j, t)
                    if g < 3:
                        turn_max(g + 1)
                    weigh(g)
                    turn_back(g)

                pe.wait_ge(ctx_made, b * 4 + 4)
                flip(pe, (F0, F1), ctxt, ident[:, :], flipped)
                pe.wait_ge(lo_made, b * 6 + 4)
                for t in range(T):
                    out = (F2, F3)[t // 2][:, (t % 2) * D:(t % 2 + 1) * D]
                    for k in range(DK):
                        last = product(pe, out, halves(xt, k, t * P, P), halves(wo, k, 0, D), k == 0, k == DK - 1)
                    if t % 2:
                        last.then_inc(attn_out, 1)
                pe.wait_ge(norm_step, b * 2 * NORM_STEPS + 2 * NORM_STEPS)
                flip(pe, (F0, F1), ctxt, ident[:, :], flipped)
                pe.wait_ge(lo_made, b * 6 + 6)
                outs = (F2, F3, o_bank[:, :], n_bank[:, :])

                def down(m):
                    pe.wait_ge(ff_lo, b * FK + m + 1)
                    for t in range(T):
                        last = product(pe, outs[t][:, 0:D], halves((ring_hi, ring_lo), m % 4, t * P, P),
                                       halves(w2, m, 0, D), m == 0, m == FK - 1)
                    last.then_inc(down_done, 1)

                for m in range(FK):
                    if m >= 2:
                        pe.wait_ge(gelu_done, b * FK + m - 1)
                    for k in range(DK):
                        last = product(pe, bank[m % 2][:, :], halves(w1, k, m * P, P), halves(xt, k, 0, S), k == 0, k == DK - 1)
                    last.then_inc(up_done, 1)
                    if m >= 2:
                        down(m - 2)
                down(FK - 2)
                down(FK - 1)

        @block.scalar
        def _(act):
            act.wait_ge(small_loaded, 16 * 13)
            act.wait_ge(weights_loaded, 96)
            act.wait_ge(halves_made, 1)
            for n in range(3):
                act.activation(w_hi[:, n * 2048:(n + 1) * 2048], raw[:, n, :, :].rearrange("p t s -> p (t s)"),
                               ACT.Copy).then_inc(halves_made, 1)
            with act.Fori(0, B) as b:
                def affine(at, scale, add, used):
                    for k in range(DK):
                        act.wait_ge(flipped, b * 6 + at + k + 1)
                        act.activation(y[:, k, :], flips[:, k, :], ACT.Identity, bias=add[:, k:k + 1],
                                       scale=scale[:, k:k + 1]).then_inc(affine_made, 1)

                affine(0, g1, be1, None)
                for n, (src, add) in enumerate(((bank[0][:, :], bq[:, 0:1]), (bank[1][:, :], bq[:, 1:2]),
                                                (F2, bk[:, 0:1]), (F3, bk[:, 1:2]))):
                    act.wait_ge(projected, b * 4 + n + 1)
                    act.activation(ring_hi[:, n, :], src, ACT.Identity, bias=add).then_inc(part_hi, 1)
                for g in range(4):
                    for j in range(4):
                        for kt in range(T):
                            if j == 0 and kt == 0:
                                act.wait_ge(weighed, b * 4 + g)
                            act.wait_ge(shifted, b * 64 + 16 * g + 4 * j + kt + 1)
                            act.activation(probs[:, j, kt, kt * P:S], flips[:, kt, kt * P:S], ACT.Exp).then_inc(exped, 1)
                    act.wait_ge(weighed, b * 4 + g + 1)
                    act.wait_ge(o_turned, b * 4 + g)
                    act.activation(o_sb[:, :], o_bank[:, :], ACT.Copy).then_inc(o_copied, 1)
                for k in range(DK):
                    act.wait_ge(flipped, b * 6 + 3 + k)
                    act.activation(xt_hi[:, k, :], flips[:, k, :], ACT.Copy).then_inc(ctx_hi, 1)
                affine(4, g2, be2, None)
                for m in range(FK):
                    act.wait_ge(up_done, b * FK + m + 1)
                    if m < 2:
                        act.wait_ge(lo_made, b * 6 + 5 + m)
                    else:
                        act.wait_ge(ff_lo, b * FK + m - 1)
                    act.activation(y[:, m % 2, :], bank[m % 2][:, :], ACT.Gelu, bias=b1[:, m:m + 1]).then_inc(gelu_done, 1)

        @block.vector
        def _(dve):
            dve.wait_ge(small_loaded, 16 * 13)
            dve.wait_ge(weights_loaded, 96)
            dve.tensor_scalar(raw[:, 0, 0, :], raw[:, 0, 0, :], SC, None, ALU.mult).then_inc(halves_made, 1)
            dve.tensor_copy(ident_bf[:, :], ident[:, :]).then_inc(set_step, 1)
            dve.tensor_copy(causal_qk[:, :], causal[:, :]).then_inc(set_step, 1)
            dve.tensor_scalar(bq[:, :], bq[:, :], SC, None, ALU.mult).then_inc(set_step, 1)
            dve.wait_ge(max_turned, 1)
            dve.tensor_copy(causal_kq[:, :], bank[0][:, 0:P]).then_inc(set_step, 1)
            for n in range(3):
                dve.wait_ge(halves_made, 2 + n)
                dve.tensor_tensor(w_lo[:, n * 2048:(n + 1) * 2048], raw[:, n, :, :].rearrange("p t s -> p (t s)"),
                                  w_hi[:, n * 2048:(n + 1) * 2048].bitcast(F32), ALU.subtract).then_inc(set_step, 1)
            dve.wait_ge(set_step, SET)
            dve.wait_ge(pool_set, 3)
            with dve.Fori(0, B) as b:
                base = b * 2 * NORM_STEPS

                def cut(at):
                    for k in range(DK):
                        dve.wait_ge(affine_made, b * 4 + at + k + 1)
                        dve.tensor_copy(xt_hi[:, k, :], y[:, k, :]).then_inc(hi_made, 1)
                        dve.wait_ge(hi_made, b * 4 + at + k + 1)
                        dve.tensor_tensor(xt_lo[:, k, :], y[:, k, :], xt_hi[:, k, :].bitcast(F32), ALU.subtract).then_inc(lo_made, 1)

                dve.wait_ge(x_loaded, b * 16 + 16)
                layer_norm(dve, dve_passed, x, ctxt, stats, mv, nt, 1e-5, norm_step, base)
                cut(0)
                for n, (src, add) in enumerate(((bank[0][:, :], bq[:, 0:1]), (bank[1][:, :], bq[:, 1:2]),
                                                (F2, bk[:, 0:1]), (F3, bk[:, 1:2]))):
                    dve.wait_ge(part_hi, b * 4 + n + 1)
                    dve.scalar_tensor_tensor(out=ring_lo[:, n, :], in0=src, scalar=add, in1=ring_hi[:, n, :].bitcast(F32),
                                             op0=ALU.add, op1=ALU.subtract).then_inc(part_lo, 1)
                for i in range(2):
                    dve.wait_ge(v_projected, b * 2 + i + 1)
                    dve.tensor_tensor(v_one[:, 2 * i:2 * i + 2, :, 0:DH],
                                      flips[:, i, :].rearrange("p (t h d) -> p t h d", t=2, d=DH),
                                      over_rows(bv[:, :], 2).rearrange("p t (h d) -> p t h d", d=DH), ALU.add).then_inc(v_ready, 1)
                dve.wait_ge(out_stored, b * 16)
                dve.tensor_tensor(res[:, :, :], x[:, :, :], over_rows(bo[:, :]), ALU.add).then_inc(res_step, 1)

                def maxima(g):
                    for n in range(16 * g, 16 * g + 16):
                        t = n % 4
                        dve.wait_ge(scores_ready, b * 64 + n + 1)
                        dve.tensor_reduce(less_max[:, g % 2, n % 16:n % 16 + 1], bank[n % 2][:, 0:(t + 1) * P], AX.X, ALU.max,
                                          negate=True).then_inc(maxed, 1)
                    dve.wait_ge(max_turned, b * 4 + g + 2)
                    if g >= 2:
                        dve.wait_ge(row_loaded[g % 2], b * 32 + 16)
                    dve.tensor_copy(max_row[:, g % 2, :], n_bank[0:4 * T, 0:P]).then_inc(row_made, 1)

                def normalise(g):
                    dve.wait_ge(o_turned, b * 4 + g + 1)
                    o = n_bank[:, :].rearrange("p (t h c) -> p t h c", t=T, h=4)
                    dve.reciprocal(one_over[:, :, :], o[:, :, :, DH]).then_inc(inverted, 1)
                    dve.wait_ge(inverted, b * 4 + g + 1)
                    dve.tensor_tensor(ctxt[:, :, g * 64:g * 64 + 64].rearrange("p t (h d) -> p t h d", d=DH),
                                      o[:, :, :, 0:DH], one_over[:, :, :].unsqueeze(3).to_broadcast([P, T, 4, DH]),
                                      ALU.mult).then_inc(ctx_made, 1)

                maxima(0)
                for g in range(4):
                    if g < 3:
                        maxima(g + 1)
                    normalise(g)
                for k in range(DK):
                    dve.wait_ge(ctx_hi, b * 2 + k + 1)
                    dve.tensor_tensor(xt_lo[:, k, :], flips[:, k, :], xt_hi[:, k, :].bitcast(F32), ALU.subtract).then_inc(lo_made, 1)
                dve.wait_ge(res_step, b * 3 + 1)
                for i in range(2):
                    dve.wait_ge(attn_out, b * 2 + i + 1)
                    dve.tensor_tensor(res[:, 2 * i:2 * i + 2, :], flips[:, 2 + i, :].rearrange("p (t d) -> p t d", d=D),
                                      res[:, 2 * i:2 * i + 2, :], ALU.add).then_inc(first_res, 1)
                dve.wait_ge(first_res, b * 2 + 2)
                layer_norm(dve, dve_passed, res, ctxt, stats, mv, nt, 1e-5, norm_step, base + NORM_STEPS)
                dve.wait_ge(norm_step, base + 2 * NORM_STEPS)
                dve.tensor_tensor(res[:, :, :], res[:, :, :], over_rows(b2[:, :]), ALU.add).then_inc(res_step, 1)
                dve.wait_ge(res_step, b * 3 + 2)
                dve.tensor_tensor(res[:, :, :], res[:, :, :], x[:, :, :], ALU.subtract).then_inc(res_step, 1)
                dve.tensor_copy(gate[:, :], gates[:, bass.ds(b, 1)]).then_inc(mixed, 1)
                cut(2)
                for m in range(FK):
                    dve.wait_ge(gelu_done, b * FK + m + 1)
                    if m >= 4:
                        dve.wait_ge(down_done, b * FK + m - 3)
                    dve.tensor_copy(ring_hi[:, m % 4, :], y[:, m % 2, :]).then_inc(ff_hi, 1)
                    dve.wait_ge(ff_hi, b * FK + m + 1)
                    dve.tensor_tensor(ring_lo[:, m % 4, :], y[:, m % 2, :], ring_hi[:, m % 4, :].bitcast(F32),
                                      ALU.subtract).then_inc(ff_lo, 1)
                dve.wait_ge(down_done, b * FK + FK)
                dve.wait_ge(res_step, b * 3 + 3)
                for t, src in enumerate((F2, F3, o_bank[:, :], n_bank[:, :])):
                    dve.tensor_tensor(res[:, t, :], src[:, 0:D], res[:, t, :], ALU.add).then_inc(mixed, 1)
                    dve.wait_ge(mixed, b * 5 + 2 + t)
                    dve.scalar_tensor_tensor(out=res[:, t, :], in0=res[:, t, :], scalar=gate[:, :], in1=x[:, t, :],
                                             op0=ALU.mult, op1=ALU.add).then_inc(out_ready, 1)


COMMON = {"mask": "mask_Bx1xSxS_bk0", "bias": "fside_Bx16xSxS_0", "timestep": "itok_B_34_63", "expert": "itok_B_0_15",
          "mlp_expert": "itok_B_0_7", "gate": "condB_gatescore"}


def layers_program(nc, args, out):
    def layer_weights(n):
        prefix = f"L{n}_cond_"
        return {name[len(prefix):]: ap for name, ap in args.items() if name.startswith(prefix)}

    def internal(name, shape):
        return nc.dram_tensor(name, shape, F32, kind="Internal").ap()

    between = [internal(f"between{n}", [B, S, D]) for n in range(3)]
    scratch = {"halves": internal("halves", [4, D, S]), "ada": internal("ada_rows", [B, 2 * D])}
    adapter_layer(nc, args["x"], between[0], layer_weights(0), args)
    biased_attention_layer(nc, between[0], between[1], layer_weights(1), args, scratch)
    expert_mlp_layer(nc, between[1], between[2], layer_weights(2), args)
    causal_attention_layer(nc, between[2], out, layer_weights(3), args, scratch)


def kernel(**inputs):
    import concourse.bacc as bacc
    from concourse.bass_utils import run_bass_kernel_spmd

    nc = bacc.Bacc("TRN2", target_bir_lowering=False, num_devices=1)
    given = {name: np.ascontiguousarray(a) for name, a in inputs.items()}
    data = {name: a for name, a in given.items() if name == "x" or name.startswith("L")}
    data.update({name: given[full] for name, full in COMMON.items()})
    data["mask"] = data["mask"].reshape(B, S, S)
    data["bias"] = data["bias"].reshape(B * H, S, S)
    data["ident"] = np.eye(P, dtype=np.float32)
    data["freq"] = np.exp(np.arange(P, dtype=np.float32) * np.float32(-math.log(10000.0) / (P - 1))).reshape(P, 1)
    data["causal"] = np.where(np.arange(P)[:, None] >= np.arange(P)[None, :], 0, MASKED).astype(np.float32)
    arrays, args = {}, {}
    for name, a in data.items():
        arrays[f"in_{name}_dram"] = a
        args[name] = nc.dram_tensor(f"in_{name}_dram", a.shape, mybir.dt.from_np(a.dtype), kind="ExternalInput").ap()
    out = nc.dram_tensor("out_0_dram", (B, S, D), F32, kind="ExternalOutput").ap()
    layers_program(nc, args, out)
    r = run_bass_kernel_spmd(nc, [arrays], core_ids=[0])
    return r.results[0]["out_0_dram"]
```

```python
import math
from contextlib import ExitStack

import numpy as np

import concourse.bass as bass
from concourse import mybir

F32 = mybir.dt.float32
F32R = mybir.dt.float32r
BF16 = mybir.dt.bfloat16
I32 = mybir.dt.int32
U8 = mybir.dt.uint8
ALU = mybir.AluOpType
ACT = mybir.ActivationFunctionType
AX = mybir.AxisListType

P = 128
B, S, D = 4, 512, 256
T = S // P
DK = D // P
H = 16
DH = D // H
F = 1024
FK = F // P
A = 64
SC = 1.0 / math.sqrt(DH)
MASKED = -1.0e30
ROUND = 1.5 * 2.0 ** 23
TURN = (6.28125, 0.0019354820251464844, 2 * math.pi - 6.28125 - 0.0019354820251464844)
PI_BELOW = 3.1415925
SIN_READY = 12
NORM_ROOT = 20
NORM_STEPS = NORM_ROOT + T


SLOTS = 5
LAG = 5
AHEAD = 22
X_STEPS = NORM_ROOT + 2 * T


def settle(eng, passed):
    eng.sem_inc(passed, 1)


def norm_stats(dve, src, stats, t, norm_step):
    dve.bn_stats(stats[:, t, :], src[:, t, :]).then_inc(norm_step, 1)


def norm_root(dve, passed, stats, mv, tmp, eps, norm_step, base):
    dve.wait_ge(norm_step, base + 4)
    settle(dve, passed)
    for t in range(T):
        dve.bn_aggr(mv[:, t, :], stats[:, t, :]).then_inc(norm_step, 1)
    var, bits, y, q = tmp[:, 0, :], tmp[:, 1, :], tmp[:, 2, :], tmp[:, 3, :]
    dve.wait_ge(norm_step, base + 8)
    dve.tensor_scalar(var, mv[:, :, 1], eps, None, ALU.add).then_inc(norm_step, 1)
    dve.wait_ge(norm_step, base + 9)
    dve.tensor_scalar(bits.bitcast(I32), var.bitcast(I32), 1, None,
                      ALU.logical_shift_right).then_inc(norm_step, 1)
    dve.wait_ge(norm_step, base + 10)
    dve.tensor_scalar(y.bitcast(I32), bits.bitcast(I32), -1.0, float(0x5F3759DF), ALU.mult,
                      ALU.add).then_inc(norm_step, 1)
    for n in range(3):
        dve.wait_ge(norm_step, base + 11 + 3 * n)
        dve.tensor_tensor(q, y, y, ALU.mult).then_inc(norm_step, 1)
        dve.wait_ge(norm_step, base + 12 + 3 * n)
        dve.scalar_tensor_tensor(out=q, in0=q, scalar=-0.5, in1=var, op0=ALU.mult,
                                 op1=ALU.mult).then_inc(norm_step, 1)
        dve.wait_ge(norm_step, base + 13 + 3 * n)
        dve.scalar_tensor_tensor(out=y, in0=q, scalar=1.5, in1=y, op0=ALU.add,
                                 op1=ALU.mult).then_inc(norm_step, 1)


def layer_norm(dve, passed, src, dst, stats, mv, tmp, eps, norm_step, base):
    for t in range(T):
        norm_stats(dve, src, stats, t, norm_step)
    norm_root(dve, passed, stats, mv, tmp, eps, norm_step, base)
    dve.wait_ge(norm_step, base + NORM_ROOT)
    for t in range(T):
        dve.tensor_scalar(dst[:, t, :], src[:, t, :], mv[:, t, 0:1], tmp[:, 2, t:t + 1], ALU.subtract,
                          ALU.mult).then_inc(norm_step, 1)


def product(pe, out, a, b, first, last):
    pe.matmul(out, a[0], b[0], start=first, stop=False)
    pe.matmul(out, a[0], b[1], start=False, stop=False)
    return pe.matmul(out, a[1], b[0], start=False, stop=last)


def flip(pe, banks, src, ident, flipped):
    for dk in range(DK):
        for t in range(T):
            last = pe.transpose(banks[dk][:, t * P:(t + 1) * P], src[:, t, dk * P:(dk + 1) * P], ident)
        last.then_inc(flipped, 1)


def over_rows(ap, n=T):
    return ap.unsqueeze(1).to_broadcast([P, n, D])


def adapter_layer(nc, x_in, x_out, w, c):
    with ExitStack() as ctx:
        def sb(name, shape, dt=F32):
            return ctx.enter_context(nc.sbuf_tensor("a_" + name, shape, dt))

        def sem(name):
            return nc.alloc_semaphore("a_" + name)

        bank = [ctx.enter_context(nc.psum_tensor(f"a_bank{i}", [P, 512], F32)) for i in range(4)]
        flips = ctx.enter_context(nc.psum_tensor("a_flips", [P, DK, 512], F32))
        ident = sb("ident", [P, P])
        down_raw, up_raw = sb("down_raw", [A, D]), sb("up_raw", [P, DK, A])
        down_t, up_t = sb("down_t", [P, DK, A]), sb("up_t", [A, D])
        down_b, up_b = sb("down_b", [A, 1]), sb("up_b", [P, D])
        gamma, beta = sb("gamma", [P, D]), sb("beta", [P, D])
        ids, id_row = sb("ids", [A, B], I32), sb("id_row", [1, B], I32)
        idf, valid, invalid, past = sb("idf", [A, B]), sb("valid", [A, B]), sb("invalid", [A, B]), sb("past", [A, B])
        x, xb, y = sb("x", [P, 2, T, D]), sb("xb", [P, T, D]), sb("y", [P, T, D])
        xt = sb("xt", [P, DK, S])
        e_raw, e_b, e_emb = sb("e_raw", [A, 2, A]), sb("e_b", [A, 2, 1]), sb("e_emb", [A, 2, 1])
        keep, e_t, add = sb("keep", [A, 2, A]), sb("e_t", [A, 2, A]), sb("add", [A, 2, 1])
        hid, hid2 = sb("hid", [A, S]), sb("hid2", [A, S])
        stats, mv, nt = sb("stats", [P, T, 6]), sb("mv", [P, T, 2]), sb("nt", [P, 4, T])

        dve_passed, pe_passed = sem("dve_passed"), sem("pe_passed")
        ids_loaded, small_loaded, set_flipped, set_step = sem("ids_loaded"), sem("small_loaded"), sem("set_flipped"), sem("set_step")
        x_loaded, expert_loaded = [sem("x_loaded0"), sem("x_loaded1")], [sem("expert_loaded0"), sem("expert_loaded1")]
        flipped, turned, expert_turned, kept, expert_made = (
            sem(n) for n in ("flipped", "turned", "expert_turned", "kept", "expert_made"))
        down_done, hid_made, expert_done, hid2_made, up_done = (
            sem(n) for n in ("down_done", "hid_made", "expert_done", "hid2_made", "up_done"))
        xb_made, summed, norm_step, scaled, y_made, y_stored = (
            sem(n) for n in ("xb_made", "summed", "norm_step", "scaled", "y_made", "y_stored"))
        block = ctx.enter_context(nc.Block())

        @block.sync
        def _(sp):
            spread = lambda a, n: a.rearrange("(o n) -> o n", o=1).to_broadcast([n, a.shape[0]])
            col = lambda a: a.rearrange("(p o) -> p o", o=1)
            sp.dma_start(id_row[:, :], spread(c["expert"], 1)).then_inc(ids_loaded, 16)
            for dst, src in ((ident[:, :], c["ident"]), (down_raw[:, :], w["down_W"]),
                             (up_raw[:, :, :], w["up_W"].rearrange("(k p) a -> p k a", p=P)),
                             (down_b[:, :], col(w["down_b"])), (up_b[:, :], spread(w["up_b"], P)),
                             (gamma[:, :], spread(w["ln_gamma"], P)), (beta[:, :], spread(w["ln_beta"], P)),
                             (ids[:, :], spread(c["expert"], A))):
                sp.dma_start(dst, src).then_inc(small_loaded, 16)
            sp.wait_ge(ids_loaded, 16)
            row = sp.alloc_register("a_expert")
            with sp.Fori(0, B // 2) as pair:
                for s in range(2):
                    b = pair * 2 + s
                    sp.wait_ge(y_stored, pair * 32)
                    sp.dma_start(x[:, s, :, :], x_in[bass.ds(b, 1)].rearrange("b (t p) d -> p (b t) d", p=P)).then_inc(x_loaded[s], 16)
                    sp.reg_alu(row, sp.value_load(id_row[0:1, bass.ds(b, 1)]), 0, ALU.max)
                    sp.reg_alu(row, row, w["expert_W"].shape[0] - 1, ALU.min)
                    e = sp.snap(row, min_val=0, max_val=w["expert_W"].shape[0] - 1)
                    sp.dma_start(e_raw[:, s, :], w["expert_W"][bass.ds(e, 1)].rearrange("e o a -> o (e a)")).then_inc(expert_loaded[s], 16)
                    sp.dma_start(e_b[:, s, :], w["expert_b"][bass.ds(e, 1)].rearrange("e a -> a e"),
                                 allow_slow_non_contiguous=True).then_inc(expert_loaded[s], 16)
                    sp.dma_start(e_emb[:, s, :], w["domain_emb"][bass.ds(e, 1)].rearrange("e a -> a e"),
                                 allow_slow_non_contiguous=True).then_inc(expert_loaded[s], 16)
                for s in range(2):
                    sp.wait_ge(y_made, pair * 2 + s + 1)
                    sp.dma_start(x_out[bass.ds(pair * 2 + s, 1)].rearrange("b (t p) d -> p (b t) d", p=P), y[:, :, :]).then_inc(y_stored, 16)
            sp.wait_ge(y_stored, 16 * B)

        @block.tensor
        def _(pe):
            pe.wait_ge(small_loaded, 128)
            for k in range(DK):
                pe.transpose(bank[0][:, k * A:(k + 1) * A], down_raw[:, k * P:(k + 1) * P], ident[0:A, 0:A])
            for k in range(DK):
                last = pe.transpose(bank[1][0:A, k * P:(k + 1) * P], up_raw[:, k, :], ident[:, :])
            last.then_inc(set_flipped, 1)
            pe.wait_ge(set_step, 2)
            with pe.Fori(0, B // 2) as pair:
                for s in range(2):
                    b = pair * 2 + s
                    pe.wait_ge(x_loaded[s], pair * 16 + 16)
                    flip(pe, (flips[:, 0, :], flips[:, 1, :]), x[:, s, :, :], ident[:, :], flipped)
                    pe.wait_ge(expert_loaded[s], pair * 48 + 48)
                    pe.wait_ge(hid2_made, b)
                    settle(pe, pe_passed)
                    pe.transpose(bank[1][0:A, 0:A], e_raw[:, s, :], ident[0:A, 0:A]).then_inc(expert_turned, 1)
                    pe.wait_ge(turned, b + 1)
                    for k in range(DK):
                        last = pe.matmul(bank[0][0:A, :], down_t[:, k, :], xt[:, k, :], start=k == 0, stop=k == DK - 1)
                    last.then_inc(down_done, 1)
                    pe.wait_ge(hid_made, b + 1)
                    pe.wait_ge(expert_made, b + 1)
                    settle(pe, pe_passed)
                    pe.matmul(bank[1][0:A, :], e_t[:, s, :], hid[:, :], start=True, stop=True).then_inc(expert_done, 1)
                    pe.wait_ge(hid2_made, b + 1)
                    pe.wait_ge(summed, b * 2)
                    for t in range(T):
                        last = pe.matmul(bank[2 + t // 2][:, (t % 2) * D:(t % 2 + 1) * D], hid2[:, t * P:(t + 1) * P], up_t[:, :],
                                         start=True, stop=True)
                        if t % 2:
                            last.then_inc(up_done, 1)

        @block.scalar
        def _(act):
            act.wait_ge(set_step, 2)
            with act.Fori(0, B // 2) as pair:
                for s in range(2):
                    b = pair * 2 + s
                    act.wait_ge(flipped, b * 2 + 2)
                    act.wait_ge(down_done, b)
                    act.activation(xt[:, :, :], flips[:, :, :], ACT.Copy).then_inc(turned, 1)
                    act.wait_ge(down_done, b + 1)
                    act.activation(hid[:, :], bank[0][0:A, :], ACT.Gelu, bias=down_b[:, :]).then_inc(hid_made, 1)
                    act.wait_ge(expert_done, b + 1)
                    act.wait_ge(up_done, b * 2)
                    act.activation(hid2[:, :], bank[1][0:A, :], ACT.Identity, bias=add[:, s, :]).then_inc(hid2_made, 1)

        @block.vector
        def _(dve):
            dve.wait_ge(small_loaded, 128)
            dve.wait_ge(set_flipped, 1)
            dve.tensor_copy(down_t[:, :, :], bank[0][:, 0:DK * A].rearrange("p (k a) -> p k a", k=DK)).then_inc(set_step, 1)
            dve.tensor_copy(up_t[:, :], bank[1][0:A, 0:D]).then_inc(set_step, 1)
            n_experts = float(w["expert_W"].shape[0])
            dve.tensor_copy(idf[:, :], ids[:, :]).then_inc(set_step, 1)
            dve.wait_ge(set_step, 3)
            dve.tensor_scalar(past[:, :], idf[:, :], n_experts, None, ALU.is_lt).then_inc(set_step, 1)
            dve.wait_ge(set_step, 4)
            dve.scalar_tensor_tensor(out=valid[:, :], in0=idf[:, :], scalar=0.0, in1=past[:, :], op0=ALU.is_ge,
                                     op1=ALU.mult).then_inc(set_step, 1)
            dve.wait_ge(set_step, 5)
            dve.tensor_scalar(invalid[:, :], valid[:, :], -1.0, 1.0, ALU.mult, ALU.add).then_inc(set_step, 1)
            dve.wait_ge(set_step, 6)
            with dve.Fori(0, B // 2) as pair:
                for s in range(2):
                    b = pair * 2 + s
                    base = b * NORM_STEPS
                    dve.wait_ge(expert_loaded[s], pair * 48 + 48)
                    dve.tensor_scalar(keep[:, s, :], ident[0:A, 0:A], invalid[:, bass.ds(b, 1)], None, ALU.mult).then_inc(kept, 1)
                    dve.wait_ge(kept, b + 1)
                    dve.wait_ge(expert_turned, b + 1)
                    dve.scalar_tensor_tensor(out=add[:, s, :], in0=e_b[:, s, :], scalar=valid[:, bass.ds(b, 1)],
                                             in1=e_emb[:, s, :], op0=ALU.mult, op1=ALU.add)
                    dve.scalar_tensor_tensor(out=e_t[:, s, :], in0=bank[1][0:A, 0:A], scalar=valid[:, bass.ds(b, 1)],
                                             in1=keep[:, s, :], op0=ALU.mult, op1=ALU.add).then_inc(expert_made, 1)
                    dve.wait_ge(x_loaded[s], pair * 16 + 16)
                    dve.tensor_tensor(xb[:, :, :], x[:, s, :, :], over_rows(up_b[:, :]), ALU.add).then_inc(xb_made, 1)
                    dve.wait_ge(xb_made, b + 1)
                    for i in range(2):
                        dve.wait_ge(up_done, b * 2 + i + 1)
                        dve.tensor_tensor(xb[:, 2 * i:2 * i + 2, :], bank[2 + i][:, :].rearrange("p (t d) -> p t d", d=D),
                                          xb[:, 2 * i:2 * i + 2, :], ALU.add).then_inc(summed, 1)
                    dve.wait_ge(summed, b * 2 + 2)
                    dve.wait_ge(y_stored, b * 16)
                    layer_norm(dve, dve_passed, xb, y, stats, mv, nt, 1e-5, norm_step, base)
                    dve.wait_ge(norm_step, base + NORM_STEPS)
                    dve.tensor_tensor(y[:, :, :], y[:, :, :], over_rows(gamma[:, :]), ALU.mult).then_inc(scaled, 1)
                    dve.wait_ge(scaled, b + 1)
                    dve.tensor_tensor(y[:, :, :], y[:, :, :], over_rows(beta[:, :]), ALU.add).then_inc(y_made, 1)


def biased_attention_layer(nc, x_in, x_out, w, c, scratch, sems):
    qk_dram, ada_dram = scratch["halves"], scratch["ada"]
    with ExitStack() as ctx:
        def sb(name, shape, dt=F32):
            return ctx.enter_context(nc.sbuf_tensor("b_" + name, shape, dt))

        def sem(name):
            sems[name] = nc.alloc_semaphore("b_" + name)
            return sems[name]

        bank = [ctx.enter_context(nc.psum_tensor(f"b_bank{i}", [P, 512], F32)) for i in range(2)]
        flips = ctx.enter_context(nc.psum_tensor("b_flips", [P, 4, 512], F32))
        o_bank = ctx.enter_context(nc.psum_tensor("b_obank", [P, 512], F32))
        n_bank = ctx.enter_context(nc.psum_tensor("b_nbank", [P, 512], F32))
        F0, F1, F2, F3 = (flips[:, i, :] for i in range(4))

        w_hi, w_lo = sb("w_hi", [P, 12 * 512], F32R), sb("w_lo", [P, 12 * 512], F32R)

        def weight(at, n, k):
            return tuple(x[:, at:at + n * k].rearrange("p (k n) -> p k n", k=k) for x in (w_hi, w_lo))

        wq, wk, wv, wo = (weight(512 * i, D, DK) for i in range(4))
        w1, w2 = weight(2048, F, DK), weight(4096, D, FK)
        ident, ident_bf = sb("ident", [P, P]), sb("ident_bf", [P, P], BF16)
        bq, bk = sb("bq", [P, DK]), sb("bk", [P, DK])
        b1, g2, be2 = sb("b1", [P, FK]), sb("g2", [P, DK]), sb("be2", [P, DK])
        bv, bo, b2 = sb("bv", [P, D]), sb("bo", [P, D]), sb("b2", [P, D])
        x = sb("x", [P, T, D])
        res = sb("res", [P, T, D])
        ctxt = sb("ctxt", [P, T, D])
        xt_hi, xt_lo = sb("xt_hi", [P, DK, S], F32R), sb("xt_lo", [P, DK, S], F32R)
        ct_hi, ct_lo = sb("ct_hi", [P, DK, S], F32R), sb("ct_lo", [P, DK, S], F32R)
        y = sb("y", [P, 2, S])
        v_one = sb("v_one", [P, T, H, 32])
        q_stack, k_stack = sb("q_stack", [P, 4, S], F32R), sb("k_stack", [P, 4, S], F32R)
        mask_u8, mask_add = sb("mask_u8", [P, T, S], U8), sb("mask_add", [P, T, S], BF16)
        bias = sb("bias", [P, 4, T, S])
        shared_at = nc.sbuf_base
        scores = sb("scores", [P, 2, T, S])
        ring = nc.alloc_sbuf_tensor_at("b_ring", [P, 2, 4, S], F32R, offset=shared_at)
        ring_hi, ring_lo = ring[:, 0, :, :], ring[:, 1, :, :]
        less_max = sb("less_max", [P, 2, T])
        probs = sb("probs", [P, SLOTS, T, S])
        o_sb = sb("o_sb", [P, S])
        one_over = sb("one_over", [P, T, 4])
        ada = sb("ada", [P, 2, D])
        stats, mv, nt = sb("stats", [P, T, 6]), sb("mv", [P, T, 2]), sb("nt", [P, 4, T])
        emb = sb("emb", [P, 8, B])
        tstep = sb("tstep", [P, B], I32)
        freq = sb("freq", [P, 1])
        adarow, adab = o_sb[0:B, :], y[0:B, 0, :]

        pool_passed, dve_passed = sem("pool_passed"), sem("dve_passed")
        small_loaded, ada_in_loaded, weights_loaded, mlp_loaded = (
            sem(n) for n in ("small_loaded", "ada_in_loaded", "weights_loaded", "mlp_loaded"))
        sp_passed = sem("sp_passed")
        halves_made, set_step, zeros_set, attn_set = sem("halves_made"), sem("set_step"), sem("zeros_set"), sem("attn_set")
        w_low, sin_done, ada_done, ada_stored = sem("w_low"), sem("sin_done"), sem("ada_done"), sem("ada_stored")
        x_loaded, mask_loaded, ada_loaded = sem("x_loaded"), sem("mask_loaded"), sem("ada_loaded")
        bias_loaded = [sem(f"bias_loaded{i}") for i in range(4)]
        x_step, norm_step, res_begun, res_step, mask_made = (
            sem(n) for n in ("x_step", "norm_step", "res_begun", "res_step", "mask_made"))
        x_flipped, x_high, x_low, projected, part_hi, part_lo, v_projected, v_ready = (
            sem(n) for n in ("x_flipped", "x_high", "x_low", "projected", "part_hi", "part_lo", "v_projected", "v_ready"))
        halves_stored, stack_loaded = sem("halves_stored"), [sem(f"stack_loaded{i}") for i in range(4)]
        scores_ready, scored, shifted_outer, shifted_inner = (
            sem(n) for n in ("scores_ready", "scored", "shifted_outer", "shifted_inner"))
        turned, exped, weighed, o_copied, o_turned, inverted, ctx_made = (
            sem(n) for n in ("turned", "exped", "weighed", "o_copied", "o_turned", "inverted", "ctx_made"))
        flipped, c_high, c_low, affine_made, attn_out, first_res = (
            sem(n) for n in ("flipped", "c_high", "c_low", "affine_made", "attn_out", "first_res"))
        up_done, gelu_done, ff_hi, ff_lo, down_done, out_ready, out_stored = (
            sem(n) for n in ("up_done", "gelu_done", "ff_hi", "ff_lo", "down_done", "out_ready", "out_stored"))

        def load_stack(eng, group):
            heads = qk_dram[:, group * 64:group * 64 + 64, :].rearrange("c (h r) n -> c r h n", r=DH)
            for i in range(4):
                at = 64 * (group % 2) + DH * i
                eng.dma_start(q_stack[at:at + DH, :, :].bitcast(F32), heads[i % 2]).then_inc(stack_loaded[group], 16)
                eng.dma_start(k_stack[at:at + DH, :, :].bitcast(F32), heads[2 + i // 2]).then_inc(stack_loaded[group], 16)

        block = ctx.enter_context(nc.Block())

        @block.sync
        def _(sp):
            raw = bias
            for i, name in enumerate(("Wq", "Wk", "Wv", "Wo")):
                sp.dma_start(raw[:, 0, i, :].rearrange("p (k n) -> p k n", k=DK),
                             w[name].rearrange("(k p) n -> p k n", p=P)).then_inc(weights_loaded, 16)
            sp.dma_start(raw[:, 3, 0:2, :], w["W_ada"].rearrange("(k p) n -> p k n", p=P)).then_inc(weights_loaded, 16)

            def load_x(b):
                sp.dma_start(x[:, :, :], x_in[bass.ds(b, 1)].rearrange("b (t p) d -> p (b t) d", p=P)).then_inc(x_loaded, 16)

            def load_ada(b):
                sp.dma_start(ada[:, :, :].rearrange("p a d -> p (a d)"),
                             ada_dram[bass.ds(b, 1), :].to_broadcast([P, 2 * D])).then_inc(ada_loaded, 16)

            def load_mask(b):
                sp.dma_start(mask_u8[:, :, :], c["mask"][bass.ds(b, 1)].rearrange("b (t p) k -> p (b t) k", p=P)).then_inc(mask_loaded, 16)

            def load_bias(b, n):
                sp.dma_start(bias[:, n % 4, :, :], c["bias"][bass.ds(b * H + n, 1)].rearrange("h (t p) k -> p (h t) k", p=P)
                             ).then_inc(bias_loaded[n % 4], 16)

            load_x(0)
            load_mask(0)
            sp.dma_start(raw[:, 1, :, :].rearrange("p t s -> p (t s)").rearrange("p (k n) -> p k n", k=DK),
                         w["W1"].rearrange("(k p) n -> p k n", p=P)).then_inc(mlp_loaded, 16)
            sp.dma_start(raw[:, 2, :, :].rearrange("p t s -> p (t s)").rearrange("p (k n) -> p k n", k=FK),
                         w["W2"].rearrange("(k p) n -> p k n", p=P)).then_inc(mlp_loaded, 16)
            sp.wait_ge(ada_done, 3)
            sp.dma_start(ada_dram, adarow).then_inc(ada_stored, 16)
            sp.wait_ge(ada_stored, 16)
            load_ada(0)
            def spread_halves(b):
                for n in range(4):
                    sp.wait_ge(part_lo, b * 4 + n + 1)
                    part = qk_dram[2 * (n // 2):2 * (n // 2) + 2, (n % 2) * P:(n % 2 + 1) * P, :]
                    sp.dma_start(part.rearrange("c p n -> p c n"), ring[:, :, n, :].bitcast(F32)).then_inc(halves_stored, 16)
                sp.wait_ge(halves_stored, b * 64 + 64)
                load_stack(sp, 0)
                load_stack(sp, 1)

            spread_halves(0)
            sp.wait_ge(w_low, 3)
            for n in range(4):
                load_bias(0, n)

            def batch(b, last):
                for n in range(12 if last else H):
                    sp.wait_ge(scored, b * 64 + 4 * n + 4)
                    settle(sp, sp_passed)
                    load_bias(b, n + 4)
                    if n == 6 and not last:
                        sp.wait_ge(res_begun, b + 1)
                        settle(sp, sp_passed)
                        load_x(b + 1)
                        load_ada(b + 1)
                        sp.wait_ge(mask_made, b + 1)
                        settle(sp, sp_passed)
                        load_mask(b + 1)
                if not last:
                    spread_halves(b + 1)
                sp.wait_ge(out_ready, b * T + T)
                sp.dma_start(x_out[bass.ds(b, 1)].rearrange("b (t p) d -> p (b t) d", p=P), res[:, :, :]).then_inc(out_stored, 16)

            with sp.Fori(0, B - 1) as b:
                batch(b, False)
            batch(B - 1, True)
            sp.wait_ge(out_stored, 16 * B)

        @block.gpsimd
        def _(pool):
            bc = lambda a, n: a.rearrange("(o n) -> o n", o=1).to_broadcast([n, a.shape[0]])
            cols = lambda a: a.rearrange("(k p) -> p k", p=P)
            for dst, src in ((bq[:, :], cols(w["bq"])), (bk[:, :], cols(w["bk"])), (bv[:, :], bc(w["bv"], P)),
                             (bo[:, :], bc(w["bo"], P)), (b1[:, :], cols(w["b1"])), (g2[:, :], cols(w["g2"])),
                             (be2[:, :], cols(w["beta2"])), (b2[:, :], bc(w["b2"], P))):
                pool.dma_start(dst, src, allow_slow_non_contiguous=True).then_inc(small_loaded, 16)
            pool.memset(v_one[:, :, :, :], 0.0).then_inc(zeros_set, 1)
            pool.wait_ge(zeros_set, 1)
            pool.memset(v_one[:, :, :, DH:DH + 1], 1.0).then_inc(zeros_set, 1)

            def convert_mask(b):
                pool.wait_ge(mask_loaded, b * 16 + 16)
                pool.wait_ge(scored, b * 64)
                settle(pool, pool_passed)
                pool.tensor_scalar(mask_add[:, :, :], mask_u8[:, :, :], MASKED, None, ALU.mult).then_inc(mask_made, 1)

            def batch(b, last):
                for group in (2, 3):
                    pool.wait_ge(scored, b * 64 + 16 * (group - 1))
                    settle(pool, pool_passed)
                    load_stack(pool, group)
                if not last:
                    convert_mask(b + 1)

            convert_mask(0)
            with pool.Fori(0, B - 1) as b:
                batch(b, False)
            batch(B - 1, True)

        @block.tensor
        def _(pe):
            pe.wait_ge(sin_done, 2)
            pe.wait_ge(weights_loaded, 80)
            for k in range(2):
                last = pe.matmul(o_bank[0:B, :], emb[:, 6 + k, :], bias[:, 3, k, :], start=k == 0, stop=k == 1)
            last.then_inc(ada_done, 1)

            def halves(m, k, lo, n):
                return tuple(x[:, k, lo:lo + n] for x in m)

            xt, ct = (xt_hi, xt_lo), (ct_hi, ct_lo)

            def flip_x(b):
                pe.wait_ge(x_step, b * X_STEPS + X_STEPS)
                pe.wait_ge(scored, b * 64)
                flip(pe, (bank[0], bank[1]), x, ident[:, :], x_flipped)

            def project_qk(b):
                pe.wait_ge(x_low, b * 2 + 2)
                for n, (m, out) in enumerate(((wq, F0), (wq, F1), (wk, F2), (wk, F3))):
                    for k in range(DK):
                        last = product(pe, out, halves(m, k, (n % 2) * P, P), halves(xt, k, 0, S), k == 0, k == DK - 1)
                    last.then_inc(projected, 1)

            def project_v(b):
                for t in range(T):
                    out = (o_bank, n_bank)[t // 2][:, (t % 2) * D:(t % 2 + 1) * D]
                    for k in range(DK):
                        last = product(pe, out, halves(xt, k, t * P, P), halves(wv, k, 0, D), k == 0, k == DK - 1)
                    if t % 2:
                        last.then_inc(v_projected, 1)

            def batch(b, last_batch):
                def score(n, t):
                    if n == 0 and t == 0:
                        pe.wait_ge(mask_made, b + 1)
                        pe.wait_ge(gelu_done, b * FK)
                    if n % 4 == 0 and t == 0:
                        pe.wait_ge(stack_loaded[n // 4], b * 128 + 128)
                    if 4 * n + t >= 2:
                        pe.wait_ge(scored, b * 64 + 4 * n + t - 1)
                    rows = slice(64 * (n // 4 % 2), 64 * (n // 4 % 2) + 64)
                    pe.matmul(bank[t % 2][:, :], q_stack[rows, n % 4, t * P:(t + 1) * P], k_stack[rows, n % 4, :],
                              start=True, stop=False)
                    pe.matmul(bank[t % 2][:, :], ident_bf[:, :], mask_add[:, t, :], start=False,
                              stop=True).then_inc(scores_ready, 1)

                def turn(n, kt):
                    if n == 0 and kt == 0:
                        pe.wait_ge(out_ready, b * T)
                        pe.wait_ge(part_lo, b * 4 + 4)
                    if kt == 0:
                        pe.wait_ge(shifted_outer, b * 32 + 2 * n + 2)
                        pe.wait_ge(shifted_inner, b * 32 + 2 * n + 2)
                    if kt % 2 == 0 and n:
                        pe.wait_ge(exped, b * 32 + 2 * n - 1 + kt // 2)
                    for t in range(T):
                        last = pe.transpose(flips[:, kt, t * P:(t + 1) * P],
                                            scores[:, n % 2, t, kt * P:(kt + 1) * P], ident[:, :])
                    last.then_inc(turned, 1)

                def weigh(group, kt):
                    if kt == 0:
                        pe.wait_ge(exped, b * 32 + 8 * group + 8)
                    if kt == 0 and group:
                        pe.wait_ge(o_copied, b * 4 + group)
                    elif kt == 0:
                        pe.wait_ge(v_ready, b * 2 + 2)
                    for j in range(4):
                        last = pe.matmul(o_bank[32 * j:32 * j + 32, :], v_one[:, kt, 4 * group + j, :],
                                         probs[:, (4 * group + j) % SLOTS, kt, :], start=kt == 0, stop=kt == T - 1,
                                         skip_group_check=True)
                    if kt == T - 1:
                        last.then_inc(weighed, 1)

                def turn_back(group):
                    pe.wait_ge(o_copied, b * 4 + group + 1)
                    pe.wait_ge(ctx_made, b * 4 + group)
                    for t in range(T):
                        last = pe.transpose(n_bank[:, t * P:(t + 1) * P], o_sb[:, t * P:(t + 1) * P], ident[:, :])
                    last.then_inc(o_turned, 1)

                for step in range(T * H + LAG):
                    if step < T * H:
                        score(step // T, step % T)
                    if step >= LAG:
                        turn((step - LAG) // T, (step - LAG) % T)
                    group, at = divmod(step - 4 * T - LAG - 1, 4 * T)
                    if 0 <= group < 3 and at < T:
                        weigh(group, at)
                    if 0 <= group < 3 and at == T + 2:
                        turn_back(group)
                if not last_batch:
                    flip_x(b + 1)
                for kt in range(T):
                    weigh(3, kt)
                turn_back(3)
                if not last_batch:
                    project_qk(b + 1)
                pe.wait_ge(ctx_made, b * 4 + 4)
                if last_batch:
                    pe.wait_ge(scored, B * 64)
                flip(pe, (bank[0], bank[1]), ctxt, ident[:, :], flipped)
                if not last_batch:
                    project_v(b + 1)
                    pe.wait_ge(part_lo, (b + 1) * 4 + 2)
                pe.wait_ge(c_low, b * 4 + 2)
                for t in range(T):
                    out = (F0, F1)[t // 2][:, (t % 2) * D:(t % 2 + 1) * D]
                    for k in range(DK):
                        last = product(pe, out, halves(ct, k, t * P, P), halves(wo, k, 0, D), k == 0, k == DK - 1)
                    if t % 2:
                        last.then_inc(attn_out, 1)
                pe.wait_ge(norm_step, b * NORM_STEPS + NORM_STEPS)
                flip(pe, (bank[0], bank[1]), ctxt, ident[:, :], flipped)
                pe.wait_ge(c_low, b * 4 + 4)
                if not last_batch:
                    pe.wait_ge(part_lo, (b + 1) * 4 + 4)
                    pe.wait_ge(v_ready, (b + 1) * 2 + 2)
                outs = (F2, F3, o_bank[:, :], n_bank[:, :])

                def down(m):
                    pe.wait_ge(ff_lo, b * FK + m + 1)
                    for t in range(T):
                        last = product(pe, outs[t][:, 0:D], halves((ring_hi, ring_lo), m % 4, t * P, P),
                                       halves(w2, m, 0, D), m == 0, m == FK - 1)
                    last.then_inc(down_done, 1)

                for m in range(FK):
                    if m >= 2:
                        pe.wait_ge(gelu_done, b * FK + m - 1)
                    for k in range(DK):
                        last = product(pe, bank[m % 2][:, :], halves(w1, k, m * P, P), halves(ct, k, 0, S), k == 0, k == DK - 1)
                    last.then_inc(up_done, 1)
                    if m >= 2:
                        down(m - 2)
                down(FK - 2)
                down(FK - 1)

            pe.wait_ge(w_low, 1)
            flip_x(0)
            project_qk(0)
            pe.wait_ge(ada_done, 3)
            project_v(0)
            pe.wait_ge(w_low, 3)
            with pe.Fori(0, B - 1) as b:
                batch(b, False)
            batch(B - 1, True)

        @block.scalar
        def _(act):
            bc = lambda a, n: a.rearrange("(o n) -> o n", o=1).to_broadcast([n, a.shape[0]])
            for dst, src in ((freq[:, :], c["freq"]), (tstep[:, :], bc(c["timestep"], P)), (ident[:, :], c["ident"]),
                             (adab, bc(w["b_ada"], B))):
                act.dma_start(dst, src, allow_slow_non_contiguous=True).then_inc(ada_in_loaded, 16)
            act.wait_ge(set_step, SIN_READY)
            act.activation(emb[:, 4:6, :], emb[:, 2:4, :], ACT.Sin).then_inc(sin_done, 1)
            act.wait_ge(sin_done, 1)
            act.activation(emb[:, 6:8, :], emb[:, 4:6, :], ACT.Silu).then_inc(sin_done, 1)

            def weight_high(n):
                act.activation(w_hi[:, n * 2048:(n + 1) * 2048], bias[:, n, :, :].rearrange("p t s -> p (t s)"),
                               ACT.Copy).then_inc(halves_made, 1)

            def x_highs(b):
                for k in range(DK):
                    act.wait_ge(x_flipped, b * 2 + k + 1)
                    act.activation(xt_hi[:, k, :], bank[k][:, :], ACT.Copy).then_inc(x_high, 1)

            def part_highs(b):
                for n, add in enumerate((bq[:, 0:1], bq[:, 1:2], bk[:, 0:1], bk[:, 1:2])):
                    act.wait_ge(projected, b * 4 + n + 1)
                    act.activation(ring_hi[:, n, :], flips[:, n, :], ACT.Identity, bias=add).then_inc(part_hi, 1)

            def batch(b, last):
                def copy_o(group):
                    act.wait_ge(weighed, b * 4 + group + 1)
                    act.wait_ge(o_turned, b * 4 + group)
                    act.activation(o_sb[:, :], o_bank[:, :], ACT.Copy).then_inc(o_copied, 1)

                for n in range(H + 1):
                    for half in range(2):
                        if n < H:
                            act.wait_ge(scored, b * 64 + 4 * n + half + 2)
                            act.activation(scores[:, n % 2, half + 1, :], scores[:, n % 2, half + 1, :], ACT.Identity,
                                           bias=less_max[:, n % 2, half + 1:half + 2], scale=-1.0).then_inc(shifted_inner, 1)
                        if n % 4 == 2 and n > 4 and half == 0:
                            copy_o(n // 4 - 1)
                        if n:
                            act.wait_ge(turned, b * 64 + 4 * n + 2 * half - 2)
                            act.activation(probs[:, (n - 1) % SLOTS, 2 * half:2 * half + 2, :],
                                           flips[:, 2 * half:2 * half + 2, :], ACT.Exp).then_inc(exped, 1)
                if not last:
                    x_highs(b + 1)
                copy_o(3)
                if not last:
                    part_highs(b + 1)
                for k in range(DK):
                    act.wait_ge(flipped, b * 4 + k + 1)
                    act.activation(ct_hi[:, k, :], bank[k][:, :], ACT.Copy).then_inc(c_high, 1)
                for k in range(DK):
                    act.wait_ge(flipped, b * 4 + 3 + k)
                    act.wait_ge(ff_lo, b * FK)
                    act.activation(y[:, k, :], bank[k][:, :], ACT.Identity, bias=be2[:, k:k + 1],
                                   scale=g2[:, k:k + 1]).then_inc(affine_made, 1)
                for m in range(FK):
                    act.wait_ge(up_done, b * FK + m + 1)
                    if m < 2:
                        act.wait_ge(c_low, b * 4 + 3 + m)
                    else:
                        act.wait_ge(ff_lo, b * FK + m - 1)
                    act.activation(y[:, m % 2, :], bank[m % 2][:, :], ACT.Gelu_apprx_sigmoid,
                                   bias=b1[:, m:m + 1]).then_inc(gelu_done, 1)

            act.wait_ge(halves_made, 1)
            weight_high(0)
            x_highs(0)
            act.wait_ge(attn_set, 1)
            part_highs(0)
            act.wait_ge(mlp_loaded, 32)
            weight_high(1)
            weight_high(2)
            act.wait_ge(small_loaded, 128)
            with act.Fori(0, B - 1) as b:
                batch(b, False)
            batch(B - 1, True)

        @block.vector
        def _(dve):
            dve.wait_ge(ada_in_loaded, 16 * 4)
            step = [0]

            def link(ins):
                step[0] += 1
                ins.then_inc(set_step, 1)
                dve.wait_ge(set_step, step[0])

            angle, turns, r, cosr = emb[:, 0, :], emb[:, 1, :], emb[:, 2, :], emb[:, 3, :]
            link(dve.tensor_copy(r, tstep[:, :]))
            link(dve.tensor_scalar(angle, r, 40.0, freq[:, 0:1], ALU.mult, ALU.mult))
            link(dve.tensor_scalar(turns, angle, 1.0 / (2 * math.pi), ROUND, ALU.mult, ALU.add))
            link(dve.tensor_scalar(turns, turns, -ROUND, None, ALU.add))
            link(dve.tensor_copy(r, angle))
            for part in TURN:
                link(dve.scalar_tensor_tensor(out=r, in0=turns, scalar=-part, in1=r, op0=ALU.mult, op1=ALU.add))
            link(dve.tensor_scalar(cosr, r, math.pi / 2, None, ALU.add))
            link(dve.tensor_scalar(angle, cosr, math.pi, -2 * math.pi, ALU.is_gt, ALU.mult))
            link(dve.tensor_tensor(cosr, cosr, angle, ALU.add))
            link(dve.tensor_scalar(emb[:, 2:4, :], emb[:, 2:4, :], PI_BELOW, -PI_BELOW, ALU.min, ALU.max))
            assert step[0] == SIN_READY
            dve.wait_ge(weights_loaded, 80)
            dve.tensor_scalar(bias[:, 0, 0, :], bias[:, 0, 0, :], SC, None, ALU.mult).then_inc(halves_made, 1)
            dve.tensor_copy(ident_bf[:, :], ident[:, :]).then_inc(set_step, 1)
            dve.wait_ge(ada_done, 1)
            dve.tensor_tensor(adarow, o_bank[0:B, :], adab, ALU.add).then_inc(ada_done, 1)
            dve.wait_ge(ada_done, 2)
            dve.tensor_scalar(adarow[:, 0:D], adarow[:, 0:D], 1.0, None, ALU.add).then_inc(ada_done, 1)
            dve.wait_ge(small_loaded, 128)
            dve.tensor_scalar(bq[:, :], bq[:, :], SC, None, ALU.mult).then_inc(attn_set, 1)

            def weight_low(n):
                dve.wait_ge(halves_made, 2 + n)
                dve.tensor_tensor(w_lo[:, n * 2048:(n + 1) * 2048], bias[:, n, :, :].rearrange("p t s -> p (t s)"),
                                  w_hi[:, n * 2048:(n + 1) * 2048].bitcast(F32), ALU.subtract).then_inc(w_low, 1)

            def norm_x(b, n):
                at = b * X_STEPS
                if n == 0:
                    dve.wait_ge(x_loaded, b * 16 + 16)
                    for t in range(T):
                        norm_stats(dve, x, stats, t, x_step)
                if n == 1:
                    norm_root(dve, dve_passed, stats, mv, nt, 1e-5, x_step, at)
                if n == 2:
                    dve.wait_ge(ada_loaded, b * 16 + 16)
                    dve.wait_ge(x_step, at + NORM_ROOT)
                    for t in range(T):
                        dve.scalar_tensor_tensor(out=x[:, t, :], in0=x[:, t, :], scalar=mv[:, t, 0:1], in1=ada[:, 0, :],
                                                 op0=ALU.subtract, op1=ALU.mult).then_inc(x_step, 1)
                if n == 3:
                    for t in range(T):
                        dve.wait_ge(x_step, at + NORM_ROOT + T + t)
                        dve.scalar_tensor_tensor(out=x[:, t, :], in0=x[:, t, :], scalar=nt[:, 2, t:t + 1], in1=ada[:, 1, :],
                                                 op0=ALU.mult, op1=ALU.add).then_inc(x_step, 1)

            def x_lows(b):
                for k in range(DK):
                    dve.wait_ge(x_high, b * 2 + k + 1)
                    dve.tensor_tensor(xt_lo[:, k, :], bank[k][:, :], xt_hi[:, k, :].bitcast(F32), ALU.subtract).then_inc(x_low, 1)

            def part_lows(b):
                for n, add in enumerate((bq[:, 0:1], bq[:, 1:2], bk[:, 0:1], bk[:, 1:2])):
                    dve.wait_ge(part_hi, b * 4 + n + 1)
                    dve.scalar_tensor_tensor(out=ring_lo[:, n, :], in0=flips[:, n, :], scalar=add,
                                             in1=ring_hi[:, n, :].bitcast(F32), op0=ALU.add, op1=ALU.subtract).then_inc(part_lo, 1)

            def take_v(b):
                for i, src in enumerate((o_bank, n_bank)):
                    dve.wait_ge(v_projected, b * 2 + i + 1)
                    dve.tensor_tensor(v_one[:, 2 * i:2 * i + 2, :, 0:DH], src[:, :].rearrange("p (t h d) -> p t h d", t=2, d=DH),
                                      over_rows(bv[:, :], 2).rearrange("p t (h d) -> p t h d", d=DH), ALU.add).then_inc(v_ready, 1)

            def batch(b, last):
                def normalise(group):
                    dve.wait_ge(o_turned, b * 4 + group + 1)
                    o = n_bank[:, :].rearrange("p (t h c) -> p t h c", t=T, h=4)
                    dve.reciprocal(one_over[:, :, :], o[:, :, :, DH]).then_inc(inverted, 1)
                    dve.wait_ge(inverted, b * 4 + group + 1)
                    dve.tensor_tensor(ctxt[:, :, group * 64:group * 64 + 64].rearrange("p t (h d) -> p t h d", d=DH),
                                      o[:, :, :, 0:DH], one_over[:, :, :].unsqueeze(3).to_broadcast([P, T, 4, DH]),
                                      ALU.mult).then_inc(ctx_made, 1)

                dve.wait_ge(halves_stored, b * 64 + 64)
                for n in range(H):
                    for t in range(T):
                        if t == 0:
                            dve.wait_ge(bias_loaded[n % 4], b * 64 + 16 * (n // 4 + 1))
                            if n >= 2:
                                dve.wait_ge(turned, b * 64 + 4 * n - 4)
                        dve.wait_ge(scores_ready, b * 64 + 4 * n + t + 1)
                        settle(dve, dve_passed)
                        dve.tensor_tensor_reduce(out=scores[:, n % 2, t, :], in0=bank[t % 2][:, :], in1=bias[:, n % 4, t, :],
                                                 scale=-1.0, scalar=3.0e38, op0=ALU.add, op1=ALU.min,
                                                 accum_out=less_max[:, n % 2, t:t + 1]).then_inc(scored, 1)
                        if t in (0, 3):
                            dve.wait_ge(scored, b * 64 + 4 * n + t + 1)
                            dve.tensor_scalar(scores[:, n % 2, t, :], scores[:, n % 2, t, :], -1.0, less_max[:, n % 2, t:t + 1],
                                              ALU.mult, ALU.add).then_inc(shifted_outer, 1)
                        if n % 4 == 3 and n > 4 and t == 2:
                            normalise(n // 4 - 1)
                        if n == 3 and t == 1:
                            dve.wait_ge(out_stored, b * 16)
                            dve.tensor_tensor(res[:, :, :], x[:, :, :], over_rows(bo[:, :]), ALU.add).then_inc(res_begun, 1)
                        if not last and t == 3 and 8 <= n < 12:
                            norm_x(b + 1, n - 8)
                if not last:
                    x_lows(b + 1)
                normalise(3)
                if not last:
                    part_lows(b + 1)
                for k in range(DK):
                    dve.wait_ge(c_high, b * 2 + k + 1)
                    dve.tensor_tensor(ct_lo[:, k, :], bank[k][:, :], ct_hi[:, k, :].bitcast(F32), ALU.subtract).then_inc(c_low, 1)
                if not last:
                    take_v(b + 1)
                dve.wait_ge(res_begun, b + 1)
                for i in range(2):
                    dve.wait_ge(attn_out, b * 2 + i + 1)
                    dve.tensor_tensor(res[:, 2 * i:2 * i + 2, :], flips[:, i, :].rearrange("p (t d) -> p t d", d=D),
                                      res[:, 2 * i:2 * i + 2, :], ALU.add).then_inc(first_res, 1)
                dve.wait_ge(first_res, b * 2 + 2)
                layer_norm(dve, dve_passed, res, ctxt, stats, mv, nt, 1e-5, norm_step, b * NORM_STEPS)
                dve.wait_ge(norm_step, b * NORM_STEPS + NORM_STEPS)
                dve.tensor_tensor(res[:, :, :], res[:, :, :], over_rows(b2[:, :]), ALU.add).then_inc(res_step, 1)
                for k in range(DK):
                    dve.wait_ge(affine_made, b * 2 + k + 1)
                    dve.tensor_copy(ct_hi[:, k, :], y[:, k, :]).then_inc(ff_hi, 1)
                    dve.wait_ge(ff_hi, b * (DK + FK) + k + 1)
                    dve.tensor_tensor(ct_lo[:, k, :], y[:, k, :], ct_hi[:, k, :].bitcast(F32), ALU.subtract).then_inc(c_low, 1)
                if not last:
                    dve.wait_ge(halves_stored, (b + 1) * 64 + 64)
                for m in range(FK):
                    dve.wait_ge(gelu_done, b * FK + m + 1)
                    if m >= 4:
                        dve.wait_ge(down_done, b * FK + m - 3)
                    dve.tensor_copy(ring_hi[:, m % 4, :], y[:, m % 2, :]).then_inc(ff_hi, 1)
                    dve.wait_ge(ff_hi, b * (DK + FK) + DK + m + 1)
                    dve.tensor_tensor(ring_lo[:, m % 4, :], y[:, m % 2, :], ring_hi[:, m % 4, :].bitcast(F32),
                                      ALU.subtract).then_inc(ff_lo, 1)
                dve.wait_ge(down_done, b * FK + FK)
                dve.wait_ge(res_step, b + 1)
                for t, src in enumerate((F2, F3, o_bank[:, :], n_bank[:, :])):
                    dve.tensor_tensor(res[:, t, :], src[:, 0:D], res[:, t, :], ALU.add).then_inc(out_ready, 1)

            for n in range(2):
                norm_x(0, n)
            weight_low(0)
            for n in range(2, 4):
                norm_x(0, n)
            x_lows(0)
            part_lows(0)
            dve.wait_ge(zeros_set, 2)
            take_v(0)
            weight_low(1)
            weight_low(2)
            with dve.Fori(0, B - 1) as b:
                batch(b, False)
            batch(B - 1, True)


def expert_mlp_layer(nc, x_in, x_out, w, c):
    n_experts = w["Wi"].shape[0]
    with ExitStack() as ctx:
        def sb(name, shape, dt=F32):
            return ctx.enter_context(nc.sbuf_tensor("c_" + name, shape, dt))

        def sem(name):
            return nc.alloc_semaphore("c_" + name)

        bank = [ctx.enter_context(nc.psum_tensor(f"c_bank{i}", [P, 512], F32)) for i in range(2)]
        flips = ctx.enter_context(nc.psum_tensor("c_flips", [P, DK, 512], F32))
        outs = [ctx.enter_context(nc.psum_tensor(f"c_out{i}", [P, 512], F32)) for i in range(4)]
        ident, id_row = sb("ident", [P, P]), sb("id_row", [1, B], I32)
        x, y = sb("x", [P, 2, T, D]), sb("y", [P, T, D])
        raw = sb("raw", [P, 2, 2048])
        w_hi, w_lo = sb("w_hi", [P, 2, 2, 2048], F32R), sb("w_lo", [P, 2, 2, 2048], F32R)
        bi = sb("bi", [P, 2, FK])
        bo, gamma, beta = sb("bo", [P, 2, D]), sb("gamma", [P, 2, D]), sb("beta", [P, 2, D])
        xt_hi, xt_lo = sb("xt_hi", [P, DK, S], F32R), sb("xt_lo", [P, DK, S], F32R)
        g = sb("g", [P, 2, S])
        ring_hi, ring_lo = sb("ring_hi", [P, 4, S], F32R), sb("ring_lo", [P, 4, S], F32R)
        stats, mv, nt = sb("stats", [P, T, 6]), sb("mv", [P, T, 2]), sb("nt", [P, 4, T])

        dve_passed, pool_passed = sem("dve_passed"), sem("pool_passed")
        ids_loaded, ident_loaded = sem("ids_loaded"), sem("ident_loaded")
        x_loaded, raw_loaded, small_loaded = ([sem(f"{n}{s}") for s in range(2)] for n in ("x_loaded", "raw_loaded", "small_loaded"))
        w_hi_made, w_lo_made, flipped, hi_made, lo_made = (
            sem(n) for n in ("w_hi_made", "w_lo_made", "flipped", "hi_made", "lo_made"))
        up_done, gelu_done, ff_hi, ff_lo, down_done = (sem(n) for n in ("up_done", "gelu_done", "ff_hi", "ff_lo", "down_done"))
        biased, summed, norm_step, scaled, y_made, y_stored = (
            sem(n) for n in ("biased", "summed", "norm_step", "scaled", "y_made", "y_stored"))
        block = ctx.enter_context(nc.Block())

        @block.sync
        def _(sp):
            sp.dma_start(id_row[:, :], c["mlp_expert"].rearrange("(o n) -> o n", o=1)).then_inc(ids_loaded, 16)
            sp.dma_start(ident[:, :], c["ident"]).then_inc(ident_loaded, 16)
            sp.wait_ge(ids_loaded, 16)
            row = sp.alloc_register("c_expert")
            with sp.Fori(0, B // 2) as pair:
                for s in range(2):
                    b = pair * 2 + s
                    sp.reg_alu(row, sp.value_load(id_row[0:1, bass.ds(b, 1)]), 0, ALU.max)
                    sp.reg_alu(row, row, n_experts - 1, ALU.min)
                    e = sp.snap(row, min_val=0, max_val=n_experts - 1)
                    sp.wait_ge(y_made, pair * 2)
                    sp.dma_start(x[:, s, :, :], x_in[bass.ds(b, 1)].rearrange("b (t p) d -> p (b t) d", p=P)).then_inc(x_loaded[s], 16)
                    for dst, name in ((bo, "bo"), (gamma, "gamma"), (beta, "beta")):
                        sp.dma_start(dst[:, s, :], w[name][bass.ds(e, 1), :].to_broadcast([P, D])).then_inc(small_loaded[s], 16)
                    sp.dma_start(bi[:, s, :], w["bi"][bass.ds(e, 1)].rearrange("e (k p) -> p (e k)", p=P),
                                 allow_slow_non_contiguous=True).then_inc(small_loaded[s], 16)
                    for i, (name, k) in enumerate((("Wi", DK), ("Wo", FK))):
                        sp.wait_ge(w_lo_made, b * 2 + i)
                        if i == 0:
                            sp.wait_ge(w_lo_made, b * 2)
                        sp.dma_start(raw[:, i, :].rearrange("p (k n) -> p k n", k=k),
                                     w[name][bass.ds(e, 1)].rearrange("e (k p) n -> p (e k) n", p=P)).then_inc(raw_loaded[i], 16)
                for s in range(2):
                    sp.wait_ge(y_made, pair * 2 + s + 1)
                    sp.dma_start(x_out[bass.ds(pair * 2 + s, 1)].rearrange("b (t p) d -> p (b t) d", p=P), y[:, :, :]).then_inc(y_stored, 16)
            sp.wait_ge(y_stored, 16 * B)

        @block.gpsimd
        def _(pool):
            with pool.Fori(0, B // 2) as pair:
                for s in range(2):
                    b = pair * 2 + s
                    for i in range(2):
                        pool.wait_ge(raw_loaded[i], b * 16 + 16)
                        pool.wait_ge(y_made, pair * 2)
                        settle(pool, pool_passed)
                        pool.tensor_copy(w_hi[:, s, i, :], raw[:, i, :]).then_inc(w_hi_made, 1)
                        pool.wait_ge(w_hi_made, b * 2 + i + 1)
                        settle(pool, pool_passed)
                        pool.tensor_tensor(w_lo[:, s, i, :], raw[:, i, :], w_hi[:, s, i, :].bitcast(F32),
                                           ALU.subtract).then_inc(w_lo_made, 1)

        @block.tensor
        def _(pe):
            pe.wait_ge(ident_loaded, 16)
            xt = (xt_hi, xt_lo)
            with pe.Fori(0, B // 2) as pair:
                for s in range(2):
                    b = pair * 2 + s
                    w1 = tuple(m[:, s, 0, :].rearrange("p (k n) -> p k n", k=DK) for m in (w_hi, w_lo))
                    w2 = tuple(m[:, s, 1, :].rearrange("p (k n) -> p k n", k=FK) for m in (w_hi, w_lo))
                    pe.wait_ge(x_loaded[s], pair * 16 + 16)
                    flip(pe, (flips[:, 0, :], flips[:, 1, :]), x[:, s, :, :], ident[:, :], flipped)
                    pe.wait_ge(lo_made, b * 2 + 2)
                    pe.wait_ge(w_lo_made, b * 2 + 1)

                    def down(m):
                        if m == 0:
                            pe.wait_ge(w_lo_made, b * 2 + 2)
                            pe.wait_ge(summed, b * T)
                        pe.wait_ge(ff_lo, b * FK + m + 1)
                        for t in range(T):
                            a = tuple(r[:, m % 4, t * P:(t + 1) * P] for r in (ring_hi, ring_lo))
                            last = product(pe, outs[t][:, 0:D], a, tuple(x[:, m, :] for x in w2), m == 0, m == FK - 1)
                        last.then_inc(down_done, 1)

                    for m in range(FK):
                        if m >= 2:
                            pe.wait_ge(gelu_done, b * FK + m - 1)
                        for k in range(DK):
                            last = product(pe, bank[m % 2][:, :], tuple(x[:, k, m * P:(m + 1) * P] for x in w1),
                                           tuple(x[:, k, :] for x in xt), k == 0, k == DK - 1)
                        last.then_inc(up_done, 1)
                        if m >= 2:
                            down(m - 2)
                    down(FK - 2)
                    down(FK - 1)

        @block.scalar
        def _(act):
            with act.Fori(0, B // 2) as pair:
                for s in range(2):
                    b = pair * 2 + s
                    for k in range(DK):
                        act.wait_ge(flipped, b * 2 + k + 1)
                        act.wait_ge(up_done, b * FK)
                        act.activation(xt_hi[:, k, :], flips[:, k, :], ACT.Copy).then_inc(hi_made, 1)
                    act.wait_ge(small_loaded[s], pair * 64 + 64)
                    for m in range(FK):
                        act.wait_ge(up_done, b * FK + m + 1)
                        if m >= 2:
                            act.wait_ge(ff_lo, b * FK + m - 1)
                        act.activation(g[:, m % 2, :], bank[m % 2][:, :], ACT.Gelu, bias=bi[:, s, m:m + 1]).then_inc(gelu_done, 1)

        @block.vector
        def _(dve):
            with dve.Fori(0, B // 2) as pair:
                for s in range(2):
                    b = pair * 2 + s
                    base = b * NORM_STEPS
                    for k in range(DK):
                        dve.wait_ge(hi_made, b * 2 + k + 1)
                        dve.tensor_tensor(xt_lo[:, k, :], flips[:, k, :], xt_hi[:, k, :].bitcast(F32), ALU.subtract).then_inc(lo_made, 1)
                    dve.wait_ge(small_loaded[s], pair * 64 + 64)
                    dve.tensor_tensor(x[:, s, :, :], x[:, s, :, :], over_rows(bo[:, s, :]), ALU.add).then_inc(biased, 1)
                    for m in range(FK):
                        dve.wait_ge(gelu_done, b * FK + m + 1)
                        if m >= 4:
                            dve.wait_ge(down_done, b * FK + m - 3)
                        dve.tensor_copy(ring_hi[:, m % 4, :], g[:, m % 2, :]).then_inc(ff_hi, 1)
                        dve.wait_ge(ff_hi, b * FK + m + 1)
                        dve.tensor_tensor(ring_lo[:, m % 4, :], g[:, m % 2, :], ring_hi[:, m % 4, :].bitcast(F32),
                                          ALU.subtract).then_inc(ff_lo, 1)
                    dve.wait_ge(down_done, b * FK + FK)
                    dve.wait_ge(biased, b + 1)
                    for t in range(T):
                        dve.tensor_tensor(x[:, s, t, :], outs[t][:, 0:D], x[:, s, t, :], ALU.add).then_inc(summed, 1)
                    dve.wait_ge(summed, b * T + T)
                    dve.wait_ge(y_stored, b * 16)
                    layer_norm(dve, dve_passed, x[:, s, :, :], y, stats, mv, nt, 1e-12, norm_step, base)
                    dve.wait_ge(norm_step, base + NORM_STEPS)
                    dve.tensor_tensor(y[:, :, :], y[:, :, :], over_rows(gamma[:, s, :]), ALU.mult).then_inc(scaled, 1)
                    dve.wait_ge(scaled, b + 1)
                    dve.tensor_tensor(y[:, :, :], y[:, :, :], over_rows(beta[:, s, :]), ALU.add).then_inc(y_made, 1)


def causal_attention_layer(nc, x_in, x_out, w, c, scratch, sems):
    qk_dram = scratch["halves"]
    with ExitStack() as ctx:
        def sb(name, shape, dt=F32):
            return ctx.enter_context(nc.sbuf_tensor("d_" + name, shape, dt))

        def sem(name):
            return nc.alloc_semaphore("d_" + name)

        def shared(*names):
            return (sems[n] for n in names)

        bank = [ctx.enter_context(nc.psum_tensor(f"d_bank{i}", [P, 512], F32)) for i in range(2)]
        flips = ctx.enter_context(nc.psum_tensor("d_flips", [P, 4, 512], F32))
        o_bank = ctx.enter_context(nc.psum_tensor("d_obank", [P, 512], F32))
        n_bank = ctx.enter_context(nc.psum_tensor("d_nbank", [P, 512], F32))
        F0, F1, F2, F3 = (flips[:, i, :] for i in range(4))

        w_hi, w_lo = sb("w_hi", [P, 12 * 512], F32R), sb("w_lo", [P, 12 * 512], F32R)

        def weight(at, n, k):
            return tuple(x[:, at:at + n * k].rearrange("p (k n) -> p k n", k=k) for x in (w_hi, w_lo))

        wq, wk, wv, wo = (weight(512 * i, D, DK) for i in range(4))
        w1, w2 = weight(2048, F, DK), weight(4096, D, FK)
        ident, ident_bf, causal = sb("ident", [P, P]), sb("ident_bf", [P, P], BF16), sb("causal", [P, P])
        causal_qk, causal_kq = sb("causal_qk", [P, P], BF16), sb("causal_kq", [P, P], BF16)
        bq, bk, b1 = sb("bq", [P, DK]), sb("bk", [P, DK]), sb("b1", [P, FK])
        g1, be1, g2, be2 = (sb(n, [P, DK]) for n in ("g1", "be1", "g2", "be2"))
        bv, bo, b2 = sb("bv", [P, D]), sb("bo", [P, D]), sb("b2", [P, D])
        gates, gate = sb("gates", [P, B]), sb("gate", [P, 1])
        xn, x, res, ctxt = (sb(n, [P, T, D]) for n in ("xn", "x", "res", "ctxt"))
        xt_hi, xt_lo = sb("xt_hi", [P, DK, S], F32R), sb("xt_lo", [P, DK, S], F32R)
        ct_hi, ct_lo = sb("ct_hi", [P, DK, S], F32R), sb("ct_lo", [P, DK, S], F32R)
        y = sb("y", [P, 2, S])
        v_one = sb("v_one", [P, T, H, 32])
        q_stack, k_stack = sb("q_stack", [DH * 4 + 1, H, S], F32R), sb("k_stack", [DH * 4 + 1, H, S], F32R)
        less_max, max_row = sb("less_max", [P, 2, 4 * T]), sb("max_row", [4 * T, 2, P], F32R)
        shared_at = nc.sbuf_base
        probs = sb("probs", [P, SLOTS, T, S])
        ring = nc.alloc_sbuf_tensor_at("d_ring", [P, 2, 4, S], F32R, offset=shared_at)
        ring_hi, ring_lo = ring[:, 0, :, :], ring[:, 1, :, :]
        o_sb, one_over = sb("o_sb", [P, S]), sb("one_over", [P, T, 4])
        stats, mv, nt = sb("stats", [P, T, 6]), sb("mv", [P, T, 2]), sb("nt", [P, 4, T])

        early_loaded, small_loaded, weights_loaded, mlp_loaded, halves_made, set_step, pool_set, w_low = (
            sem(n) for n in ("early_loaded", "small_loaded", "weights_loaded", "mlp_loaded", "halves_made", "set_step",
                             "pool_set", "w_low"))
        xn_loaded, xn_step, x_affine, max_turned, row_made, shifted, exped, delta_step, mixed = (
            sem(n) for n in ("xn_loaded", "xn_step", "x_affine", "max_turned", "row_made", "shifted", "exped",
                             "delta_step", "mixed"))
        row_loaded = [sem("row_loaded0"), sem("row_loaded1")]
        dve_passed, sp_passed, x_loaded, norm_step, res_begun = shared("dve_passed", "sp_passed", "x_loaded", "norm_step", "res_begun")
        x_flipped, x_high, x_low, projected, part_hi, part_lo, v_projected, v_ready = shared(
            "x_flipped", "x_high", "x_low", "projected", "part_hi", "part_lo", "v_projected", "v_ready")
        halves_stored, first_stack, rest_stack, scores_ready, scored = shared(
            "halves_stored", "stack_loaded0", "stack_loaded1", "scores_ready", "scored")
        weighed, o_copied, o_turned, inverted, ctx_made = shared("weighed", "o_copied", "o_turned", "inverted", "ctx_made")
        flipped, c_high, c_low, affine_made, attn_out, first_res = shared(
            "flipped", "c_high", "c_low", "affine_made", "attn_out", "first_res")
        up_done, gelu_done, ff_hi, ff_lo, down_done, out_ready, out_stored = shared(
            "up_done", "gelu_done", "ff_hi", "ff_lo", "down_done", "out_ready", "out_stored")
        spread = lambda a: a.rearrange("(o n) -> o n", o=1).to_broadcast([P, a.shape[0]])
        cols = lambda a: a.rearrange("(k p) -> p k", p=P)
        row_step = lambda ap: ap.rearrange("b (t p) d -> p (b t) d", p=P)
        block = ctx.enter_context(nc.Block())
        raw = probs

        @block.sync
        def _(sp):
            def load_xn(b):
                sp.dma_start(xn[:, :, :], row_step(x_in[bass.ds(b - B, 1)])).then_inc(xn_loaded, 16)

            def load_x(b):
                sp.dma_start(x[:, :, :], row_step(x_in[bass.ds(b - B, 1)])).then_inc(x_loaded, 16)

            load_xn(B)
            for i, name in enumerate(("Wq", "Wk", "Wv", "Wo")):
                sp.dma_start(raw[:, 2, i, :].rearrange("p (k n) -> p k n", k=DK),
                             w[name].rearrange("(k p) n -> p k n", p=P)).then_inc(weights_loaded, 16)
            for i, (name, k) in enumerate((("W1", DK), ("W2", FK))):
                sp.dma_start(raw[:, 3 + i, :, :].rearrange("p t s -> p (t s)").rearrange("p (k n) -> p k n", k=k),
                             w[name].rearrange("(k p) n -> p k n", p=P)).then_inc(mlp_loaded, 16)
            load_x(B)

            def spread_halves(b):
                for n in range(4):
                    sp.wait_ge(part_lo, b * 4 + n + 1)
                    part = qk_dram[2 * (n // 2):2 * (n // 2) + 2, (n % 2) * P:(n % 2 + 1) * P, :]
                    sp.dma_start(part.rearrange("c p n -> p c n"), ring[:, :, n, :].bitcast(F32)).then_inc(halves_stored, 16)
                sp.wait_ge(halves_stored, b * 64 + 64)
                for first, last, loaded in ((0, 4, first_stack), (4, H, rest_stack)):
                    heads = qk_dram[:, first * DH:last * DH, :].rearrange("c (h r) n -> c r h n", r=DH)
                    for i in range(4):
                        rows = slice(DH * i, DH * i + DH)
                        sp.dma_start(q_stack[rows, first:last, :].bitcast(F32), heads[i % 2]).then_inc(loaded, 16)
                        sp.dma_start(k_stack[rows, first:last, :].bitcast(F32), heads[2 + i // 2]).then_inc(loaded, 16)

            def batch(b, last):
                for g in range(4):
                    if g == 0 and not last:
                        sp.wait_ge(x_flipped, b * 2 + 2)
                        settle(sp, sp_passed)
                        load_xn(b + 1)
                    sp.wait_ge(row_made, (b - B) * 4 + g + 1)
                    sp.dma_start(q_stack[4 * DH:4 * DH + 1, 4 * g:4 * g + 4, :].rearrange("o h (t n) -> o (h t) n", n=P).bitcast(F32),
                                 max_row[:, g % 2, :].bitcast(F32)).then_inc(row_loaded[g % 2], 16)
                if not last:
                    spread_halves(b + 1)
                sp.wait_ge(out_ready, b * T + T)
                settle(sp, sp_passed)
                sp.dma_start(row_step(x_out[bass.ds(b - B, 1)]), res[:, :, :]).then_inc(out_stored, 16)
                if not last:
                    load_x(b + 1)

            spread_halves(B)
            with sp.Fori(B, 2 * B - 1) as b:
                batch(b, False)
            batch(2 * B - 1, True)
            sp.wait_ge(out_stored, 16 * 2 * B)

        @block.gpsimd
        def _(pool):
            for dst, src in ((bv, spread(w["bv"])), (bo, spread(w["bo"])), (b1, cols(w["b1"])), (gates, spread(c["gate"])),
                             (g2, cols(w["gamma2"])), (be2, cols(w["beta2"])), (b2, spread(w["b2"]))):
                pool.dma_start(dst[:, :], src, allow_slow_non_contiguous=True).then_inc(small_loaded, 16)
            pool.memset(k_stack[4 * DH:4 * DH + 1, :, :].bitcast(F32), 1.0).then_inc(pool_set, 1)
            pool.wait_ge(pool_set, 1)
            pool.memset(v_one[:, :, :, :], 0.0).then_inc(pool_set, 1)
            pool.wait_ge(pool_set, 2)
            pool.memset(v_one[:, :, :, DH:DH + 1], 1.0).then_inc(pool_set, 1)

        @block.tensor
        def _(pe):
            def halves(m, k, lo, n):
                return tuple(x[:, k, lo:lo + n] for x in m)

            xt, ct = (xt_hi, xt_lo), (ct_hi, ct_lo)

            def flip_x(b):
                pe.wait_ge(xn_step, (b - B) * NORM_STEPS + NORM_STEPS)
                pe.wait_ge(scored, b * 64)
                flip(pe, (bank[0], bank[1]), xn, ident[:, :], x_flipped)

            def project_qk(b):
                pe.wait_ge(x_low, b * 2 + 2)
                for n, (m, out) in enumerate(((wq, F0), (wq, F1), (wk, F2), (wk, F3))):
                    for k in range(DK):
                        last = product(pe, out, halves(m, k, (n % 2) * P, P), halves(xt, k, 0, S), k == 0, k == DK - 1)
                    last.then_inc(projected, 1)

            def project_v(b):
                for t in range(T):
                    out = (o_bank, n_bank)[t // 2][:, (t % 2) * D:(t % 2 + 1) * D]
                    for k in range(DK):
                        last = product(pe, out, halves(xt, k, t * P, P), halves(wv, k, 0, D), k == 0, k == DK - 1)
                    if t % 2:
                        last.then_inc(v_projected, 1)

            def batch(b, last_batch):
                at = b - B

                def score(n):
                    if n == 0:
                        pe.wait_ge(first_stack, b * 128 + 128)
                        pe.wait_ge(gelu_done, b * FK)
                    if n == 16:
                        pe.wait_ge(rest_stack, b * 128 + 128)
                    if n >= 2:
                        pe.wait_ge(scored, b * 64 + n - 1)
                    h, t = divmod(n, T)
                    pe.matmul(bank[n % 2][:, 0:(t + 1) * P], q_stack[0:4 * DH, h, t * P:(t + 1) * P],
                              k_stack[0:4 * DH, h, 0:(t + 1) * P], start=True, stop=False)
                    pe.matmul(bank[n % 2][:, t * P:(t + 1) * P], ident_bf[:, :], causal_qk[:, :], start=False,
                              stop=True).then_inc(scores_ready, 1)

                def turn_max(g):
                    pe.wait_ge(scored, b * 64 + 16 * g + 16)
                    if g < 2:
                        pe.wait_ge(v_ready, b * 2 + 2)
                        pe.wait_ge(out_ready, b * T)
                        pe.wait_ge(row_made, at * 4 + g)
                    else:
                        pe.wait_ge(ctx_made, b * 4 + g - 1)
                    pe.transpose(n_bank[0:4 * T, 0:P], less_max[:, g % 2, :], ident[:, :]).then_inc(max_turned, 1)

                def score_keys(n):
                    if n % 16 == 0:
                        pe.wait_ge(row_loaded[n // 16 % 2], at * 32 + 16 * (n // 32 + 1))
                    if n == 0:
                        pe.wait_ge(part_lo, b * 4 + 4)
                        pe.wait_ge(out_ready, b * T)
                    if n >= 4:
                        pe.wait_ge(exped, at * 64 + n - 3)
                    h, kt = divmod(n, T)
                    pe.matmul(flips[:, kt, kt * P:S], k_stack[:, h, kt * P:(kt + 1) * P], q_stack[:, h, kt * P:S],
                              start=True, stop=False)
                    pe.matmul(flips[:, kt, kt * P:(kt + 1) * P], ident_bf[:, :], causal_kq[:, :], start=False,
                              stop=True).then_inc(shifted, 1)

                def weigh(g, kt):
                    if kt == 0:
                        pe.wait_ge(exped, at * 64 + 16 * g + 16)
                        pe.wait_ge(o_copied, b * 4 + g)
                    for j in range(4):
                        last = pe.matmul(o_bank[32 * j:32 * j + 32, kt * P:S], v_one[:, kt, 4 * g + j, :],
                                         probs[:, (4 * g + j) % SLOTS, kt, kt * P:S], start=kt == 0, stop=kt == T - 1,
                                         skip_group_check=True)
                    if kt == T - 1:
                        last.then_inc(weighed, 1)

                def turn_back(g):
                    pe.wait_ge(o_copied, b * 4 + g + 1)
                    pe.wait_ge(row_made, at * 4 + min(g + 2, 4))
                    pe.wait_ge(ctx_made, b * 4 + g)
                    for t in range(T):
                        last = pe.transpose(n_bank[:, t * P:(t + 1) * P], o_sb[:, t * P:(t + 1) * P], ident[:, :])
                    last.then_inc(o_turned, 1)

                for step in range(-AHEAD, T * H):
                    if step + AHEAD < T * H:
                        score(step + AHEAD)
                    if step in (-5, 11, 27, 43):
                        turn_max((step + 5) // 16)
                    if step >= 0:
                        score_keys(step)
                    group, part = divmod(step - 17, 16)
                    if group >= 0 and part < T:
                        weigh(group, part)
                    if group >= 0 and part == T + 1:
                        turn_back(group)
                if not last_batch:
                    flip_x(b + 1)
                for kt in range(T):
                    weigh(3, kt)
                turn_back(3)
                if not last_batch:
                    project_qk(b + 1)
                pe.wait_ge(ctx_made, b * 4 + 4)
                flip(pe, (bank[0], bank[1]), ctxt, ident[:, :], flipped)
                if not last_batch:
                    project_v(b + 1)
                    pe.wait_ge(part_lo, (b + 1) * 4 + 2)
                pe.wait_ge(c_low, b * 4 + 2)
                for t in range(T):
                    out = (F0, F1)[t // 2][:, (t % 2) * D:(t % 2 + 1) * D]
                    for k in range(DK):
                        last = product(pe, out, halves(ct, k, t * P, P), halves(wo, k, 0, D), k == 0, k == DK - 1)
                    if t % 2:
                        last.then_inc(attn_out, 1)
                pe.wait_ge(norm_step, b * NORM_STEPS + NORM_STEPS)
                flip(pe, (bank[0], bank[1]), ctxt, ident[:, :], flipped)
                pe.wait_ge(c_low, b * 4 + 4)
                if not last_batch:
                    pe.wait_ge(part_lo, (b + 1) * 4 + 4)
                    pe.wait_ge(v_ready, (b + 1) * 2 + 2)
                outs = (F2, F3, o_bank[:, :], n_bank[:, :])

                def down(m):
                    pe.wait_ge(ff_lo, b * FK + m + 1)
                    for t in range(T):
                        last = product(pe, outs[t][:, 0:D], halves((ring_hi, ring_lo), m % 4, t * P, P),
                                       halves(w2, m, 0, D), m == 0, m == FK - 1)
                    last.then_inc(down_done, 1)

                for m in range(FK):
                    if m >= 2:
                        pe.wait_ge(gelu_done, b * FK + m - 1)
                    for k in range(DK):
                        last = product(pe, bank[m % 2][:, :], halves(w1, k, m * P, P), halves(ct, k, 0, S), k == 0, k == DK - 1)
                    last.then_inc(up_done, 1)
                    if m >= 2:
                        down(m - 2)
                down(FK - 2)
                down(FK - 1)

            pe.wait_ge(early_loaded, 16 * 6)
            pe.transpose(n_bank[:, 0:P], causal[:, :], ident[:, :]).then_inc(max_turned, 1)
            pe.wait_ge(w_low, 1)
            flip_x(B)
            project_qk(B)
            pe.wait_ge(set_step, 4)
            project_v(B)
            pe.wait_ge(w_low, 3)
            with pe.Fori(B, 2 * B - 1) as b:
                batch(b, False)
            batch(2 * B - 1, True)

        @block.scalar
        def _(act):
            for dst, src in ((ident, c["ident"]), (causal, c["causal"]), (g1, cols(w["gamma1"])), (be1, cols(w["beta1"])),
                             (bq, cols(w["bq"])), (bk, cols(w["bk"]))):
                act.dma_start(dst[:, :], src, allow_slow_non_contiguous=True).then_inc(early_loaded, 16)

            def weight_high(n):
                act.activation(w_hi[:, n * 2048:(n + 1) * 2048], raw[:, 2 + n, :, :].rearrange("p t s -> p (t s)"),
                               ACT.Copy).then_inc(halves_made, 1)

            def affine(k, scale, add, made):
                act.activation(y[:, k, :], bank[k][:, :], ACT.Identity, bias=add[:, k:k + 1],
                               scale=scale[:, k:k + 1]).then_inc(made, 1)

            def x_affines(b):
                act.wait_ge(ff_lo, b * FK - FK)
                for k in range(DK):
                    act.wait_ge(x_flipped, b * 2 + k + 1)
                    affine(k, g1, be1, x_affine)

            def part_highs(b):
                for n, add in enumerate((bq[:, 0:1], bq[:, 1:2], bk[:, 0:1], bk[:, 1:2])):
                    act.wait_ge(projected, b * 4 + n + 1)
                    act.activation(ring_hi[:, n, :], flips[:, n, :], ACT.Identity, bias=add).then_inc(part_hi, 1)

            def batch(b, last):
                def copy_o(group):
                    act.wait_ge(weighed, b * 4 + group + 1)
                    act.wait_ge(o_turned, b * 4 + group)
                    act.activation(o_sb[:, :], o_bank[:, :], ACT.Copy).then_inc(o_copied, 1)

                for n in range(T * H):
                    h, kt = divmod(n, T)
                    if n % 16 == 4 and n > 16:
                        copy_o(n // 16 - 1)
                    act.wait_ge(shifted, (b - B) * 64 + n + 1)
                    act.activation(probs[:, h % SLOTS, kt, kt * P:S], flips[:, kt, kt * P:S], ACT.Exp).then_inc(exped, 1)
                if not last:
                    x_affines(b + 1)
                copy_o(3)
                if not last:
                    part_highs(b + 1)
                for k in range(DK):
                    act.wait_ge(flipped, b * 4 + k + 1)
                    act.activation(ct_hi[:, k, :], bank[k][:, :], ACT.Copy).then_inc(c_high, 1)
                for k in range(DK):
                    act.wait_ge(flipped, b * 4 + 3 + k)
                    if not last:
                        act.wait_ge(x_low, b * 2 + 3 + k)
                    affine(k, g2, be2, affine_made)
                for m in range(FK):
                    act.wait_ge(up_done, b * FK + m + 1)
                    if m < 2:
                        act.wait_ge(c_low, b * 4 + 3 + m)
                    else:
                        act.wait_ge(ff_lo, b * FK + m - 1)
                    act.activation(y[:, m % 2, :], bank[m % 2][:, :], ACT.Gelu, bias=b1[:, m:m + 1]).then_inc(gelu_done, 1)

            act.wait_ge(halves_made, 1)
            weight_high(0)
            act.wait_ge(early_loaded, 16 * 6)
            x_affines(B)
            act.wait_ge(set_step, 3)
            part_highs(B)
            act.wait_ge(mlp_loaded, 32)
            weight_high(1)
            weight_high(2)
            act.wait_ge(small_loaded, 16 * 7)
            with act.Fori(B, 2 * B - 1) as b:
                batch(b, False)
            batch(2 * B - 1, True)

        @block.vector
        def _(dve):
            def weight_low(n):
                dve.wait_ge(halves_made, 2 + n)
                dve.tensor_tensor(w_lo[:, n * 2048:(n + 1) * 2048], raw[:, 2 + n, :, :].rearrange("p t s -> p (t s)"),
                                  w_hi[:, n * 2048:(n + 1) * 2048].bitcast(F32), ALU.subtract).then_inc(w_low, 1)

            def norm_x(b, n):
                at = (b - B) * NORM_STEPS
                if n == 0:
                    dve.wait_ge(xn_loaded, (b - B) * 16 + 16)
                    for t in range(T):
                        norm_stats(dve, xn, stats, t, xn_step)
                if n == 1:
                    norm_root(dve, dve_passed, stats, mv, nt, 1e-5, xn_step, at)
                if n == 2:
                    dve.wait_ge(xn_step, at + NORM_ROOT)
                    for t in range(T):
                        dve.tensor_scalar(xn[:, t, :], xn[:, t, :], mv[:, t, 0:1], nt[:, 2, t:t + 1], ALU.subtract,
                                          ALU.mult).then_inc(xn_step, 1)

            def cut(k, to_hi, to_lo, high, at, low):
                dve.tensor_copy(to_hi[:, k, :], y[:, k, :]).then_inc(high, 1)
                dve.wait_ge(high, at + k + 1)
                dve.tensor_tensor(to_lo[:, k, :], y[:, k, :], to_hi[:, k, :].bitcast(F32), ALU.subtract).then_inc(low, 1)

            def cut_x(b):
                for k in range(DK):
                    dve.wait_ge(x_affine, (b - B) * 2 + k + 1)
                    cut(k, xt_hi, xt_lo, x_high, b * 2, x_low)

            def part_lows(b):
                for n, add in enumerate((bq[:, 0:1], bq[:, 1:2], bk[:, 0:1], bk[:, 1:2])):
                    dve.wait_ge(part_hi, b * 4 + n + 1)
                    dve.scalar_tensor_tensor(out=ring_lo[:, n, :], in0=flips[:, n, :], scalar=add,
                                             in1=ring_hi[:, n, :].bitcast(F32), op0=ALU.add, op1=ALU.subtract).then_inc(part_lo, 1)

            def take_v(b):
                for i, src in enumerate((o_bank, n_bank)):
                    dve.wait_ge(v_projected, b * 2 + i + 1)
                    dve.tensor_tensor(v_one[:, 2 * i:2 * i + 2, :, 0:DH], src[:, :].rearrange("p (t h d) -> p t h d", t=2, d=DH),
                                      over_rows(bv[:, :], 2).rearrange("p t (h d) -> p t h d", d=DH), ALU.add).then_inc(v_ready, 1)

            def batch(b, last):
                at = b - B

                def take_row(g):
                    dve.wait_ge(max_turned, at * 4 + g + 2)
                    if g >= 2:
                        dve.wait_ge(row_loaded[g % 2], at * 32 + 16)
                    dve.tensor_copy(max_row[:, g % 2, :], n_bank[0:4 * T, 0:P]).then_inc(row_made, 1)

                def normalise(g):
                    dve.wait_ge(o_turned, b * 4 + g + 1)
                    o = n_bank[:, :].rearrange("p (t h c) -> p t h c", t=T, h=4)
                    dve.reciprocal(one_over[:, :, :], o[:, :, :, DH]).then_inc(inverted, 1)
                    dve.wait_ge(inverted, b * 4 + g + 1)
                    dve.tensor_tensor(ctxt[:, :, g * 64:g * 64 + 64].rearrange("p t (h d) -> p t h d", d=DH),
                                      o[:, :, :, 0:DH], one_over[:, :, :].unsqueeze(3).to_broadcast([P, T, 4, DH]),
                                      ALU.mult).then_inc(ctx_made, 1)

                for n in range(T * H):
                    t, group = n % T, n // 16
                    dve.wait_ge(scores_ready, b * 64 + n + 1)
                    dve.tensor_reduce(less_max[:, group % 2, n % 16:n % 16 + 1], bank[n % 2][:, 0:(t + 1) * P], AX.X, ALU.max,
                                      negate=True).then_inc(scored, 1)
                    if n % 16 == AHEAD - 21 and group:
                        take_row(group - 1)
                    if n == 3:
                        dve.wait_ge(x_loaded, b * 16 + 16)
                        dve.wait_ge(out_stored, b * 16)
                        dve.tensor_tensor(res[:, :, :], x[:, :, :], over_rows(bo[:, :]), ALU.add).then_inc(res_begun, 1)
                    if not last and 32 <= n < 44 and t == 0:
                        norm_x(b + 1, (n - 32) // T)
                    if n % 16 == AHEAD - 10 and group >= 2:
                        normalise(group - 2)
                take_row(3)
                normalise(2)
                if not last:
                    cut_x(b + 1)
                normalise(3)
                if not last:
                    part_lows(b + 1)
                for k in range(DK):
                    dve.wait_ge(c_high, b * 2 + k + 1)
                    dve.tensor_tensor(ct_lo[:, k, :], bank[k][:, :], ct_hi[:, k, :].bitcast(F32), ALU.subtract).then_inc(c_low, 1)
                if not last:
                    take_v(b + 1)
                dve.wait_ge(res_begun, b + 1)
                for i in range(2):
                    dve.wait_ge(attn_out, b * 2 + i + 1)
                    dve.tensor_tensor(res[:, 2 * i:2 * i + 2, :], flips[:, i, :].rearrange("p (t d) -> p t d", d=D),
                                      res[:, 2 * i:2 * i + 2, :], ALU.add).then_inc(first_res, 1)
                dve.wait_ge(first_res, b * 2 + 2)
                layer_norm(dve, dve_passed, res, ctxt, stats, mv, nt, 1e-5, norm_step, b * NORM_STEPS)
                for k in range(DK):
                    dve.wait_ge(affine_made, b * 2 + k + 1)
                    cut(k, ct_hi, ct_lo, ff_hi, b * (DK + FK), c_low)
                dve.wait_ge(norm_step, b * NORM_STEPS + NORM_STEPS)
                dve.tensor_tensor(res[:, :, :], res[:, :, :], over_rows(b2[:, :]), ALU.add).then_inc(delta_step, 1)
                dve.wait_ge(delta_step, at * 2 + 1)
                dve.tensor_tensor(res[:, :, :], res[:, :, :], x[:, :, :], ALU.subtract).then_inc(delta_step, 1)
                dve.tensor_copy(gate[:, :], gates[:, bass.ds(b - B, 1)]).then_inc(mixed, 1)
                if not last:
                    dve.wait_ge(halves_stored, (b + 1) * 64 + 64)
                for m in range(FK):
                    dve.wait_ge(gelu_done, b * FK + m + 1)
                    if m >= 4:
                        dve.wait_ge(down_done, b * FK + m - 3)
                    dve.tensor_copy(ring_hi[:, m % 4, :], y[:, m % 2, :]).then_inc(ff_hi, 1)
                    dve.wait_ge(ff_hi, b * (DK + FK) + DK + m + 1)
                    dve.tensor_tensor(ring_lo[:, m % 4, :], y[:, m % 2, :], ring_hi[:, m % 4, :].bitcast(F32),
                                      ALU.subtract).then_inc(ff_lo, 1)
                dve.wait_ge(down_done, b * FK + FK)
                dve.wait_ge(delta_step, at * 2 + 2)
                for t, src in enumerate((F2, F3, o_bank[:, :], n_bank[:, :])):
                    dve.tensor_tensor(res[:, t, :], src[:, 0:D], res[:, t, :], ALU.add).then_inc(mixed, 1)
                for t in range(T):
                    dve.wait_ge(mixed, at * 5 + 2 + t)
                    dve.scalar_tensor_tensor(out=res[:, t, :], in0=res[:, t, :], scalar=gate[:, :], in1=x[:, t, :],
                                             op0=ALU.mult, op1=ALU.add).then_inc(out_ready, 1)

            norm_x(B, 0)
            norm_x(B, 1)
            dve.wait_ge(weights_loaded, 64)
            dve.tensor_scalar(raw[:, 2, 0, :], raw[:, 2, 0, :], SC, None, ALU.mult).then_inc(halves_made, 1)
            norm_x(B, 2)
            dve.wait_ge(early_loaded, 16 * 6)
            dve.tensor_scalar(bq[:, :], bq[:, :], SC, None, ALU.mult).then_inc(set_step, 1)
            dve.tensor_copy(ident_bf[:, :], ident[:, :]).then_inc(set_step, 1)
            dve.tensor_copy(causal_qk[:, :], causal[:, :]).then_inc(set_step, 1)
            dve.wait_ge(max_turned, 1)
            dve.tensor_copy(causal_kq[:, :], n_bank[:, 0:P]).then_inc(set_step, 1)
            weight_low(0)
            cut_x(B)
            part_lows(B)
            dve.wait_ge(pool_set, 3)
            dve.wait_ge(small_loaded, 16 * 7)
            take_v(B)
            weight_low(1)
            weight_low(2)
            with dve.Fori(B, 2 * B - 1) as b:
                batch(b, False)
            batch(2 * B - 1, True)


COMMON = {"mask": "mask_Bx1xSxS_bk0", "bias": "fside_Bx16xSxS_0", "timestep": "itok_B_34_63", "expert": "itok_B_0_15",
          "mlp_expert": "itok_B_0_7", "gate": "condB_gatescore"}


def layers_program(nc, args, out):
    def layer_weights(n):
        prefix = f"L{n}_cond_"
        return {name[len(prefix):]: ap for name, ap in args.items() if name.startswith(prefix)}

    def internal(name, shape):
        return nc.dram_tensor(name, shape, F32, kind="Internal").ap()

    between = [internal(f"between{n}", [B, S, D]) for n in range(3)]
    scratch = {"halves": internal("halves", [4, D, S]), "ada": internal("ada_rows", [B, 2 * D])}
    sems = {}
    sems = {}
    sems = {}
    sems = {}
    sems = {}
    adapter_layer(nc, args["x"], between[0], layer_weights(0), args)
    biased_attention_layer(nc, between[0], between[1], layer_weights(1), args, scratch, sems)
    expert_mlp_layer(nc, between[1], between[2], layer_weights(2), args)
    causal_attention_layer(nc, between[2], out, layer_weights(3), args, scratch, sems)


def kernel(**inputs):
    import concourse.bacc as bacc
    from concourse.bass_utils import run_bass_kernel_spmd

    nc = bacc.Bacc("TRN2", target_bir_lowering=False, num_devices=1)
    given = {name: np.ascontiguousarray(a) for name, a in inputs.items()}
    data = {name: a for name, a in given.items() if name == "x" or name.startswith("L")}
    data.update({name: given[full] for name, full in COMMON.items()})
    data["mask"] = data["mask"].reshape(B, S, S)
    data["bias"] = data["bias"].reshape(B * H, S, S)
    data["ident"] = np.eye(P, dtype=np.float32)
    data["freq"] = np.exp(np.arange(P, dtype=np.float32) * np.float32(-math.log(10000.0) / (P - 1))).reshape(P, 1)
    data["causal"] = np.where(np.arange(P)[:, None] >= np.arange(P)[None, :], 0, MASKED).astype(np.float32)
    arrays, args = {}, {}
    for name, a in data.items():
        arrays[f"in_{name}_dram"] = a
        args[name] = nc.dram_tensor(f"in_{name}_dram", a.shape, mybir.dt.from_np(a.dtype), kind="ExternalInput").ap()
    out = nc.dram_tensor("out_0_dram", (B, S, D), F32, kind="ExternalOutput").ap()
    layers_program(nc, args, out)
    r = run_bass_kernel_spmd(nc, [arrays], core_ids=[0])
    return r.results[0]["out_0_dram"]
```

```python
import math
from contextlib import ExitStack

import numpy as np

import concourse.bass as bass
from concourse import mybir

F32 = mybir.dt.float32
F32R = mybir.dt.float32r
BF16 = mybir.dt.bfloat16
I32 = mybir.dt.int32
U8 = mybir.dt.uint8
ALU = mybir.AluOpType
ACT = mybir.ActivationFunctionType
AX = mybir.AxisListType

P = 128
B, S, D = 4, 512, 256
T = S // P
DK = D // P
H = 16
DH = D // H
F = 1024
FK = F // P
A = 64
SC = 1.0 / math.sqrt(DH)
MASKED = -1.0e30
ROUND = 1.5 * 2.0 ** 23
TURN = (6.28125, 0.0019354820251464844, 2 * math.pi - 6.28125 - 0.0019354820251464844)
PI_BELOW = 3.1415925
SIN_READY = 12
NORM_ROOT = 20
NORM_STEPS = NORM_ROOT + T


SLOTS = 5
LAG = 5
AHEAD = 20
X_STEPS = NORM_ROOT + 2 * T


def settle(eng, passed):
    eng.sem_inc(passed, 1)


def norm_stats(dve, src, stats, t, norm_step):
    dve.bn_stats(stats[:, t, :], src[:, t, :]).then_inc(norm_step, 1)


def norm_guess(dve, passed, stats, mv, tmp, eps, norm_step, base):
    dve.wait_ge(norm_step, base + 4)
    settle(dve, passed)
    for t in range(T):
        dve.bn_aggr(mv[:, t, :], stats[:, t, :]).then_inc(norm_step, 1)
    var, bits, y = tmp[:, 0, :], tmp[:, 1, :], tmp[:, 2, :]
    dve.wait_ge(norm_step, base + 8)
    dve.tensor_scalar(var, mv[:, :, 1], eps, None, ALU.add).then_inc(norm_step, 1)
    dve.wait_ge(norm_step, base + 9)
    dve.tensor_scalar(bits.bitcast(I32), var.bitcast(I32), 1, None,
                      ALU.logical_shift_right).then_inc(norm_step, 1)
    dve.wait_ge(norm_step, base + 10)
    dve.tensor_scalar(y.bitcast(I32), bits.bitcast(I32), -1.0, float(0x5F3759DF), ALU.mult,
                      ALU.add).then_inc(norm_step, 1)


def norm_newton(dve, n, tmp, norm_step, base):
    var, y, q = tmp[:, 0, :], tmp[:, 2, :], tmp[:, 3, :]
    dve.wait_ge(norm_step, base + 11 + 3 * n)
    dve.tensor_tensor(q, y, y, ALU.mult).then_inc(norm_step, 1)
    dve.wait_ge(norm_step, base + 12 + 3 * n)
    dve.scalar_tensor_tensor(out=q, in0=q, scalar=-0.5, in1=var, op0=ALU.mult,
                             op1=ALU.mult).then_inc(norm_step, 1)
    dve.wait_ge(norm_step, base + 13 + 3 * n)
    dve.scalar_tensor_tensor(out=y, in0=q, scalar=1.5, in1=y, op0=ALU.add,
                             op1=ALU.mult).then_inc(norm_step, 1)


def norm_root(dve, passed, stats, mv, tmp, eps, norm_step, base):
    norm_guess(dve, passed, stats, mv, tmp, eps, norm_step, base)
    for n in range(3):
        norm_newton(dve, n, tmp, norm_step, base)


def layer_norm(dve, passed, src, dst, stats, mv, tmp, eps, norm_step, base):
    for t in range(T):
        norm_stats(dve, src, stats, t, norm_step)
    norm_root(dve, passed, stats, mv, tmp, eps, norm_step, base)
    dve.wait_ge(norm_step, base + NORM_ROOT)
    for t in range(T):
        dve.tensor_scalar(dst[:, t, :], src[:, t, :], mv[:, t, 0:1], tmp[:, 2, t:t + 1], ALU.subtract,
                          ALU.mult).then_inc(norm_step, 1)


def product(pe, out, a, b, first, last):
    pe.matmul(out, a[0], b[0], start=first, stop=False)
    pe.matmul(out, a[0], b[1], start=False, stop=False)
    return pe.matmul(out, a[1], b[0], start=False, stop=last)


def flip(pe, banks, src, ident, flipped):
    for dk in range(DK):
        for t in range(T):
            last = pe.transpose(banks[dk][:, t * P:(t + 1) * P], src[:, t, dk * P:(dk + 1) * P], ident)
        last.then_inc(flipped, 1)


def over_rows(ap, n=T):
    return ap.unsqueeze(1).to_broadcast([P, n, D])


class CutWeights:

    def __init__(self, nc, ctx, w, prefix):
        self.w, self.prefix = w, prefix
        self.hi = ctx.enter_context(nc.sbuf_tensor(prefix + "w_hi", [P, 3, 2048], F32R))
        self.lo = ctx.enter_context(nc.sbuf_tensor(prefix + "w_lo", [P, 3, 2048], F32R))
        self.loaded, self.scaled, self.high, self.low = (
            nc.alloc_semaphore(prefix + n) for n in ("w_loaded", "w_scaled", "w_high", "w_low"))

    def raw_place(self, nc, ctx):
        return ctx.enter_context(nc.sbuf_tensor(self.prefix + "w_raw", [P, 3, 2048], F32))

    def cut(self, pool, raw):
        for i, name in enumerate(("Wq", "Wk", "Wv", "Wo")):
            pool.dma_start(raw[:, 0, i * 512:(i + 1) * 512].rearrange("p (k n) -> p k n", k=DK),
                           self.w[name].rearrange("(k p) n -> p k n", p=P)).then_inc(self.loaded, 16)
        for i, (name, k) in enumerate((("W1", DK), ("W2", FK))):
            pool.dma_start(raw[:, 1 + i, :].rearrange("p (k n) -> p k n", k=k),
                           self.w[name].rearrange("(k p) n -> p k n", p=P)).then_inc(self.loaded, 16)
        pool.wait_ge(self.loaded, 96)
        pool.tensor_scalar(raw[:, 0, 0:512], raw[:, 0, 0:512], SC, None, ALU.mult).then_inc(self.scaled, 1)
        pool.wait_ge(self.scaled, 1)
        for n in range(3):
            pool.tensor_copy(self.hi[:, n, :], raw[:, n, :]).then_inc(self.high, 1)
            pool.wait_ge(self.high, n + 1)
            pool.tensor_tensor(self.lo[:, n, :], raw[:, n, :], self.hi[:, n, :].bitcast(F32), ALU.subtract).then_inc(self.low, 1)
        pool.wait_ge(self.low, 3)

    def halves(self):
        def of(n, lo, hi, k):
            return tuple(x[:, n, lo:hi].rearrange("p (k n) -> p k n", k=k) for x in (self.hi, self.lo))

        return (*(of(0, 512 * i, 512 * i + 512, DK) for i in range(4)), of(1, 0, 2048, DK), of(2, 0, 2048, FK))


class AdaptiveRows:

    def __init__(self, nc, ctx, w, c, dram):
        def sb(name, shape, dt=F32):
            return ctx.enter_context(nc.sbuf_tensor("adapt_" + name, shape, dt))

        self.w, self.c, self.dram = w, c, dram
        self.tstep, self.freq, self.emb = sb("tstep", [P, B], I32), sb("freq", [P, 1]), sb("emb", [P, 8, B])
        self.w_ada, self.bias, self.rows = sb("w", [P, DK, 2 * D]), sb("bias", [B, 2 * D]), sb("rows", [B, 2 * D])
        self.bank = ctx.enter_context(nc.psum_tensor("adapt_bank", [P, 512], F32))
        self.steps_loaded, self.w_loaded, self.angle_step, self.sin_done, self.made, self.stored = (
            nc.alloc_semaphore("adapt_" + n) for n in ("steps_loaded", "w_loaded", "angle_step", "sin_done", "made", "stored"))

    def load(self, act):
        spread = lambda a, n: a.rearrange("(o n) -> o n", o=1).to_broadcast([n, a.shape[0]])
        for dst, src in ((self.freq, self.c["freq"]), (self.tstep, spread(self.c["timestep"], P))):
            act.dma_start(dst[:, :], src).then_inc(self.steps_loaded, 16)
        act.dma_start(self.w_ada[:, :, :], self.w["W_ada"].rearrange("(k p) n -> p k n", p=P)).then_inc(self.w_loaded, 16)
        act.dma_start(self.bias[:, :], spread(self.w["b_ada"], B)).then_inc(self.w_loaded, 16)

    def angles(self, dve):
        step = [0]

        def link(ins):
            step[0] += 1
            ins.then_inc(self.angle_step, 1)
            dve.wait_ge(self.angle_step, step[0])

        emb = self.emb
        angle, turns, r, cosr = emb[:, 0, :], emb[:, 1, :], emb[:, 2, :], emb[:, 3, :]
        dve.wait_ge(self.steps_loaded, 32)
        link(dve.tensor_copy(r, self.tstep[:, :]))
        link(dve.tensor_scalar(angle, r, 40.0, self.freq[:, 0:1], ALU.mult, ALU.mult))
        link(dve.tensor_scalar(turns, angle, 1.0 / (2 * math.pi), ROUND, ALU.mult, ALU.add))
        link(dve.tensor_scalar(turns, turns, -ROUND, None, ALU.add))
        link(dve.tensor_copy(r, angle))
        for part in TURN:
            link(dve.scalar_tensor_tensor(out=r, in0=turns, scalar=-part, in1=r, op0=ALU.mult, op1=ALU.add))
        link(dve.tensor_scalar(cosr, r, math.pi / 2, None, ALU.add))
        link(dve.tensor_scalar(angle, cosr, math.pi, -2 * math.pi, ALU.is_gt, ALU.mult))
        link(dve.tensor_tensor(cosr, cosr, angle, ALU.add))
        link(dve.tensor_scalar(emb[:, 2:4, :], emb[:, 2:4, :], PI_BELOW, -PI_BELOW, ALU.min, ALU.max))
        assert step[0] == SIN_READY

    def sinusoids(self, act):
        act.wait_ge(self.angle_step, SIN_READY)
        act.activation(self.emb[:, 4:6, :], self.emb[:, 2:4, :], ACT.Sin).then_inc(self.sin_done, 1)
        act.wait_ge(self.sin_done, 1)
        act.activation(self.emb[:, 6:8, :], self.emb[:, 4:6, :], ACT.Silu).then_inc(self.sin_done, 1)

    def multiply(self, pe):
        pe.wait_ge(self.sin_done, 2)
        pe.wait_ge(self.w_loaded, 32)
        for k in range(DK):
            last = pe.matmul(self.bank[0:B, :], self.emb[:, 6 + k, :], self.w_ada[:, k, :], start=k == 0, stop=k == DK - 1)
        last.then_inc(self.made, 1)

    def shift(self, dve):
        dve.wait_ge(self.made, 1)
        dve.tensor_tensor(self.rows[:, :], self.bank[0:B, :], self.bias[:, :], ALU.add).then_inc(self.made, 1)
        dve.wait_ge(self.made, 2)
        dve.tensor_scalar(self.rows[:, 0:D], self.rows[:, 0:D], 1.0, None, ALU.add).then_inc(self.made, 1)

    def store(self, sp):
        sp.wait_ge(self.made, 3)
        sp.dma_start(self.dram, self.rows[:, :]).then_inc(self.stored, 16)
        sp.wait_ge(self.stored, 16)


def adapter_layer(nc, x_in, x_out, w, c, following, adaptive):
    with ExitStack() as ctx:
        def sb(name, shape, dt=F32):
            return ctx.enter_context(nc.sbuf_tensor("a_" + name, shape, dt))

        def sem(name):
            return nc.alloc_semaphore("a_" + name)

        bank = [ctx.enter_context(nc.psum_tensor(f"a_bank{i}", [P, 512], F32)) for i in range(4)]
        flips = ctx.enter_context(nc.psum_tensor("a_flips", [P, DK, 512], F32))
        ident = sb("ident", [P, P])
        down_raw, up_raw = sb("down_raw", [A, D]), sb("up_raw", [P, DK, A])
        down_t, up_t = sb("down_t", [P, DK, A]), sb("up_t", [A, D])
        down_b, up_b = sb("down_b", [A, 1]), sb("up_b", [P, D])
        gamma, beta = sb("gamma", [P, D]), sb("beta", [P, D])
        ids, id_row = sb("ids", [A, B], I32), sb("id_row", [1, B], I32)
        idf, valid, invalid, past = sb("idf", [A, B]), sb("valid", [A, B]), sb("invalid", [A, B]), sb("past", [A, B])
        x, xb, y = sb("x", [P, T, D]), sb("xb", [P, T, D]), sb("y", [P, T, D])
        xt = sb("xt", [P, DK, S])
        e_raw, e_b, e_emb = sb("e_raw", [A, A]), sb("e_b", [A, 1]), sb("e_emb", [A, 1])
        keep, e_t, add = sb("keep", [A, A]), sb("e_t", [A, A]), sb("add", [A, 1])
        hid, hid2 = sb("hid", [A, S]), sb("hid2", [A, S])
        stats, mv, nt = sb("stats", [P, T, 6]), sb("mv", [P, T, 2]), sb("nt", [P, 4, T])
        raw_next = following.raw_place(nc, ctx)
        rows = adaptive(nc, ctx)

        dve_passed, pe_passed, sp_passed = sem("dve_passed"), sem("pe_passed"), sem("sp_passed")
        ids_loaded, ident_loaded, small_loaded, set_flipped, set_step = (
            sem(n) for n in ("ids_loaded", "ident_loaded", "small_loaded", "set_flipped", "set_step"))
        x_loaded, expert_loaded, rows_loaded = sem("x_loaded"), sem("expert_loaded"), sem("rows_loaded")
        flipped, turned, expert_turned, kept, added, expert_made = (
            sem(n) for n in ("flipped", "turned", "expert_turned", "kept", "added", "expert_made"))
        down_done, hid_made, expert_done, hid2_made, up_done = (
            sem(n) for n in ("down_done", "hid_made", "expert_done", "hid2_made", "up_done"))
        xb_made, summed, norm_step, scaled, y_made, y_stored = (
            sem(n) for n in ("xb_made", "summed", "norm_step", "scaled", "y_made", "y_stored"))
        block = ctx.enter_context(nc.Block())

        @block.sync
        def _(sp):
            spread = lambda a, n: a.rearrange("(o n) -> o n", o=1).to_broadcast([n, a.shape[0]])
            col = lambda a: a.rearrange("(p o) -> p o", o=1)
            n_experts = w["expert_W"].shape[0]
            row = sp.alloc_register("a_expert")

            def load_x(b):
                sp.dma_start(x[:, :, :], x_in[bass.ds(b, 1)].rearrange("b (t p) d -> p (b t) d", p=P)).then_inc(x_loaded, 16)

            def load_expert(b):
                sp.reg_alu(row, sp.value_load(id_row[0:1, bass.ds(b, 1)]), 0, ALU.max)
                sp.reg_alu(row, row, n_experts - 1, ALU.min)
                e = sp.snap(row, min_val=0, max_val=n_experts - 1)
                sp.dma_start(e_raw[:, :], w["expert_W"][bass.ds(e, 1)].rearrange("e o a -> o (e a)")).then_inc(expert_loaded, 16)
                sp.dma_start(e_b[:, :], w["expert_b"][bass.ds(e, 1)].rearrange("e a -> a e"),
                             allow_slow_non_contiguous=True).then_inc(expert_loaded, 16)
                sp.dma_start(e_emb[:, :], w["domain_emb"][bass.ds(e, 1)].rearrange("e a -> a e"),
                             allow_slow_non_contiguous=True).then_inc(expert_loaded, 16)

            sp.dma_start(id_row[:, :], spread(c["expert"], 1)).then_inc(ids_loaded, 16)
            sp.dma_start(ident[:, :], c["ident"]).then_inc(ident_loaded, 16)
            load_x(0)
            for dst, src in ((down_raw[:, :], w["down_W"]), (up_raw[:, :, :], w["up_W"].rearrange("(k p) a -> p k a", p=P)),
                             (down_b[:, :], col(w["down_b"])), (ids[:, :], spread(c["expert"], A))):
                sp.dma_start(dst, src).then_inc(small_loaded, 16)
            sp.wait_ge(ids_loaded, 16)
            load_expert(0)
            for dst, src in ((up_b, w["up_b"]), (gamma, w["ln_gamma"]), (beta, w["ln_beta"])):
                sp.dma_start(dst[:, :], spread(src, P)).then_inc(rows_loaded, 16)

            def store_y(b):
                sp.wait_ge(y_made, b + 1)
                settle(sp, sp_passed)
                sp.dma_start(x_out[bass.ds(b, 1)].rearrange("b (t p) d -> p (b t) d", p=P), y[:, :, :]).then_inc(y_stored, 16)

            def load_next(b):
                sp.wait_ge(expert_made, b + 1)
                settle(sp, sp_passed)
                load_expert(b + 1)
                sp.wait_ge(xb_made, b + 1)
                sp.wait_ge(flipped, b * 2 + 2)
                settle(sp, sp_passed)
                load_x(b + 1)

            load_next(0)
            with sp.Fori(1, B - 1) as b:
                store_y(b - 1)
                load_next(b)
            rows.store(sp)
            store_y(B - 2)
            store_y(B - 1)
            sp.wait_ge(y_stored, 16 * B)

        @block.gpsimd
        def _(pool):
            following.cut(pool, raw_next)

        @block.tensor
        def _(pe):
            def flip_x(b):
                pe.wait_ge(x_loaded, b * 16 + 16)
                pe.wait_ge(turned, b)
                flip(pe, (flips[:, 0, :], flips[:, 1, :]), x, ident[:, :], flipped)

            def batch(b, last_batch):
                pe.wait_ge(expert_loaded, b * 48 + 48)
                pe.wait_ge(hid2_made, b)
                settle(pe, pe_passed)
                pe.transpose(bank[1][0:A, 0:A], e_raw[:, :], ident[0:A, 0:A]).then_inc(expert_turned, 1)
                pe.wait_ge(turned, b + 1)
                for k in range(DK):
                    last = pe.matmul(bank[0][0:A, :], down_t[:, k, :], xt[:, k, :], start=k == 0, stop=k == DK - 1)
                last.then_inc(down_done, 1)
                pe.wait_ge(hid_made, b + 1)
                pe.wait_ge(expert_made, b + 1)
                settle(pe, pe_passed)
                pe.matmul(bank[1][0:A, :], e_t[:, :], hid[:, :], start=True, stop=True).then_inc(expert_done, 1)
                pe.wait_ge(hid2_made, b + 1)
                pe.wait_ge(summed, b * 2)
                for t in range(T):
                    last = pe.matmul(bank[2 + t // 2][:, (t % 2) * D:(t % 2 + 1) * D], hid2[:, t * P:(t + 1) * P], up_t[:, :],
                                     start=True, stop=True)
                    if t % 2:
                        last.then_inc(up_done, 1)
                if not last_batch:
                    flip_x(b + 1)

            pe.wait_ge(ident_loaded, 16)
            flip_x(0)
            pe.wait_ge(small_loaded, 64)
            for k in range(DK):
                pe.transpose(bank[0][:, k * A:(k + 1) * A], down_raw[:, k * P:(k + 1) * P], ident[0:A, 0:A])
            for k in range(DK):
                last = pe.transpose(bank[1][0:A, k * P:(k + 1) * P], up_raw[:, k, :], ident[:, :])
            last.then_inc(set_flipped, 1)
            pe.wait_ge(set_step, 2)
            batch(0, False)
            rows.multiply(pe)
            with pe.Fori(1, B - 1) as b:
                batch(b, False)
            batch(B - 1, True)

        @block.scalar
        def _(act):
            rows.load(act)
            rows.sinusoids(act)
            with act.Fori(0, B) as b:
                act.wait_ge(flipped, b * 2 + 2)
                act.wait_ge(down_done, b)
                act.activation(xt[:, :, :], flips[:, :, :], ACT.Copy).then_inc(turned, 1)
                act.wait_ge(down_done, b + 1)
                act.wait_ge(small_loaded, 64)
                act.activation(hid[:, :], bank[0][0:A, :], ACT.Gelu, bias=down_b[:, :]).then_inc(hid_made, 1)
                act.wait_ge(expert_done, b + 1)
                act.wait_ge(up_done, b * 2)
                act.activation(hid2[:, :], bank[1][0:A, :], ACT.Identity, bias=add[:, :]).then_inc(hid2_made, 1)

        @block.vector
        def _(dve):
            rows.angles(dve)
            dve.wait_ge(small_loaded, 64)
            dve.wait_ge(set_flipped, 1)
            dve.tensor_copy(down_t[:, :, :], bank[0][:, 0:DK * A].rearrange("p (k a) -> p k a", k=DK)).then_inc(set_step, 1)
            dve.tensor_copy(up_t[:, :], bank[1][0:A, 0:D]).then_inc(set_step, 1)
            n_experts = float(w["expert_W"].shape[0])
            dve.tensor_copy(idf[:, :], ids[:, :]).then_inc(set_step, 1)
            dve.wait_ge(set_step, 3)
            dve.tensor_scalar(past[:, :], idf[:, :], n_experts, None, ALU.is_lt).then_inc(set_step, 1)
            dve.wait_ge(set_step, 4)
            dve.scalar_tensor_tensor(out=valid[:, :], in0=idf[:, :], scalar=0.0, in1=past[:, :], op0=ALU.is_ge,
                                     op1=ALU.mult).then_inc(set_step, 1)
            dve.wait_ge(set_step, 5)
            dve.tensor_scalar(invalid[:, :], valid[:, :], -1.0, 1.0, ALU.mult, ALU.add).then_inc(set_step, 1)
            dve.wait_ge(set_step, 6)

            def finish(b):
                base = b * NORM_STEPS
                norm_root(dve, dve_passed, stats, mv, nt, 1e-5, norm_step, base)
                dve.wait_ge(norm_step, base + NORM_ROOT)
                dve.wait_ge(y_stored, b * 16)
                for t in range(T):
                    dve.tensor_scalar(y[:, t, :], xb[:, t, :], mv[:, t, 0:1], nt[:, 2, t:t + 1], ALU.subtract,
                                      ALU.mult).then_inc(norm_step, 1)
                dve.wait_ge(norm_step, base + NORM_STEPS)
                dve.tensor_tensor(y[:, :, :], y[:, :, :], over_rows(gamma[:, :]), ALU.mult).then_inc(scaled, 1)
                dve.wait_ge(scaled, b + 1)
                dve.tensor_tensor(y[:, :, :], y[:, :, :], over_rows(beta[:, :]), ALU.add).then_inc(y_made, 1)

            def batch(b, first):
                dve.wait_ge(expert_loaded, b * 48 + 48)
                dve.wait_ge(expert_done, b)
                dve.tensor_scalar(keep[:, :], ident[0:A, 0:A], invalid[:, bass.ds(b, 1)], None, ALU.mult).then_inc(kept, 1)
                dve.wait_ge(hid2_made, b)
                dve.scalar_tensor_tensor(out=add[:, :], in0=e_b[:, :], scalar=valid[:, bass.ds(b, 1)],
                                         in1=e_emb[:, :], op0=ALU.mult, op1=ALU.add).then_inc(added, 1)
                dve.wait_ge(added, b + 1)
                dve.wait_ge(kept, b + 1)
                dve.wait_ge(expert_turned, b + 1)
                dve.scalar_tensor_tensor(out=e_t[:, :], in0=bank[1][0:A, 0:A], scalar=valid[:, bass.ds(b, 1)],
                                         in1=keep[:, :], op0=ALU.mult, op1=ALU.add).then_inc(expert_made, 1)
                if not first:
                    finish(b - 1)
                else:
                    dve.wait_ge(rows_loaded, 48)
                dve.wait_ge(x_loaded, b * 16 + 16)
                dve.tensor_tensor(xb[:, :, :], x[:, :, :], over_rows(up_b[:, :]), ALU.add).then_inc(xb_made, 1)
                dve.wait_ge(xb_made, b + 1)
                for i in range(2):
                    dve.wait_ge(up_done, b * 2 + i + 1)
                    dve.tensor_tensor(xb[:, 2 * i:2 * i + 2, :], bank[2 + i][:, :].rearrange("p (t d) -> p t d", d=D),
                                      xb[:, 2 * i:2 * i + 2, :], ALU.add).then_inc(summed, 1)
                dve.wait_ge(summed, b * 2 + 2)
                for t in range(T):
                    norm_stats(dve, xb, stats, t, norm_step)

            batch(0, True)
            rows.shift(dve)
            with dve.Fori(1, B) as b:
                batch(b, False)
            finish(B - 1)


def biased_attention_layer(nc, x_in, x_out, w, c, scratch, sems, weights):
    qk_dram, ada_dram = scratch["halves"], scratch["ada"]
    with ExitStack() as ctx:
        def sb(name, shape, dt=F32):
            return ctx.enter_context(nc.sbuf_tensor("b_" + name, shape, dt))

        def sem(name):
            sems[name] = nc.alloc_semaphore("b_" + name)
            return sems[name]

        bank = [ctx.enter_context(nc.psum_tensor(f"b_bank{i}", [P, 512], F32)) for i in range(2)]
        flips = ctx.enter_context(nc.psum_tensor("b_flips", [P, 4, 512], F32))
        o_bank = ctx.enter_context(nc.psum_tensor("b_obank", [P, 512], F32))
        n_bank = ctx.enter_context(nc.psum_tensor("b_nbank", [P, 512], F32))
        F0, F1, F2, F3 = (flips[:, i, :] for i in range(4))

        wq, wk, wv, wo, w1, w2 = weights.halves()
        ident, ident_bf = sb("ident", [P, P]), sb("ident_bf", [P, P], BF16)
        bq, bk = sb("bq", [P, DK]), sb("bk", [P, DK])
        b1, g2, be2 = sb("b1", [P, FK]), sb("g2", [P, DK]), sb("be2", [P, DK])
        bv, bo, b2 = sb("bv", [P, D]), sb("bo", [P, D]), sb("b2", [P, D])
        x = sb("x", [P, T, D])
        res = sb("res", [P, T, D])
        ctxt = sb("ctxt", [P, T, D])
        xt_hi, xt_lo = sb("xt_hi", [P, DK, S], F32R), sb("xt_lo", [P, DK, S], F32R)
        ct_hi, ct_lo = sb("ct_hi", [P, DK, S], F32R), sb("ct_lo", [P, DK, S], F32R)
        y = sb("y", [P, 2, S])
        v_one = sb("v_one", [P, T, H, 32])
        q_stack, k_stack = sb("q_stack", [P, 4, S], F32R), sb("k_stack", [P, 4, S], F32R)
        mask_u8, mask_add = sb("mask_u8", [P, T, S], U8), sb("mask_add", [P, T, S], BF16)
        bias = sb("bias", [P, 4, T, S])
        shared_at = nc.sbuf_base
        scores = sb("scores", [P, 2, T, S])
        ring = nc.alloc_sbuf_tensor_at("b_ring", [P, 2, 4, S], F32R, offset=shared_at)
        ring_hi, ring_lo = ring[:, 0, :, :], ring[:, 1, :, :]
        less_max = sb("less_max", [P, 2, T])
        probs = sb("probs", [P, SLOTS, T, S])
        o_sb = sb("o_sb", [P, S])
        one_over = sb("one_over", [P, T, 4])
        ada = sb("ada", [P, 2, D])
        stats, mv, nt = sb("stats", [P, T, 6]), sb("mv", [P, T, 2]), sb("nt", [P, 4, T])

        pool_passed, dve_passed = sem("pool_passed"), sem("dve_passed")
        small_loaded, ident_loaded = sem("small_loaded"), sem("ident_loaded")
        sp_passed = sem("sp_passed")
        ident_cast, zeros_set, attn_set = sem("ident_cast"), sem("zeros_set"), sem("attn_set")
        x_loaded, mask_loaded, ada_loaded = sem("x_loaded"), sem("mask_loaded"), sem("ada_loaded")
        bias_loaded = [sem(f"bias_loaded{i}") for i in range(4)]
        x_step, norm_step, res_begun, res_step, mask_made = (
            sem(n) for n in ("x_step", "norm_step", "res_begun", "res_step", "mask_made"))
        x_flipped, x_high, x_low, projected, part_hi, part_lo, v_projected, v_ready = (
            sem(n) for n in ("x_flipped", "x_high", "x_low", "projected", "part_hi", "part_lo", "v_projected", "v_ready"))
        halves_stored, stack_loaded = sem("halves_stored"), [sem(f"stack_loaded{i}") for i in range(4)]
        scores_ready, scored, shifted_outer, shifted_inner = (
            sem(n) for n in ("scores_ready", "scored", "shifted_outer", "shifted_inner"))
        turned, exped, weighed, o_copied, o_turned, inverted, ctx_made = (
            sem(n) for n in ("turned", "exped", "weighed", "o_copied", "o_turned", "inverted", "ctx_made"))
        flipped, c_high, c_low, affine_made, attn_out, first_res = (
            sem(n) for n in ("flipped", "c_high", "c_low", "affine_made", "attn_out", "first_res"))
        up_done, gelu_done, ff_hi, ff_lo, down_done, out_ready, out_stored = (
            sem(n) for n in ("up_done", "gelu_done", "ff_hi", "ff_lo", "down_done", "out_ready", "out_stored"))

        def load_stack(eng, group):
            heads = qk_dram[:, group * 64:group * 64 + 64, :].rearrange("c (h r) n -> c r h n", r=DH)
            for i in range(4):
                at = 64 * (group % 2) + DH * i
                eng.dma_start(q_stack[at:at + DH, :, :].bitcast(F32), heads[i % 2]).then_inc(stack_loaded[group], 16)
                eng.dma_start(k_stack[at:at + DH, :, :].bitcast(F32), heads[2 + i // 2]).then_inc(stack_loaded[group], 16)

        block = ctx.enter_context(nc.Block())

        @block.sync
        def _(sp):
            def load_x(b):
                sp.dma_start(x[:, :, :], x_in[bass.ds(b, 1)].rearrange("b (t p) d -> p (b t) d", p=P)).then_inc(x_loaded, 16)

            def load_ada(b):
                sp.dma_start(ada[:, :, :].rearrange("p a d -> p (a d)"),
                             ada_dram[bass.ds(b, 1), :].to_broadcast([P, 2 * D])).then_inc(ada_loaded, 16)

            def load_mask(b):
                sp.dma_start(mask_u8[:, :, :], c["mask"][bass.ds(b, 1)].rearrange("b (t p) k -> p (b t) k", p=P)).then_inc(mask_loaded, 16)

            def load_bias(b, n):
                sp.dma_start(bias[:, n % 4, :, :], c["bias"][bass.ds(b * H + n, 1)].rearrange("h (t p) k -> p (h t) k", p=P)
                             ).then_inc(bias_loaded[n % 4], 16)

            sp.dma_start(ident[:, :], c["ident"]).then_inc(ident_loaded, 16)
            load_x(0)
            load_ada(0)
            load_mask(0)
            def spread_halves(b):
                for n in range(4):
                    sp.wait_ge(part_lo, b * 4 + n + 1)
                    part = qk_dram[2 * (n // 2):2 * (n // 2) + 2, (n % 2) * P:(n % 2 + 1) * P, :]
                    sp.dma_start(part.rearrange("c p n -> p c n"), ring[:, :, n, :].bitcast(F32)).then_inc(halves_stored, 16)
                sp.wait_ge(halves_stored, b * 64 + 64)
                load_stack(sp, 0)
                load_stack(sp, 1)

            for n in range(4):
                load_bias(0, n)
            spread_halves(0)

            def batch(b, last):
                for n in range(12 if last else H):
                    sp.wait_ge(scored, b * 64 + 4 * n + 4)
                    settle(sp, sp_passed)
                    load_bias(b, n + 4)
                    if n == 6 and not last:
                        sp.wait_ge(res_begun, b * T + T)
                        settle(sp, sp_passed)
                        load_x(b + 1)
                        load_ada(b + 1)
                        sp.wait_ge(mask_made, b + 1)
                        settle(sp, sp_passed)
                        load_mask(b + 1)
                if not last:
                    spread_halves(b + 1)
                sp.wait_ge(out_ready, b * T + T)
                sp.dma_start(x_out[bass.ds(b, 1)].rearrange("b (t p) d -> p (b t) d", p=P), res[:, :, :]).then_inc(out_stored, 16)

            with sp.Fori(0, B - 1) as b:
                batch(b, False)
            batch(B - 1, True)
            sp.wait_ge(out_stored, 16 * B)

        @block.gpsimd
        def _(pool):
            bc = lambda a, n: a.rearrange("(o n) -> o n", o=1).to_broadcast([n, a.shape[0]])
            cols = lambda a: a.rearrange("(k p) -> p k", p=P)
            for dst, src in ((bq[:, :], cols(w["bq"])), (bk[:, :], cols(w["bk"])), (bv[:, :], bc(w["bv"], P)),
                             (bo[:, :], bc(w["bo"], P)), (b1[:, :], cols(w["b1"])), (g2[:, :], cols(w["g2"])),
                             (be2[:, :], cols(w["beta2"])), (b2[:, :], bc(w["b2"], P))):
                pool.dma_start(dst, src, allow_slow_non_contiguous=True).then_inc(small_loaded, 16)
            pool.memset(v_one[:, :, :, :], 0.0).then_inc(zeros_set, 1)
            pool.wait_ge(zeros_set, 1)
            pool.memset(v_one[:, :, :, DH:DH + 1], 1.0).then_inc(zeros_set, 1)

            def convert_mask(b):
                pool.wait_ge(mask_loaded, b * 16 + 16)
                pool.wait_ge(scored, b * 64)
                settle(pool, pool_passed)
                pool.tensor_scalar(mask_add[:, :, :], mask_u8[:, :, :], MASKED, None, ALU.mult).then_inc(mask_made, 1)

            def batch(b, last):
                for group in (2, 3):
                    pool.wait_ge(scored, b * 64 + 16 * (group - 1))
                    settle(pool, pool_passed)
                    load_stack(pool, group)
                if not last:
                    convert_mask(b + 1)

            convert_mask(0)
            with pool.Fori(0, B - 1) as b:
                batch(b, False)
            batch(B - 1, True)

        @block.tensor
        def _(pe):
            def halves(m, k, lo, n):
                return tuple(x[:, k, lo:lo + n] for x in m)

            xt, ct = (xt_hi, xt_lo), (ct_hi, ct_lo)

            def flip_x(b):
                pe.wait_ge(x_step, b * X_STEPS + X_STEPS)
                pe.wait_ge(scored, b * 64)
                flip(pe, (bank[0], bank[1]), x, ident[:, :], x_flipped)

            def project_qk(b, ns):
                for n in ns:
                    if n == 2:
                        pe.wait_ge(v_ready, b * 2 + 2)
                    for k in range(DK):
                        last = product(pe, (F2, F3, F0, F1)[n], halves((wq, wq, wk, wk)[n], k, (n % 2) * P, P),
                                       halves(xt, k, 0, S), k == 0, k == DK - 1)
                    last.then_inc(projected, 1)

            def project_v(b):
                pe.wait_ge(x_low, b * 2 + 2)
                for t in range(T):
                    out = (F0, F1)[t // 2][:, (t % 2) * D:(t % 2 + 1) * D]
                    for k in range(DK):
                        last = product(pe, out, halves(xt, k, t * P, P), halves(wv, k, 0, D), k == 0, k == DK - 1)
                    if t % 2:
                        last.then_inc(v_projected, 1)

            def batch(b, last_batch):
                def score(n, t):
                    if n == 0 and t == 0:
                        pe.wait_ge(mask_made, b + 1)
                        pe.wait_ge(gelu_done, b * FK)
                    if n % 4 == 0 and t == 0:
                        pe.wait_ge(stack_loaded[n // 4], b * 128 + 128)
                    if 4 * n + t >= 2:
                        pe.wait_ge(scored, b * 64 + 4 * n + t - 1)
                    rows = slice(64 * (n // 4 % 2), 64 * (n // 4 % 2) + 64)
                    pe.matmul(bank[t % 2][:, :], q_stack[rows, n % 4, t * P:(t + 1) * P], k_stack[rows, n % 4, :],
                              start=True, stop=False)
                    pe.matmul(bank[t % 2][:, :], ident_bf[:, :], mask_add[:, t, :], start=False,
                              stop=True).then_inc(scores_ready, 1)

                def turn(n, kt):
                    if n == 0 and kt == 0:
                        pe.wait_ge(out_ready, b * T)
                        pe.wait_ge(part_lo, b * 4 + 4)
                    if kt == 0:
                        pe.wait_ge(shifted_outer, b * 32 + 2 * n + 2)
                        pe.wait_ge(shifted_inner, b * 32 + 2 * n + 2)
                    if kt % 2 == 0 and n:
                        pe.wait_ge(exped, b * 32 + 2 * n - 1 + kt // 2)
                    for t in range(T):
                        last = pe.transpose(flips[:, kt, t * P:(t + 1) * P],
                                            scores[:, n % 2, t, kt * P:(kt + 1) * P], ident[:, :])
                    last.then_inc(turned, 1)

                def weigh(group, kt):
                    if kt == 0:
                        pe.wait_ge(exped, b * 32 + 8 * group + 8)
                    if kt == 0 and group:
                        pe.wait_ge(o_copied, b * 4 + group)
                    elif kt == 0:
                        pe.wait_ge(v_ready, b * 2 + 2)
                    for j in range(4):
                        last = pe.matmul(o_bank[32 * j:32 * j + 32, :], v_one[:, kt, 4 * group + j, :],
                                         probs[:, (4 * group + j) % SLOTS, kt, :], start=kt == 0, stop=kt == T - 1,
                                         skip_group_check=True)
                    if kt == T - 1:
                        last.then_inc(weighed, 1)

                def turn_back(group):
                    pe.wait_ge(o_copied, b * 4 + group + 1)
                    pe.wait_ge(ctx_made, b * 4 + group)
                    for t in range(T):
                        last = pe.transpose(n_bank[:, t * P:(t + 1) * P], o_sb[:, t * P:(t + 1) * P], ident[:, :])
                    last.then_inc(o_turned, 1)

                for step in range(T * H + LAG):
                    if step < T * H:
                        score(step // T, step % T)
                    if step >= LAG:
                        turn((step - LAG) // T, (step - LAG) % T)
                    group, at = divmod(step - 4 * T - LAG - 1, 4 * T)
                    if 0 <= group < 3 and at < T:
                        weigh(group, at)
                    if 0 <= group < 3 and at == T + 2:
                        turn_back(group)
                if not last_batch:
                    flip_x(b + 1)
                for kt in range(T):
                    weigh(3, kt)
                turn_back(3)
                if not last_batch:
                    project_v(b + 1)
                pe.wait_ge(ctx_made, b * 4 + 4)
                pe.wait_ge(scored, b * 64 + 64)
                flip(pe, (bank[0], bank[1]), ctxt, ident[:, :], flipped)
                if not last_batch:
                    project_qk(b + 1, (0,))
                pe.wait_ge(c_low, b * 4 + 2)
                for t in range(T):
                    out = (o_bank, n_bank)[t // 2][:, (t % 2) * D:(t % 2 + 1) * D]
                    for k in range(DK):
                        last = product(pe, out, halves(ct, k, t * P, P), halves(wo, k, 0, D), k == 0, k == DK - 1)
                    if t % 2:
                        last.then_inc(attn_out, 1)
                if not last_batch:
                    project_qk(b + 1, (1, 2, 3))
                pe.wait_ge(norm_step, b * NORM_STEPS + NORM_STEPS)
                flip(pe, (bank[0], bank[1]), ctxt, ident[:, :], flipped)
                if not last_batch:
                    pe.wait_ge(part_lo, (b + 1) * 4 + 2)
                outs = (F2, F3, o_bank[:, :], n_bank[:, :])

                def down(m):
                    pe.wait_ge(ff_lo, b * FK + m + 1)
                    for t in range(T):
                        last = product(pe, outs[t][:, 0:D], halves((ring_hi, ring_lo), m % 4, t * P, P),
                                       halves(w2, m, 0, D), m == 0, m == FK - 1)
                    last.then_inc(down_done, 1)

                for m in range(FK):
                    if m >= 2:
                        pe.wait_ge(gelu_done, b * FK + m - 1)
                    for k in range(DK):
                        if m == 0:
                            pe.wait_ge(c_low, b * 4 + 3 + k)
                        last = product(pe, bank[m % 2][:, :], halves(w1, k, m * P, P), halves(ct, k, 0, S), k == 0, k == DK - 1)
                    last.then_inc(up_done, 1)
                    if m >= 2:
                        down(m - 2)
                down(FK - 2)
                down(FK - 1)

            pe.wait_ge(ident_loaded, 16)
            flip_x(0)
            project_v(0)
            project_qk(0, (0, 1, 2, 3))
            with pe.Fori(0, B - 1) as b:
                batch(b, False)
            batch(B - 1, True)

        @block.scalar
        def _(act):
            def x_highs(b):
                for k in range(DK):
                    act.wait_ge(x_flipped, b * 2 + k + 1)
                    act.activation(xt_hi[:, k, :], bank[k][:, :], ACT.Copy).then_inc(x_high, 1)

            def part_highs(b):
                for n, add in enumerate((bq[:, 0:1], bq[:, 1:2], bk[:, 0:1], bk[:, 1:2])):
                    act.wait_ge(projected, b * 4 + n + 1)
                    act.activation(ring_hi[:, n, :], flips[:, (n + 2) % 4, :], ACT.Identity, bias=add).then_inc(part_hi, 1)

            def batch(b, last):
                def copy_o(group):
                    act.wait_ge(weighed, b * 4 + group + 1)
                    act.wait_ge(o_turned, b * 4 + group)
                    act.activation(o_sb[:, :], o_bank[:, :], ACT.Copy).then_inc(o_copied, 1)

                for n in range(H + 1):
                    for half in range(2):
                        if n < H:
                            act.wait_ge(scored, b * 64 + 4 * n + half + 2)
                            act.activation(scores[:, n % 2, half + 1, :], scores[:, n % 2, half + 1, :], ACT.Identity,
                                           bias=less_max[:, n % 2, half + 1:half + 2], scale=-1.0).then_inc(shifted_inner, 1)
                        if n % 4 == 2 and n > 4 and half == 0:
                            copy_o(n // 4 - 1)
                        if n:
                            act.wait_ge(turned, b * 64 + 4 * n + 2 * half - 2)
                            act.activation(probs[:, (n - 1) % SLOTS, 2 * half:2 * half + 2, :],
                                           flips[:, 2 * half:2 * half + 2, :], ACT.Exp).then_inc(exped, 1)
                if not last:
                    x_highs(b + 1)
                copy_o(3)
                for k in range(DK):
                    act.wait_ge(flipped, b * 4 + k + 1)
                    act.activation(ct_hi[:, k, :], bank[k][:, :], ACT.Copy).then_inc(c_high, 1)
                if not last:
                    part_highs(b + 1)
                for k in range(DK):
                    act.wait_ge(flipped, b * 4 + 3 + k)
                    act.wait_ge(ff_lo, b * FK)
                    act.activation(y[:, k, :], bank[k][:, :], ACT.Identity, bias=be2[:, k:k + 1],
                                   scale=g2[:, k:k + 1]).then_inc(affine_made, 1)
                for m in range(FK):
                    act.wait_ge(up_done, b * FK + m + 1)
                    if m < 2:
                        act.wait_ge(c_low, b * 4 + 3 + m)
                    else:
                        act.wait_ge(ff_lo, b * FK + m - 1)
                    act.activation(y[:, m % 2, :], bank[m % 2][:, :], ACT.Gelu_apprx_sigmoid,
                                   bias=b1[:, m:m + 1]).then_inc(gelu_done, 1)

            x_highs(0)
            act.wait_ge(attn_set, 1)
            part_highs(0)
            act.wait_ge(small_loaded, 128)
            with act.Fori(0, B - 1) as b:
                batch(b, False)
            batch(B - 1, True)

        @block.vector
        def _(dve):
            def norm_x(b, n, t):
                at = b * X_STEPS
                if n == 0:
                    if t == 0:
                        dve.wait_ge(x_loaded, b * 16 + 16)
                    norm_stats(dve, x, stats, t, x_step)
                if n == 1 and t == 0:
                    norm_guess(dve, dve_passed, stats, mv, nt, 1e-5, x_step, at)
                if n == 1 and t:
                    norm_newton(dve, t - 1, nt, x_step, at)
                if n == 2:
                    if t == 0:
                        dve.wait_ge(ada_loaded, b * 16 + 16)
                        dve.wait_ge(x_step, at + NORM_ROOT)
                    dve.scalar_tensor_tensor(out=x[:, t, :], in0=x[:, t, :], scalar=mv[:, t, 0:1], in1=ada[:, 0, :],
                                             op0=ALU.subtract, op1=ALU.mult).then_inc(x_step, 1)
                if n == 3:
                    dve.wait_ge(x_step, at + NORM_ROOT + T + t)
                    dve.scalar_tensor_tensor(out=x[:, t, :], in0=x[:, t, :], scalar=nt[:, 2, t:t + 1], in1=ada[:, 1, :],
                                             op0=ALU.mult, op1=ALU.add).then_inc(x_step, 1)

            def x_lows(b):
                for k in range(DK):
                    dve.wait_ge(x_high, b * 2 + k + 1)
                    dve.tensor_tensor(xt_lo[:, k, :], bank[k][:, :], xt_hi[:, k, :].bitcast(F32), ALU.subtract).then_inc(x_low, 1)

            def part_lows(b, ns):
                for n in ns:
                    add = (bq[:, 0:1], bq[:, 1:2], bk[:, 0:1], bk[:, 1:2])[n]
                    dve.wait_ge(part_hi, b * 4 + n + 1)
                    dve.scalar_tensor_tensor(out=ring_lo[:, n, :], in0=flips[:, (n + 2) % 4, :], scalar=add,
                                             in1=ring_hi[:, n, :].bitcast(F32), op0=ALU.add, op1=ALU.subtract).then_inc(part_lo, 1)

            def take_v(b):
                for i, src in enumerate((F0, F1)):
                    dve.wait_ge(v_projected, b * 2 + i + 1)
                    dve.tensor_tensor(v_one[:, 2 * i:2 * i + 2, :, 0:DH], src.rearrange("p (t h d) -> p t h d", t=2, d=DH),
                                      over_rows(bv[:, :], 2).rearrange("p t (h d) -> p t h d", d=DH), ALU.add).then_inc(v_ready, 1)

            def batch(b, last):
                def normalise(group):
                    dve.wait_ge(o_turned, b * 4 + group + 1)
                    o = n_bank[:, :].rearrange("p (t h c) -> p t h c", t=T, h=4)
                    dve.reciprocal(one_over[:, :, :], o[:, :, :, DH]).then_inc(inverted, 1)
                    dve.wait_ge(inverted, b * 4 + group + 1)
                    dve.tensor_tensor(ctxt[:, :, group * 64:group * 64 + 64].rearrange("p t (h d) -> p t h d", d=DH),
                                      o[:, :, :, 0:DH], one_over[:, :, :].unsqueeze(3).to_broadcast([P, T, 4, DH]),
                                      ALU.mult).then_inc(ctx_made, 1)

                dve.wait_ge(halves_stored, b * 64 + 64)
                for n in range(H):
                    for t in range(T):
                        if t == 0:
                            dve.wait_ge(bias_loaded[n % 4], b * 64 + 16 * (n // 4 + 1))
                            if n >= 2:
                                dve.wait_ge(turned, b * 64 + 4 * n - 4)
                        dve.wait_ge(scores_ready, b * 64 + 4 * n + t + 1)
                        settle(dve, dve_passed)
                        dve.tensor_tensor_reduce(out=scores[:, n % 2, t, :], in0=bank[t % 2][:, :], in1=bias[:, n % 4, t, :],
                                                 scale=-1.0, scalar=3.0e38, op0=ALU.add, op1=ALU.min,
                                                 accum_out=less_max[:, n % 2, t:t + 1]).then_inc(scored, 1)
                        if t in (0, 3):
                            dve.wait_ge(scored, b * 64 + 4 * n + t + 1)
                            dve.tensor_scalar(scores[:, n % 2, t, :], scores[:, n % 2, t, :], -1.0, less_max[:, n % 2, t:t + 1],
                                              ALU.mult, ALU.add).then_inc(shifted_outer, 1)
                        if n % 4 == 3 and n > 4 and t == 2:
                            normalise(n // 4 - 1)
                        if n == 3:
                            dve.wait_ge(out_stored, b * 16)
                            dve.tensor_tensor(res[:, t, :], x[:, t, :], bo[:, :], ALU.add).then_inc(res_begun, 1)
                        if not last and 8 <= n < 12:
                            norm_x(b + 1, n - 8, t)
                if not last:
                    x_lows(b + 1)
                normalise(3)
                if not last:
                    take_v(b + 1)
                for k in range(DK):
                    dve.wait_ge(c_high, b * 2 + k + 1)
                    dve.tensor_tensor(ct_lo[:, k, :], bank[k][:, :], ct_hi[:, k, :].bitcast(F32), ALU.subtract).then_inc(c_low, 1)
                if not last:
                    part_lows(b + 1, (0,))
                dve.wait_ge(res_begun, b * T + T)
                for i in range(2):
                    dve.wait_ge(attn_out, b * 2 + i + 1)
                    dve.tensor_tensor(res[:, 2 * i:2 * i + 2, :], (o_bank, n_bank)[i][:, :].rearrange("p (t d) -> p t d", d=D),
                                      res[:, 2 * i:2 * i + 2, :], ALU.add).then_inc(first_res, 1)
                dve.wait_ge(first_res, b * 2 + 2)
                layer_norm(dve, dve_passed, res, ctxt, stats, mv, nt, 1e-5, norm_step, b * NORM_STEPS)
                if not last:
                    part_lows(b + 1, (1, 2, 3))
                for k in range(DK):
                    dve.wait_ge(affine_made, b * 2 + k + 1)
                    dve.tensor_copy(ct_hi[:, k, :], y[:, k, :]).then_inc(ff_hi, 1)
                    dve.wait_ge(ff_hi, b * (DK + FK) + k + 1)
                    dve.tensor_tensor(ct_lo[:, k, :], y[:, k, :], ct_hi[:, k, :].bitcast(F32), ALU.subtract).then_inc(c_low, 1)
                dve.wait_ge(norm_step, b * NORM_STEPS + NORM_STEPS)
                dve.tensor_tensor(res[:, :, :], res[:, :, :], over_rows(b2[:, :]), ALU.add).then_inc(res_step, 1)
                if not last:
                    dve.wait_ge(halves_stored, (b + 1) * 64 + 64)
                for m in range(FK):
                    dve.wait_ge(gelu_done, b * FK + m + 1)
                    if m >= 4:
                        dve.wait_ge(down_done, b * FK + m - 3)
                    dve.tensor_copy(ring_hi[:, m % 4, :], y[:, m % 2, :]).then_inc(ff_hi, 1)
                    dve.wait_ge(ff_hi, b * (DK + FK) + DK + m + 1)
                    dve.tensor_tensor(ring_lo[:, m % 4, :], y[:, m % 2, :], ring_hi[:, m % 4, :].bitcast(F32),
                                      ALU.subtract).then_inc(ff_lo, 1)
                dve.wait_ge(down_done, b * FK + FK)
                dve.wait_ge(res_step, b + 1)
                for t, src in enumerate((F2, F3, o_bank[:, :], n_bank[:, :])):
                    dve.tensor_tensor(res[:, t, :], src[:, 0:D], res[:, t, :], ALU.add).then_inc(out_ready, 1)

            for n in range(4):
                for t in range(T):
                    norm_x(0, n, t)
            dve.wait_ge(ident_loaded, 16)
            dve.tensor_copy(ident_bf[:, :], ident[:, :]).then_inc(ident_cast, 1)
            dve.wait_ge(small_loaded, 128)
            dve.tensor_scalar(bq[:, :], bq[:, :], SC, None, ALU.mult).then_inc(attn_set, 1)
            x_lows(0)
            dve.wait_ge(zeros_set, 2)
            take_v(0)
            part_lows(0, range(4))
            with dve.Fori(0, B - 1) as b:
                batch(b, False)
            batch(B - 1, True)


def expert_mlp_layer(nc, x_in, x_out, w, c, following):
    n_experts = w["Wi"].shape[0]
    with ExitStack() as ctx:
        def sb(name, shape, dt=F32):
            return ctx.enter_context(nc.sbuf_tensor("c_" + name, shape, dt))

        def sem(name):
            return nc.alloc_semaphore("c_" + name)

        bank = [ctx.enter_context(nc.psum_tensor(f"c_bank{i}", [P, 512], F32)) for i in range(2)]
        flips = ctx.enter_context(nc.psum_tensor("c_flips", [P, DK, 512], F32))
        outs = [ctx.enter_context(nc.psum_tensor(f"c_out{i}", [P, 512], F32)) for i in range(4)]
        ident, id_row = sb("ident", [P, P]), sb("id_row", [1, B], I32)
        x, res, y = sb("x", [P, T, D]), sb("res", [P, T, D]), sb("y", [P, T, D])
        raw = sb("raw", [P, 2, 2048])
        w_hi, w_lo = sb("w_hi", [P, 2, 2048], F32R), sb("w_lo", [P, 2, 2048], F32R)
        bi_next, bi = sb("bi_next", [P, FK]), sb("bi", [P, FK])
        bo, gamma, beta = sb("bo", [P, D]), sb("gamma", [P, D]), sb("beta", [P, D])
        xt_hi, xt_lo = sb("xt_hi", [P, DK, S], F32R), sb("xt_lo", [P, DK, S], F32R)
        g = sb("g", [P, 2, S])
        ring_hi, ring_lo = sb("ring_hi", [P, 4, S], F32R), sb("ring_lo", [P, 4, S], F32R)
        stats, mv, nt = sb("stats", [P, T, 6]), sb("mv", [P, T, 2]), sb("nt", [P, 4, T])
        raw_next = following.raw_place(nc, ctx)

        dve_passed, sp_passed = sem("dve_passed"), sem("sp_passed")
        ids_loaded, ident_loaded, x_loaded, bi_loaded, bo_loaded, scale_loaded = (
            sem(n) for n in ("ids_loaded", "ident_loaded", "x_loaded", "bi_loaded", "bo_loaded", "scale_loaded"))
        raw_loaded = [sem("raw_loaded0"), sem("raw_loaded1")]
        w_high, w_low, flipped, x_high, x_low, bi_taken = (
            sem(n) for n in ("w_high", "w_low", "flipped", "x_high", "x_low", "bi_taken"))
        up_done, gelu_done, ff_hi, ff_lo, down_done = (sem(n) for n in ("up_done", "gelu_done", "ff_hi", "ff_lo", "down_done"))
        res_begun, summed, norm_step, scaled, y_made, y_stored = (
            sem(n) for n in ("res_begun", "summed", "norm_step", "scaled", "y_made", "y_stored"))
        block = ctx.enter_context(nc.Block())

        @block.sync
        def _(sp):
            sp.dma_start(id_row[:, :], c["mlp_expert"].rearrange("(o n) -> o n", o=1)).then_inc(ids_loaded, 16)
            sp.dma_start(ident[:, :], c["ident"]).then_inc(ident_loaded, 16)

            def expert(b, row):
                sp.reg_alu(row, sp.value_load(id_row[0:1, bass.ds(b, 1)]), 0, ALU.max)
                sp.reg_alu(row, row, n_experts - 1, ALU.min)
                return sp.snap(row, min_val=0, max_val=n_experts - 1)

            def load_x(b):
                sp.dma_start(x[:, :, :], x_in[bass.ds(b, 1)].rearrange("b (t p) d -> p (b t) d", p=P)).then_inc(x_loaded, 16)

            def load_weights(e, i):
                name, k = (("Wi", DK), ("Wo", FK))[i]
                sp.dma_start(raw[:, i, :].rearrange("p (k n) -> p k n", k=k),
                             w[name][bass.ds(e, 1)].rearrange("e (k p) n -> p (e k) n", p=P)).then_inc(raw_loaded[i], 16)

            def load_bi(e):
                sp.dma_start(bi_next[:, :], w["bi"][bass.ds(e, 1)].rearrange("e (k p) -> p (e k)", p=P),
                             allow_slow_non_contiguous=True).then_inc(bi_loaded, 16)

            def load_row(dst, name, e, loaded):
                sp.dma_start(dst[:, :], w[name][bass.ds(e, 1), :].to_broadcast([P, D])).then_inc(loaded, 16)

            def store_y(b):
                sp.wait_ge(y_made, b + 1)
                settle(sp, sp_passed)
                sp.dma_start(x_out[bass.ds(b, 1)].rearrange("b (t p) d -> p (b t) d", p=P), y[:, :, :]).then_inc(y_stored, 16)

            row, next_row = sp.alloc_register("c_expert"), sp.alloc_register("c_next_expert")
            load_x(0)
            sp.wait_ge(ids_loaded, 16)
            e = expert(0, row)
            load_weights(e, 0)
            load_bi(e)
            load_weights(e, 1)
            load_row(bo, "bo", e, bo_loaded)

            def batch(b, first, last):
                e = expert(b, row)
                if first:
                    load_row(gamma, "gamma", e, scale_loaded)
                    load_row(beta, "beta", e, scale_loaded)
                if not last:
                    e_next = expert(b + 1, next_row)
                    for i in range(2):
                        sp.wait_ge(w_low, b * 2 + i + 1)
                        load_weights(e_next, i)
                    sp.wait_ge(bi_taken, b + 1)
                    load_bi(e_next)
                if not first:
                    store_y(b - 1)
                    load_row(gamma, "gamma", e, scale_loaded)
                    load_row(beta, "beta", e, scale_loaded)
                if not last:
                    sp.wait_ge(res_begun, b + 1)
                    sp.wait_ge(flipped, b * 2 + 2)
                    settle(sp, sp_passed)
                    load_x(b + 1)
                    load_row(bo, "bo", e_next, bo_loaded)

            batch(0, True, False)
            with sp.Fori(1, B - 1) as b:
                batch(b, False, False)
            batch(B - 1, False, True)
            store_y(B - 1)
            sp.wait_ge(y_stored, 16 * B)

        @block.gpsimd
        def _(pool):
            following.cut(pool, raw_next)

        @block.tensor
        def _(pe):
            w1 = tuple(m[:, 0, :].rearrange("p (k n) -> p k n", k=DK) for m in (w_hi, w_lo))
            w2 = tuple(m[:, 1, :].rearrange("p (k n) -> p k n", k=FK) for m in (w_hi, w_lo))

            def flip_x(b):
                pe.wait_ge(x_loaded, b * 16 + 16)
                pe.wait_ge(x_low, b * 2)
                flip(pe, (flips[:, 0, :], flips[:, 1, :]), x, ident[:, :], flipped)

            def batch(b, last_batch):
                pe.wait_ge(x_low, b * 2 + 2)
                pe.wait_ge(w_low, b * 2 + 1)

                def down(m):
                    if m == 0:
                        pe.wait_ge(w_low, b * 2 + 2)
                        pe.wait_ge(summed, b * T)
                    pe.wait_ge(ff_lo, b * FK + m + 1)
                    for t in range(T):
                        a = tuple(r[:, m % 4, t * P:(t + 1) * P] for r in (ring_hi, ring_lo))
                        last = product(pe, outs[t][:, 0:D], a, tuple(x[:, m, :] for x in w2), m == 0, m == FK - 1)
                    last.then_inc(down_done, 1)

                for m in range(FK):
                    if m >= 2:
                        pe.wait_ge(gelu_done, b * FK + m - 1)
                    for k in range(DK):
                        last = product(pe, bank[m % 2][:, :], tuple(x[:, k, m * P:(m + 1) * P] for x in w1),
                                       tuple(x[:, k, :] for x in (xt_hi, xt_lo)), k == 0, k == DK - 1)
                    last.then_inc(up_done, 1)
                    if m >= 2:
                        down(m - 2)
                if not last_batch:
                    flip_x(b + 1)
                down(FK - 2)
                down(FK - 1)

            pe.wait_ge(ident_loaded, 16)
            flip_x(0)
            with pe.Fori(0, B - 1) as b:
                batch(b, False)
            batch(B - 1, True)

        @block.scalar
        def _(act):
            def highs(b, part):
                if part == 0:
                    act.wait_ge(up_done, b * FK)
                    for k in range(DK):
                        act.wait_ge(flipped, b * 2 + k + 1)
                        act.activation(xt_hi[:, k, :], flips[:, k, :], ACT.Copy).then_inc(x_high, 1)
                else:
                    act.wait_ge(down_done, b * FK)
                act.wait_ge(raw_loaded[part], b * 16 + 16)
                act.activation(w_hi[:, part, :], raw[:, part, :], ACT.Copy).then_inc(w_high, 1)

            def batch(b, last):
                for m in range(FK):
                    if m == 0:
                        act.wait_ge(bi_taken, b + 1)
                    act.wait_ge(up_done, b * FK + m + 1)
                    if m >= 2:
                        act.wait_ge(ff_lo, b * FK + m - 1)
                    else:
                        act.wait_ge(ff_lo, b * FK)
                    act.activation(g[:, m % 2, :], bank[m % 2][:, :], ACT.Gelu, bias=bi[:, m:m + 1]).then_inc(gelu_done, 1)
                if not last:
                    highs(b + 1, 0)
                    highs(b + 1, 1)

            highs(0, 0)
            highs(0, 1)
            with act.Fori(0, B - 1) as b:
                batch(b, False)
            batch(B - 1, True)

        @block.vector
        def _(dve):
            def lows(b, part):
                if part == 0:
                    for k in range(DK):
                        dve.wait_ge(x_high, b * 2 + k + 1)
                        dve.tensor_tensor(xt_lo[:, k, :], flips[:, k, :], xt_hi[:, k, :].bitcast(F32), ALU.subtract).then_inc(x_low, 1)
                dve.wait_ge(w_high, b * 2 + part + 1)
                dve.tensor_tensor(w_lo[:, part, :], raw[:, part, :], w_hi[:, part, :].bitcast(F32), ALU.subtract).then_inc(w_low, 1)

            def take_bi(b):
                dve.wait_ge(bi_loaded, b * 16 + 16)
                dve.wait_ge(gelu_done, b * FK)
                dve.tensor_copy(bi[:, :], bi_next[:, :]).then_inc(bi_taken, 1)

            def finish(b, n):
                base = b * NORM_STEPS
                if n == 0:
                    for t in range(T):
                        norm_stats(dve, res, stats, t, norm_step)
                if n == 1:
                    norm_root(dve, dve_passed, stats, mv, nt, 1e-12, norm_step, base)
                if n == 2:
                    dve.wait_ge(norm_step, base + NORM_ROOT)
                    dve.wait_ge(y_stored, b * 16)
                    for t in range(T):
                        dve.tensor_scalar(y[:, t, :], res[:, t, :], mv[:, t, 0:1], nt[:, 2, t:t + 1], ALU.subtract,
                                          ALU.mult).then_inc(norm_step, 1)
                if n == 3:
                    dve.wait_ge(norm_step, base + NORM_STEPS)
                    dve.wait_ge(scale_loaded, b * 32 + 32)
                    dve.tensor_tensor(y[:, :, :], y[:, :, :], over_rows(gamma[:, :]), ALU.mult).then_inc(scaled, 1)
                if n == 4:
                    dve.wait_ge(scaled, b + 1)
                    dve.tensor_tensor(y[:, :, :], y[:, :, :], over_rows(beta[:, :]), ALU.add).then_inc(y_made, 1)

            def batch(b, first, last):
                for m in range(FK):
                    dve.wait_ge(gelu_done, b * FK + m + 1)
                    if m >= 4:
                        dve.wait_ge(down_done, b * FK + m - 3)
                    else:
                        dve.wait_ge(down_done, b * FK)
                    dve.tensor_copy(ring_hi[:, m % 4, :], g[:, m % 2, :]).then_inc(ff_hi, 1)
                    dve.wait_ge(ff_hi, b * FK + m + 1)
                    dve.tensor_tensor(ring_lo[:, m % 4, :], g[:, m % 2, :], ring_hi[:, m % 4, :].bitcast(F32),
                                      ALU.subtract).then_inc(ff_lo, 1)
                    if not first and m < 5:
                        finish(b - 1, m)
                    if m == 5:
                        dve.wait_ge(bo_loaded, b * 16 + 16)
                        dve.wait_ge(x_loaded, b * 16 + 16)
                        dve.tensor_tensor(res[:, :, :], x[:, :, :], over_rows(bo[:, :]), ALU.add).then_inc(res_begun, 1)
                if not last:
                    take_bi(b + 1)
                    lows(b + 1, 0)
                dve.wait_ge(down_done, b * FK + FK)
                dve.wait_ge(res_begun, b + 1)
                for t in range(T):
                    dve.tensor_tensor(res[:, t, :], outs[t][:, 0:D], res[:, t, :], ALU.add).then_inc(summed, 1)
                dve.wait_ge(summed, b * T + T)
                if not last:
                    lows(b + 1, 1)

            take_bi(0)
            lows(0, 0)
            lows(0, 1)
            batch(0, True, False)
            with dve.Fori(1, B - 1) as b:
                batch(b, False, False)
            batch(B - 1, False, True)
            for n in range(5):
                finish(B - 1, n)


def causal_attention_layer(nc, x_in, x_out, w, c, scratch, sems, weights):
    qk_dram = scratch["halves"]
    with ExitStack() as ctx:
        def sb(name, shape, dt=F32):
            return ctx.enter_context(nc.sbuf_tensor("d_" + name, shape, dt))

        def sem(name):
            return nc.alloc_semaphore("d_" + name)

        def shared(*names):
            return (sems[n] for n in names)

        bank = [ctx.enter_context(nc.psum_tensor(f"d_bank{i}", [P, 512], F32)) for i in range(2)]
        flips = ctx.enter_context(nc.psum_tensor("d_flips", [P, 4, 512], F32))
        o_bank = ctx.enter_context(nc.psum_tensor("d_obank", [P, 512], F32))
        n_bank = ctx.enter_context(nc.psum_tensor("d_nbank", [P, 512], F32))
        F0, F1, F2, F3 = (flips[:, i, :] for i in range(4))

        wq, wk, wv, wo, w1, w2 = weights.halves()
        ident, ident_bf, causal = sb("ident", [P, P]), sb("ident_bf", [P, P], BF16), sb("causal", [P, P])
        causal_qk, causal_kq = sb("causal_qk", [P, P], BF16), sb("causal_kq", [P, P], BF16)
        bq, bk, b1 = sb("bq", [P, DK]), sb("bk", [P, DK]), sb("b1", [P, FK])
        g1, be1, g2, be2 = (sb(n, [P, DK]) for n in ("g1", "be1", "g2", "be2"))
        bv, bo, b2 = sb("bv", [P, D]), sb("bo", [P, D]), sb("b2", [P, D])
        gates, gate = sb("gates", [P, B]), sb("gate", [P, 1])
        xn, x, res, ctxt = (sb(n, [P, T, D]) for n in ("xn", "x", "res", "ctxt"))
        xt_hi, xt_lo = sb("xt_hi", [P, DK, S], F32R), sb("xt_lo", [P, DK, S], F32R)
        ct_hi, ct_lo = sb("ct_hi", [P, DK, S], F32R), sb("ct_lo", [P, DK, S], F32R)
        y = sb("y", [P, 2, S])
        v_one = sb("v_one", [P, T, H, 32])
        q_stack, k_stack = sb("q_stack", [DH * 4 + 1, H, S], F32R), sb("k_stack", [DH * 4 + 1, H, S], F32R)
        less_max, max_row = sb("less_max", [P, 2, 4 * T]), sb("max_row", [4 * T, 2, P], F32R)
        shared_at = nc.sbuf_base
        probs = sb("probs", [P, SLOTS, T, S])
        ring = nc.alloc_sbuf_tensor_at("d_ring", [P, 2, 4, S], F32R, offset=shared_at)
        ring_hi, ring_lo = ring[:, 0, :, :], ring[:, 1, :, :]
        o_sb, one_over = sb("o_sb", [P, S]), sb("one_over", [P, T, 4])
        stats, mv, nt = sb("stats", [P, T, 6]), sb("mv", [P, T, 2]), sb("nt", [P, 4, T])

        early_loaded, small_loaded, set_step, pool_set = (
            sem(n) for n in ("early_loaded", "small_loaded", "set_step", "pool_set"))
        xn_loaded, xn_step, x_affine, max_turned, row_made, shifted, exped, delta_step, mixed = (
            sem(n) for n in ("xn_loaded", "xn_step", "x_affine", "max_turned", "row_made", "shifted", "exped",
                             "delta_step", "mixed"))
        row_loaded = [sem("row_loaded0"), sem("row_loaded1")]
        dve_passed, sp_passed, x_loaded, norm_step, res_begun = shared("dve_passed", "sp_passed", "x_loaded", "norm_step", "res_begun")
        x_flipped, x_high, x_low, projected, part_hi, part_lo, v_projected, v_ready = shared(
            "x_flipped", "x_high", "x_low", "projected", "part_hi", "part_lo", "v_projected", "v_ready")
        halves_stored, first_stack, rest_stack, scores_ready, scored = shared(
            "halves_stored", "stack_loaded0", "stack_loaded1", "scores_ready", "scored")
        weighed, o_copied, o_turned, inverted, ctx_made = shared("weighed", "o_copied", "o_turned", "inverted", "ctx_made")
        flipped, c_high, c_low, affine_made, attn_out, first_res = shared(
            "flipped", "c_high", "c_low", "affine_made", "attn_out", "first_res")
        up_done, gelu_done, ff_hi, ff_lo, down_done, out_ready, out_stored = shared(
            "up_done", "gelu_done", "ff_hi", "ff_lo", "down_done", "out_ready", "out_stored")
        spread = lambda a: a.rearrange("(o n) -> o n", o=1).to_broadcast([P, a.shape[0]])
        cols = lambda a: a.rearrange("(k p) -> p k", p=P)
        row_step = lambda ap: ap.rearrange("b (t p) d -> p (b t) d", p=P)
        block = ctx.enter_context(nc.Block())

        @block.sync
        def _(sp):
            def load_xn(b):
                sp.dma_start(xn[:, :, :], row_step(x_in[bass.ds(b - B, 1)])).then_inc(xn_loaded, 16)

            def load_x(b):
                sp.dma_start(x[:, :, :], row_step(x_in[bass.ds(b - B, 1)])).then_inc(x_loaded, 16)

            load_xn(B)
            load_x(B)

            def spread_halves(b):
                for n in range(4):
                    sp.wait_ge(part_lo, b * 4 + n + 1)
                    part = qk_dram[2 * (n // 2):2 * (n // 2) + 2, (n % 2) * P:(n % 2 + 1) * P, :]
                    sp.dma_start(part.rearrange("c p n -> p c n"), ring[:, :, n, :].bitcast(F32)).then_inc(halves_stored, 16)
                sp.wait_ge(halves_stored, b * 64 + 64)
                for first, last, loaded in ((0, 4, first_stack), (4, H, rest_stack)):
                    heads = qk_dram[:, first * DH:last * DH, :].rearrange("c (h r) n -> c r h n", r=DH)
                    for i in range(4):
                        rows = slice(DH * i, DH * i + DH)
                        sp.dma_start(q_stack[rows, first:last, :].bitcast(F32), heads[i % 2]).then_inc(loaded, 16)
                        sp.dma_start(k_stack[rows, first:last, :].bitcast(F32), heads[2 + i // 2]).then_inc(loaded, 16)

            def send_row(b, g):
                sp.wait_ge(row_made, (b - B) * 4 + g + 1)
                sp.dma_start(q_stack[4 * DH:4 * DH + 1, 4 * g:4 * g + 4, :].rearrange("o h (t n) -> o (h t) n", n=P).bitcast(F32),
                             max_row[:, g % 2, :].bitcast(F32)).then_inc(row_loaded[g % 2], 16)

            def batch(b, last):
                if not last:
                    sp.wait_ge(x_flipped, b * 2 + 2)
                    settle(sp, sp_passed)
                    load_xn(b + 1)
                for g in range(1, 4):
                    send_row(b, g)
                if not last:
                    spread_halves(b + 1)
                    send_row(b + 1, 0)
                sp.wait_ge(out_ready, b * T + T)
                settle(sp, sp_passed)
                sp.dma_start(row_step(x_out[bass.ds(b - B, 1)]), res[:, :, :]).then_inc(out_stored, 16)
                if not last:
                    load_x(b + 1)

            spread_halves(B)
            send_row(B, 0)
            with sp.Fori(B, 2 * B - 1) as b:
                batch(b, False)
            batch(2 * B - 1, True)
            sp.wait_ge(out_stored, 16 * 2 * B)

        @block.gpsimd
        def _(pool):
            for dst, src in ((bv, spread(w["bv"])), (bo, spread(w["bo"])), (b1, cols(w["b1"])), (gates, spread(c["gate"])),
                             (g2, cols(w["gamma2"])), (be2, cols(w["beta2"])), (b2, spread(w["b2"]))):
                pool.dma_start(dst[:, :], src, allow_slow_non_contiguous=True).then_inc(small_loaded, 16)
            pool.memset(k_stack[4 * DH:4 * DH + 1, :, :].bitcast(F32), 1.0).then_inc(pool_set, 1)
            pool.wait_ge(pool_set, 1)
            pool.memset(v_one[:, :, :, :], 0.0).then_inc(pool_set, 1)
            pool.wait_ge(pool_set, 2)
            pool.memset(v_one[:, :, :, DH:DH + 1], 1.0).then_inc(pool_set, 1)

        @block.tensor
        def _(pe):
            def halves(m, k, lo, n):
                return tuple(x[:, k, lo:lo + n] for x in m)

            xt, ct = (xt_hi, xt_lo), (ct_hi, ct_lo)

            def flip_x(b):
                pe.wait_ge(xn_step, (b - B) * NORM_STEPS + NORM_STEPS)
                pe.wait_ge(scored, b * 64)
                flip(pe, (bank[0], bank[1]), xn, ident[:, :], x_flipped)

            def project_qk(b, ns):
                for n in ns:
                    if n == 2:
                        pe.wait_ge(v_ready, b * 2 + 2)
                    for k in range(DK):
                        last = product(pe, (F2, F3, F0, F1)[n], halves((wq, wq, wk, wk)[n], k, (n % 2) * P, P),
                                       halves(xt, k, 0, S), k == 0, k == DK - 1)
                    last.then_inc(projected, 1)

            def project_v(b):
                pe.wait_ge(x_low, b * 2 + 2)
                for t in range(T):
                    out = (F0, F1)[t // 2][:, (t % 2) * D:(t % 2 + 1) * D]
                    for k in range(DK):
                        last = product(pe, out, halves(xt, k, t * P, P), halves(wv, k, 0, D), k == 0, k == DK - 1)
                    if t % 2:
                        last.then_inc(v_projected, 1)

            def score(b, n):
                if n == 0:
                    pe.wait_ge(first_stack, b * 128 + 128)
                    pe.wait_ge(part_lo, b * 4 + 4)
                if n == 16:
                    pe.wait_ge(rest_stack, b * 128 + 128)
                    pe.wait_ge(row_made, (b - B) * 4 + 1)
                if n == AHEAD:
                    pe.wait_ge(gelu_done, b * FK)
                if n >= 2:
                    pe.wait_ge(scored, b * 64 + n - 1)
                h, t = divmod(n, T)
                out = (F0, F1)[n % 2] if n < AHEAD else bank[n % 2][:, :]
                pe.matmul(out[:, 0:(t + 1) * P], q_stack[0:4 * DH, h, t * P:(t + 1) * P],
                          k_stack[0:4 * DH, h, 0:(t + 1) * P], start=True, stop=False)
                pe.matmul(out[:, t * P:(t + 1) * P], ident_bf[:, :], causal_qk[:, :], start=False,
                          stop=True).then_inc(scores_ready, 1)

            def turn_max(b, g):
                pe.wait_ge(scored, b * 64 + 16 * g + 16)
                if g == 1:
                    pe.wait_ge(mixed, (b - B) * 5)
                if g > 1:
                    pe.wait_ge(ctx_made, b * 4 + g - 1)
                out = F0 if g == 0 else n_bank[:, :]
                pe.transpose(out[0:4 * T, 0:P], less_max[:, g % 2, :], ident[:, :]).then_inc(max_turned, 1)

            def batch(b, last_batch):
                at = b - B

                def score_keys(n):
                    if n % 16 == 0:
                        pe.wait_ge(row_loaded[n // 16 % 2], at * 32 + 16 * (n // 32 + 1))
                    if n == 0:
                        pe.wait_ge(scored, b * 64 + AHEAD)
                        pe.wait_ge(mixed, at * 5)
                    if n >= 4:
                        pe.wait_ge(exped, at * 64 + n - 3)
                    h, kt = divmod(n, T)
                    pe.matmul(flips[:, kt, kt * P:S], k_stack[:, h, kt * P:(kt + 1) * P], q_stack[:, h, kt * P:S],
                              start=True, stop=False)
                    pe.matmul(flips[:, kt, kt * P:(kt + 1) * P], ident_bf[:, :], causal_kq[:, :], start=False,
                              stop=True).then_inc(shifted, 1)

                def weigh(g, kt):
                    if kt == 0:
                        pe.wait_ge(exped, at * 64 + 16 * g + 16)
                        pe.wait_ge(o_copied, b * 4 + g)
                    for j in range(4):
                        last = pe.matmul(o_bank[32 * j:32 * j + 32, kt * P:S], v_one[:, kt, 4 * g + j, :],
                                         probs[:, (4 * g + j) % SLOTS, kt, kt * P:S], start=kt == 0, stop=kt == T - 1,
                                         skip_group_check=True)
                    if kt == T - 1:
                        last.then_inc(weighed, 1)

                def turn_back(g):
                    pe.wait_ge(o_copied, b * 4 + g + 1)
                    pe.wait_ge(row_made, at * 4 + min(g + 2, 4))
                    pe.wait_ge(ctx_made, b * 4 + g)
                    for t in range(T):
                        last = pe.transpose(n_bank[:, t * P:(t + 1) * P], o_sb[:, t * P:(t + 1) * P], ident[:, :])
                    last.then_inc(o_turned, 1)

                for step in range(T * H):
                    if step + AHEAD < T * H:
                        score(b, step + AHEAD)
                    if step in (13, 29, 45):
                        turn_max(b, (step + 3) // 16)
                    score_keys(step)
                    group, part = divmod(step - 17, 16)
                    if group >= 0 and part < T:
                        weigh(group, part)
                    if group >= 0 and part == T + 2:
                        turn_back(group)
                if not last_batch:
                    flip_x(b + 1)
                for kt in range(T):
                    weigh(3, kt)
                turn_back(3)
                if not last_batch:
                    project_v(b + 1)
                pe.wait_ge(ctx_made, b * 4 + 4)
                pe.wait_ge(scored, b * 64 + 64)
                flip(pe, (bank[0], bank[1]), ctxt, ident[:, :], flipped)
                if not last_batch:
                    project_qk(b + 1, (0,))
                pe.wait_ge(c_low, b * 4 + 2)
                for t in range(T):
                    out = (o_bank, n_bank)[t // 2][:, (t % 2) * D:(t % 2 + 1) * D]
                    for k in range(DK):
                        last = product(pe, out, halves(ct, k, t * P, P), halves(wo, k, 0, D), k == 0, k == DK - 1)
                    if t % 2:
                        last.then_inc(attn_out, 1)
                if not last_batch:
                    project_qk(b + 1, (1, 2, 3))
                pe.wait_ge(norm_step, b * NORM_STEPS + NORM_STEPS)
                flip(pe, (bank[0], bank[1]), ctxt, ident[:, :], flipped)
                if not last_batch:
                    pe.wait_ge(part_lo, (b + 1) * 4 + 2)
                outs = (F2, F3, o_bank[:, :], n_bank[:, :])

                def down(m):
                    pe.wait_ge(ff_lo, b * FK + m + 1)
                    for t in range(T):
                        last = product(pe, outs[t][:, 0:D], halves((ring_hi, ring_lo), m % 4, t * P, P),
                                       halves(w2, m, 0, D), m == 0, m == FK - 1)
                    last.then_inc(down_done, 1)

                for m in range(FK):
                    if m >= 4 and not last_batch:
                        for n in range(4 * m - 16, 4 * m - 14):
                            score(b + 1, n)
                    if m >= 2:
                        pe.wait_ge(gelu_done, b * FK + m - 1)
                    for k in range(DK):
                        if m == 0:
                            pe.wait_ge(c_low, b * 4 + 3 + k)
                        last = product(pe, bank[m % 2][:, :], halves(w1, k, m * P, P), halves(ct, k, 0, S), k == 0, k == DK - 1)
                    last.then_inc(up_done, 1)
                    if m >= 4 and not last_batch:
                        for n in range(4 * m - 14, 4 * m - 12):
                            score(b + 1, n)
                    if m >= 2:
                        down(m - 2)
                if not last_batch:
                    turn_max(b + 1, 0)
                    for n in (16, 17):
                        score(b + 1, n)
                down(FK - 2)
                if not last_batch:
                    for n in range(18, AHEAD):
                        score(b + 1, n)
                down(FK - 1)

            pe.wait_ge(early_loaded, 16 * 6)
            pe.transpose(n_bank[:, 0:P], causal[:, :], ident[:, :]).then_inc(max_turned, 1)
            flip_x(B)
            project_v(B)
            project_qk(B, (0, 1, 2, 3))
            for n in range(16):
                score(B, n)
            turn_max(B, 0)
            for n in range(16, AHEAD):
                score(B, n)
            with pe.Fori(B, 2 * B - 1) as b:
                batch(b, False)
            batch(2 * B - 1, True)

        @block.scalar
        def _(act):
            for dst, src in ((ident, c["ident"]), (causal, c["causal"]), (g1, cols(w["gamma1"])), (be1, cols(w["beta1"])),
                             (bq, cols(w["bq"])), (bk, cols(w["bk"]))):
                act.dma_start(dst[:, :], src, allow_slow_non_contiguous=True).then_inc(early_loaded, 16)

            def affine(k, scale, add, made):
                act.activation(y[:, k, :], bank[k][:, :], ACT.Identity, bias=add[:, k:k + 1],
                               scale=scale[:, k:k + 1]).then_inc(made, 1)

            def x_affines(b):
                act.wait_ge(ff_lo, b * FK - FK)
                for k in range(DK):
                    act.wait_ge(x_flipped, b * 2 + k + 1)
                    affine(k, g1, be1, x_affine)

            def part_highs(b):
                for n, add in enumerate((bq[:, 0:1], bq[:, 1:2], bk[:, 0:1], bk[:, 1:2])):
                    act.wait_ge(projected, b * 4 + n + 1)
                    act.activation(ring_hi[:, n, :], flips[:, (n + 2) % 4, :], ACT.Identity, bias=add).then_inc(part_hi, 1)

            def batch(b, last):
                def copy_o(group):
                    act.wait_ge(weighed, b * 4 + group + 1)
                    act.wait_ge(o_turned, b * 4 + group)
                    act.activation(o_sb[:, :], o_bank[:, :], ACT.Copy).then_inc(o_copied, 1)

                for n in range(T * H):
                    h, kt = divmod(n, T)
                    if n % 16 == 4 and n > 16:
                        copy_o(n // 16 - 1)
                    act.wait_ge(shifted, (b - B) * 64 + n + 1)
                    act.activation(probs[:, h % SLOTS, kt, kt * P:S], flips[:, kt, kt * P:S], ACT.Exp).then_inc(exped, 1)
                if not last:
                    x_affines(b + 1)
                copy_o(3)
                for k in range(DK):
                    act.wait_ge(flipped, b * 4 + k + 1)
                    act.activation(ct_hi[:, k, :], bank[k][:, :], ACT.Copy).then_inc(c_high, 1)
                if not last:
                    part_highs(b + 1)
                for k in range(DK):
                    act.wait_ge(flipped, b * 4 + 3 + k)
                    if not last:
                        act.wait_ge(x_low, b * 2 + 3 + k)
                    affine(k, g2, be2, affine_made)
                for m in range(FK):
                    act.wait_ge(up_done, b * FK + m + 1)
                    if m < 2:
                        act.wait_ge(c_low, b * 4 + 3 + m)
                    else:
                        act.wait_ge(ff_lo, b * FK + m - 1)
                    act.activation(y[:, m % 2, :], bank[m % 2][:, :], ACT.Gelu, bias=b1[:, m:m + 1]).then_inc(gelu_done, 1)

            act.wait_ge(early_loaded, 16 * 6)
            x_affines(B)
            act.wait_ge(set_step, 3)
            part_highs(B)
            act.wait_ge(small_loaded, 16 * 7)
            with act.Fori(B, 2 * B - 1) as b:
                batch(b, False)
            batch(2 * B - 1, True)

        @block.vector
        def _(dve):
            def norm_x(b, n, t):
                at = (b - B) * NORM_STEPS
                if n == 0:
                    if t == 0:
                        dve.wait_ge(xn_loaded, (b - B) * 16 + 16)
                    norm_stats(dve, xn, stats, t, xn_step)
                if n == 1 and t == 0:
                    norm_guess(dve, dve_passed, stats, mv, nt, 1e-5, xn_step, at)
                if n == 1 and t:
                    norm_newton(dve, t - 1, nt, xn_step, at)
                if n == 2:
                    if t == 0:
                        dve.wait_ge(xn_step, at + NORM_ROOT)
                    dve.tensor_scalar(xn[:, t, :], xn[:, t, :], mv[:, t, 0:1], nt[:, 2, t:t + 1], ALU.subtract,
                                      ALU.mult).then_inc(xn_step, 1)

            def cut(k, to_hi, to_lo, high, at, low):
                dve.tensor_copy(to_hi[:, k, :], y[:, k, :]).then_inc(high, 1)
                dve.wait_ge(high, at + k + 1)
                dve.tensor_tensor(to_lo[:, k, :], y[:, k, :], to_hi[:, k, :].bitcast(F32), ALU.subtract).then_inc(low, 1)

            def cut_x(b):
                for k in range(DK):
                    dve.wait_ge(x_affine, (b - B) * 2 + k + 1)
                    cut(k, xt_hi, xt_lo, x_high, b * 2, x_low)

            def part_lows(b, ns):
                for n in ns:
                    add = (bq[:, 0:1], bq[:, 1:2], bk[:, 0:1], bk[:, 1:2])[n]
                    dve.wait_ge(part_hi, b * 4 + n + 1)
                    dve.scalar_tensor_tensor(out=ring_lo[:, n, :], in0=flips[:, (n + 2) % 4, :], scalar=add,
                                             in1=ring_hi[:, n, :].bitcast(F32), op0=ALU.add, op1=ALU.subtract).then_inc(part_lo, 1)

            def take_v(b):
                for i, src in enumerate((F0, F1)):
                    dve.wait_ge(v_projected, b * 2 + i + 1)
                    dve.tensor_tensor(v_one[:, 2 * i:2 * i + 2, :, 0:DH], src.rearrange("p (t h d) -> p t h d", t=2, d=DH),
                                      over_rows(bv[:, :], 2).rearrange("p t (h d) -> p t h d", d=DH), ALU.add).then_inc(v_ready, 1)

            def take_max(b, n):
                src = (F0, F1)[n % 2] if n < AHEAD else bank[n % 2][:, :]
                dve.wait_ge(scores_ready, b * 64 + n + 1)
                dve.tensor_reduce(less_max[:, n // 16 % 2, n % 16:n % 16 + 1], src[:, 0:(n % T + 1) * P], AX.X, ALU.max,
                                  negate=True).then_inc(scored, 1)

            def take_row(b, g):
                dve.wait_ge(max_turned, (b - B) * 4 + g + 2)
                dve.wait_ge(row_loaded[g % 2], (b - B) * 32 + (16 if g >= 2 else 0))
                dve.tensor_copy(max_row[:, g % 2, :], (F0 if g == 0 else n_bank[:, :])[0:4 * T, 0:P]).then_inc(row_made, 1)

            def batch(b, last):
                at = b - B

                def normalise(g):
                    dve.wait_ge(o_turned, b * 4 + g + 1)
                    o = n_bank[:, :].rearrange("p (t h c) -> p t h c", t=T, h=4)
                    dve.reciprocal(one_over[:, :, :], o[:, :, :, DH]).then_inc(inverted, 1)
                    dve.wait_ge(inverted, b * 4 + g + 1)
                    dve.tensor_tensor(ctxt[:, :, g * 64:g * 64 + 64].rearrange("p t (h d) -> p t h d", d=DH),
                                      o[:, :, :, 0:DH], one_over[:, :, :].unsqueeze(3).to_broadcast([P, T, 4, DH]),
                                      ALU.mult).then_inc(ctx_made, 1)

                for n in range(AHEAD, T * H):
                    t, group = n % T, n // 16
                    take_max(b, n)
                    if n % 16 == AHEAD - 19 and group > 1:
                        take_row(b, group - 1)
                    if 48 <= n < 52:
                        dve.wait_ge(x_loaded, b * 16 + 16)
                        dve.wait_ge(out_stored, b * 16)
                        dve.tensor_tensor(res[:, t, :], x[:, t, :], bo[:, :], ALU.add).then_inc(res_begun, 1)
                    if not last and 32 <= n < 44:
                        norm_x(b + 1, (n - 32) // T, t)
                    if n % 16 == AHEAD - 10 and group >= 2:
                        normalise(group - 2)
                take_row(b, 3)
                normalise(2)
                if not last:
                    cut_x(b + 1)
                normalise(3)
                if not last:
                    take_v(b + 1)
                for k in range(DK):
                    dve.wait_ge(c_high, b * 2 + k + 1)
                    dve.tensor_tensor(ct_lo[:, k, :], bank[k][:, :], ct_hi[:, k, :].bitcast(F32), ALU.subtract).then_inc(c_low, 1)
                if not last:
                    part_lows(b + 1, (0,))
                dve.wait_ge(res_begun, b * T + T)
                for i in range(2):
                    dve.wait_ge(attn_out, b * 2 + i + 1)
                    dve.tensor_tensor(res[:, 2 * i:2 * i + 2, :], (o_bank, n_bank)[i][:, :].rearrange("p (t d) -> p t d", d=D),
                                      res[:, 2 * i:2 * i + 2, :], ALU.add).then_inc(first_res, 1)
                dve.wait_ge(first_res, b * 2 + 2)
                layer_norm(dve, dve_passed, res, ctxt, stats, mv, nt, 1e-5, norm_step, b * NORM_STEPS)
                if not last:
                    part_lows(b + 1, (1, 2, 3))
                for k in range(DK):
                    dve.wait_ge(affine_made, b * 2 + k + 1)
                    cut(k, ct_hi, ct_lo, ff_hi, b * (DK + FK), c_low)
                dve.wait_ge(norm_step, b * NORM_STEPS + NORM_STEPS)
                dve.tensor_tensor(res[:, :, :], res[:, :, :], over_rows(b2[:, :]), ALU.add).then_inc(delta_step, 1)
                dve.wait_ge(delta_step, at * 2 + 1)
                dve.tensor_tensor(res[:, :, :], res[:, :, :], x[:, :, :], ALU.subtract).then_inc(delta_step, 1)
                dve.tensor_copy(gate[:, :], gates[:, bass.ds(b - B, 1)]).then_inc(mixed, 1)
                if not last:
                    dve.wait_ge(halves_stored, (b + 1) * 64 + 64)
                for m in range(FK):
                    if m >= 4 and not last:
                        for n in range(4 * m - 16, 4 * m - 12):
                            take_max(b + 1, n)
                    dve.wait_ge(gelu_done, b * FK + m + 1)
                    if m >= 4:
                        dve.wait_ge(down_done, b * FK + m - 3)
                    dve.tensor_copy(ring_hi[:, m % 4, :], y[:, m % 2, :]).then_inc(ff_hi, 1)
                    dve.wait_ge(ff_hi, b * (DK + FK) + DK + m + 1)
                    dve.tensor_tensor(ring_lo[:, m % 4, :], y[:, m % 2, :], ring_hi[:, m % 4, :].bitcast(F32),
                                      ALU.subtract).then_inc(ff_lo, 1)
                if not last:
                    take_row(b + 1, 0)
                    for n in range(16, AHEAD):
                        take_max(b + 1, n)
                dve.wait_ge(down_done, b * FK + FK)
                dve.wait_ge(delta_step, at * 2 + 2)
                for t, src in enumerate((F2, F3, o_bank[:, :], n_bank[:, :])):
                    dve.tensor_tensor(res[:, t, :], src[:, 0:D], res[:, t, :], ALU.add).then_inc(mixed, 1)
                for t in range(T):
                    dve.wait_ge(mixed, at * 5 + 2 + t)
                    dve.scalar_tensor_tensor(out=res[:, t, :], in0=res[:, t, :], scalar=gate[:, :], in1=x[:, t, :],
                                             op0=ALU.mult, op1=ALU.add).then_inc(out_ready, 1)

            for n in range(3):
                for t in range(T):
                    norm_x(B, n, t)
            dve.wait_ge(early_loaded, 16 * 6)
            dve.tensor_scalar(bq[:, :], bq[:, :], SC, None, ALU.mult).then_inc(set_step, 1)
            dve.tensor_copy(ident_bf[:, :], ident[:, :]).then_inc(set_step, 1)
            dve.tensor_copy(causal_qk[:, :], causal[:, :]).then_inc(set_step, 1)
            dve.wait_ge(max_turned, 1)
            dve.tensor_copy(causal_kq[:, :], n_bank[:, 0:P]).then_inc(set_step, 1)
            cut_x(B)
            dve.wait_ge(pool_set, 3)
            dve.wait_ge(small_loaded, 16 * 7)
            take_v(B)
            part_lows(B, range(4))
            for n in range(16):
                take_max(B, n)
            take_row(B, 0)
            for n in range(16, AHEAD):
                take_max(B, n)
            with dve.Fori(B, 2 * B - 1) as b:
                batch(b, False)
            batch(2 * B - 1, True)


COMMON = {"mask": "mask_Bx1xSxS_bk0", "bias": "fside_Bx16xSxS_0", "timestep": "itok_B_34_63", "expert": "itok_B_0_15",
          "mlp_expert": "itok_B_0_7", "gate": "condB_gatescore"}


def layers_program(nc, args, out):
    def layer_weights(n):
        prefix = f"L{n}_cond_"
        return {name[len(prefix):]: ap for name, ap in args.items() if name.startswith(prefix)}

    def internal(name, shape):
        return nc.dram_tensor(name, shape, F32, kind="Internal").ap()

    between = [internal(f"between{n}", [B, S, D]) for n in range(3)]
    scratch = {"halves": internal("halves", [4, D, S]), "ada": internal("ada_rows", [B, 2 * D])}
    sems = {}
    for n, around in enumerate(((adapter_layer, biased_attention_layer), (expert_mlp_layer, causal_attention_layer))):
        first, second = 2 * n, 2 * n + 1
        x_in = between[first - 1] if n else args["x"]
        x_out = out if n else between[second]
        with ExitStack() as ctx:
            weights = CutWeights(nc, ctx, layer_weights(second), f"l{second}_")
            extra = () if n else (lambda nc, ctx: AdaptiveRows(nc, ctx, layer_weights(1), args, scratch["ada"]),)
            around[0](nc, x_in, between[first], layer_weights(first), args, weights, *extra)
            around[1](nc, between[first], x_out, layer_weights(second), args, scratch, sems, weights)


def kernel(**inputs):
    import concourse.bacc as bacc
    from concourse.bass_utils import run_bass_kernel_spmd

    nc = bacc.Bacc("TRN2", target_bir_lowering=False, num_devices=1)
    given = {name: np.ascontiguousarray(a) for name, a in inputs.items()}
    data = {name: a for name, a in given.items() if name == "x" or name.startswith("L")}
    data.update({name: given[full] for name, full in COMMON.items()})
    data["mask"] = data["mask"].reshape(B, S, S)
    data["bias"] = data["bias"].reshape(B * H, S, S)
    data["ident"] = np.eye(P, dtype=np.float32)
    data["freq"] = np.exp(np.arange(P, dtype=np.float32) * np.float32(-math.log(10000.0) / (P - 1))).reshape(P, 1)
    data["causal"] = np.where(np.arange(P)[:, None] >= np.arange(P)[None, :], 0, MASKED).astype(np.float32)
    arrays, args = {}, {}
    for name, a in data.items():
        arrays[f"in_{name}_dram"] = a
        args[name] = nc.dram_tensor(f"in_{name}_dram", a.shape, mybir.dt.from_np(a.dtype), kind="ExternalInput").ap()
    out = nc.dram_tensor("out_0_dram", (B, S, D), F32, kind="ExternalOutput").ap()
    layers_program(nc, args, out)
    r = run_bass_kernel_spmd(nc, [arrays], core_ids=[0])
    return r.results[0]["out_0_dram"]
```
